# Optimizing a Trainium2 kernel written in Bass

```python
import numpy as np
import jax
import jax.numpy as jnp

def _softmax(x, axis=-1):
    return jax.nn.softmax(x, axis=axis)

def _gelu(x):
    return jax.nn.gelu(x, approximate=True)

def _silu(x):
    return jax.nn.silu(x)

def _sigmoid(x):
    return jax.nn.sigmoid(x)

def _layernorm(x, axis=-1, eps=1e-05):
    m = jnp.mean(x, axis=axis, keepdims=True)
    v = jnp.var(x, axis=axis, keepdims=True)
    return (x - m) / jnp.sqrt(v + eps)

def _scatter_add(tgt, idx, src, axis=0):
    return tgt.at[idx].add(src)

def _segment_sum(src, seg, n):
    return jax.ops.segment_sum(src, seg, n)
kernel_name = 'mk_gnn_resnorm_d4_gnn_r32_8b1d83'

def setup_inputs(seed: int=0):
    np.random.seed(seed)
    _w = jnp.asarray

    def _rec_inputs():
        import jax
        import jax.numpy as jnp
        _gk = jax.random.key(seed)
        x = -0.0003713 + 1 * jax.random.normal(jax.random.fold_in(_gk, 1), (50000, 256), jnp.float32)
        src = jax.random.randint(jax.random.fold_in(_gk, 2), (25000,), 0, 50000, jnp.int32)
        dst = jax.random.randint(jax.random.fold_in(_gk, 3), (25000,), 0, 50000, jnp.int32)
        _o = jnp.argsort(dst, stable=True)
        src = src[_o]
        dst = dst[_o]
        edge_attr_64 = -9.77346e-05 + 0.999888 * jax.random.normal(jax.random.fold_in(_gk, 12), (25000, 64), jnp.float32)
        edge_type_16 = jax.random.randint(jax.random.fold_in(_gk, 14), (25000,), 0, 16, jnp.int32)
        edge_weight = jax.random.uniform(jax.random.fold_in(_gk, 15), (25000,), jnp.float32, 0.0, 0.999998)
        return (x, src, dst, edge_attr_64, edge_type_16, edge_weight)
    x, src, dst, edge_attr_64, edge_type_16, edge_weight = _rec_inputs()

    def _L0_gnn_setup():
        import jax, jax.numpy as jnp
        import numpy as np
        THR_A = 0.1
        THR_W = 0.1
        N, M, F_IN, F_OUT = (50000, 12500, 256, 256)
        key = jax.random.key(seed)
        k1, k2, k3, k4, k5, k6 = jax.random.split(key, 6)
        x = jax.random.normal(k1, (N, F_IN), dtype=jnp.float32)
        edge_index = jax.random.randint(k2, (2, M), 0, N, dtype=jnp.int64)
        edge_weight = jax.random.uniform(k3, (M,), dtype=jnp.float32)
        node_lock = jax.random.randint(k4, (1000,), 0, N, dtype=jnp.int64)
        W = jax.random.normal(k5, (F_OUT, F_IN), dtype=jnp.float32) / np.sqrt(F_IN)
        b = jax.random.normal(k6, (F_OUT,), dtype=jnp.float32) * 0.01
        return {'x': x, 'edge_index': edge_index, 'edge_weight': edge_weight, 'node_lock': node_lock, 'W': W, 'b': b}
    _L0_gnn_all = _L0_gnn_setup()
    _L0_gnn_in = {k: v for k, v in _L0_gnn_all.items() if k in ('node_lock', 'W', 'b')}
    del _L0_gnn_all

    def _L1_gnn_setup():
        import jax, jax.numpy as jnp
        import numpy as np
        N = 50000
        E = 25000
        D_IN = 256
        HID = 32
        HEADS = 8
        D_OUT = 64
        NEG_SLOPE = 0.2

        def _gat_conv(x, src, dst, W, att_src, att_dst, bias, heads, out_dim, concat):
            n = x.shape[0]
            h = (x @ W.T).reshape(n, heads, out_dim)
            a_s = jnp.sum(h * att_src, axis=-1)
            a_d = jnp.sum(h * att_dst, axis=-1)
            logits = jax.nn.leaky_relu(a_s[src] + a_d[dst], NEG_SLOPE)
            m = jax.ops.segment_max(logits, dst, num_segments=n)
            e = jnp.exp(logits - m[dst])
            den = jax.ops.segment_sum(e, dst, num_segments=n)
            alpha = e / (den[dst] + 1e-16)
            out = jax.ops.segment_sum(alpha[:, :, None] * h[src], dst, num_segments=n)
            out = out.reshape(n, heads * out_dim) if concat else out.mean(axis=1)
            return out + bias
        key = jax.random.key(seed)
        ks = jax.random.split(key, 12)
        x = jax.random.normal(ks[0], (N, D_IN), jnp.float32)
        edge_index = jax.random.randint(ks[1], (2, E), 0, N, dtype=jnp.int32)
        g = lambda k, shape, fan_in: jax.random.normal(k, shape, jnp.float32) / np.sqrt(fan_in)
        W0 = g(ks[2], (HEADS * HID, D_IN), D_IN)
        att_src0 = g(ks[3], (1, HEADS, HID), HID)
        att_dst0 = g(ks[4], (1, HEADS, HID), HID)
        b0 = jnp.zeros((HEADS * HID,), jnp.float32)
        W1 = g(ks[5], (1 * D_OUT, HEADS * HID), HEADS * HID)
        att_src1 = g(ks[6], (1, 1, D_OUT), D_OUT)
        att_dst1 = g(ks[7], (1, 1, D_OUT), D_OUT)
        b1 = jnp.zeros((D_OUT,), jnp.float32)
        return {'x': x, 'edge_index': edge_index, 'W0': W0, 'att_src0': att_src0, 'att_dst0': att_dst0, 'b0': b0, 'W1': W1, 'att_src1': att_src1, 'att_dst1': att_dst1, 'b1': b1}
    _L1_gnn_all = _L1_gnn_setup()
    _L1_gnn_in = {k: v for k, v in _L1_gnn_all.items() if k in ('W0', 'att_src0', 'att_dst0', 'b0', 'W1', 'att_src1', 'att_dst1', 'b1')}
    del _L1_gnn_all

    def _L2_gnn_setup():
        import jax, jax.numpy as jnp
        import numpy as np
        ALPHA = 0.2
        key = jax.random.key(seed)
        ks = jax.random.split(key, 6)
        N, E, F_IN, F_OUT, E_DIM = (50000, 25000, 256, 256, 64)
        h = jax.random.normal(ks[0], (N, F_IN), dtype=jnp.float32)
        e_feat = jax.random.normal(ks[1], (E, E_DIM), dtype=jnp.float32)
        W = jax.random.normal(ks[2], (F_OUT, F_IN), dtype=jnp.float32) * (1.0 / np.sqrt(F_IN))
        A = jax.random.normal(ks[3], (1, 2 * F_OUT + E_DIM), dtype=jnp.float32) * 0.05
        src = jax.random.randint(ks[4], (E,), 0, N, dtype=jnp.int32)
        dst = jax.random.randint(ks[5], (E,), 0, N, dtype=jnp.int32)
        return {'h': h, 'e_feat': e_feat, 'W': W, 'A': A, 'src': src, 'dst': dst}
    _L2_gnn_all = _L2_gnn_setup()
    _L2_gnn_in = {k: v for k, v in _L2_gnn_all.items() if k in ('W', 'A')}
    del _L2_gnn_all

    def _L3_gnn_setup():
        import jax, jax.numpy as jnp
        import numpy as np
        N_NODES = 50000
        N_EDGES = 25000
        HDIM = 256
        NUMRELS = 16

        def _gru_cell(x, h, w_ih, w_hh, b_ih, b_hh):
            gi = x @ w_ih.T + b_ih
            gh = h @ w_hh.T + b_hh
            i_r, i_z, i_n = jnp.split(gi, 3, axis=-1)
            h_r, h_z, h_n = jnp.split(gh, 3, axis=-1)
            r = jax.nn.sigmoid(i_r + h_r)
            z = jax.nn.sigmoid(i_z + h_z)
            n = jnp.tanh(i_n + r * h_n)
            return (1.0 - z) * n + z * h
        key = jax.random.key(seed)
        ks = jax.random.split(key, 9)
        h = jax.random.normal(ks[0], (N_NODES, HDIM), dtype=jnp.float32)
        relvectors = jax.random.normal(ks[1], (NUMRELS, HDIM), dtype=jnp.float32)
        s = 1.0 / np.sqrt(HDIM)
        w_ih = jax.random.uniform(ks[2], (3 * HDIM, HDIM), minval=-s, maxval=s, dtype=jnp.float32)
        w_hh = jax.random.uniform(ks[3], (3 * HDIM, HDIM), minval=-s, maxval=s, dtype=jnp.float32)
        b_ih = jax.random.uniform(ks[4], (3 * HDIM,), minval=-s, maxval=s, dtype=jnp.float32)
        b_hh = jax.random.uniform(ks[5], (3 * HDIM,), minval=-s, maxval=s, dtype=jnp.float32)
        edge_src = jax.random.randint(ks[6], (N_EDGES,), 0, N_NODES, dtype=jnp.int32)
        edge_dst = jax.random.randint(ks[7], (N_EDGES,), 0, N_NODES, dtype=jnp.int32)
        edge_rel = jax.random.randint(ks[8], (N_EDGES,), 0, NUMRELS, dtype=jnp.int32)
        return {'h': h, 'relvectors': relvectors, 'w_ih': w_ih, 'w_hh': w_hh, 'b_ih': b_ih, 'b_hh': b_hh, 'edge_src': edge_src, 'edge_dst': edge_dst, 'edge_rel': edge_rel}
    _L3_gnn_all = _L3_gnn_setup()
    _L3_gnn_in = {k: v for k, v in _L3_gnn_all.items() if k in ('relvectors', 'w_ih', 'w_hh', 'b_ih', 'b_hh')}
    del _L3_gnn_all
    return {'x': x, 'src': src, 'dst': dst, 'edge_attr_64': edge_attr_64, 'edge_type_16': edge_type_16, 'edge_weight': edge_weight, 'L0_gnn_node_lock': _L0_gnn_in['node_lock'], 'L0_gnn_W': _L0_gnn_in['W'], 'L0_gnn_b': _L0_gnn_in['b'], 'L1_gnn_W0': _L1_gnn_in['W0'], 'L1_gnn_att_src0': _L1_gnn_in['att_src0'], 'L1_gnn_att_dst0': _L1_gnn_in['att_dst0'], 'L1_gnn_b0': _L1_gnn_in['b0'], 'L1_gnn_W1': _L1_gnn_in['W1'], 'L1_gnn_att_src1': _L1_gnn_in['att_src1'], 'L1_gnn_att_dst1': _L1_gnn_in['att_dst1'], 'L1_gnn_b1': _L1_gnn_in['b1'], 'L2_gnn_W': _L2_gnn_in['W'], 'L2_gnn_A': _L2_gnn_in['A'], 'L3_gnn_relvectors': _L3_gnn_in['relvectors'], 'L3_gnn_w_ih': _L3_gnn_in['w_ih'], 'L3_gnn_w_hh': _L3_gnn_in['w_hh'], 'L3_gnn_b_ih': _L3_gnn_in['b_ih'], 'L3_gnn_b_hh': _L3_gnn_in['b_hh']}

def reference(x, src, dst, edge_attr_64, edge_type_16, edge_weight, L0_gnn_node_lock, L0_gnn_W, L0_gnn_b, L1_gnn_W0, L1_gnn_att_src0, L1_gnn_att_dst0, L1_gnn_b0, L1_gnn_W1, L1_gnn_att_src1, L1_gnn_att_dst1, L1_gnn_b1, L2_gnn_W, L2_gnn_A, L3_gnn_relvectors, L3_gnn_w_ih, L3_gnn_w_hh, L3_gnn_b_ih, L3_gnn_b_hh):
    import jax
    import jax.numpy as jnp

    def _L0_gnn_ref(x, edge_index, edge_weight, node_lock, W, b):
        import jax, jax.numpy as jnp
        import numpy as np
        THR_A = 0.1
        THR_W = 0.1
        N, M, F_IN, F_OUT = (50000, 12500, 256, 256)
        n, f_in = x.shape
        norm_node_in = jnp.linalg.norm(x, axis=0)
        norm_all_in = jnp.linalg.norm(norm_node_in) / f_in
        thr_wi = THR_W * norm_all_in / norm_node_in
        W_pruned = jnp.where(jnp.abs(W) < thr_wi[None, :], 0.0, W)
        W_eff = jnp.where(norm_all_in > 1e-08, W_pruned, W)
        h = x @ W_eff.T
        src, dst = (edge_index[0], edge_index[1])
        locked = jnp.zeros((n,), dtype=bool).at[node_lock].set(True)
        lock = locked[dst] | (src == dst)
        msg = edge_weight[:, None] * h[src]
        norm_feat_msg = jnp.linalg.norm(msg, axis=1)
        norm_all_msg = jnp.sum(norm_feat_msg) / msg.shape[0]
        mask0 = (norm_feat_msg < THR_A * norm_all_msg) & ~lock
        msg = jnp.where(mask0[:, None], 0.0, msg)
        out = jax.ops.segment_sum(msg, dst, num_segments=n) + b
        return out

    def _L1_gnn_ref(x, edge_index, W0, att_src0, att_dst0, b0, W1, att_src1, att_dst1, b1):
        import jax, jax.numpy as jnp
        import numpy as np
        N = 50000
        E = 25000
        D_IN = 256
        HID = 32
        HEADS = 8
        D_OUT = 64
        NEG_SLOPE = 0.2

        def _gat_conv(x, src, dst, W, att_src, att_dst, bias, heads, out_dim, concat):
            n = x.shape[0]
            h = (x @ W.T).reshape(n, heads, out_dim)
            a_s = jnp.sum(h * att_src, axis=-1)
            a_d = jnp.sum(h * att_dst, axis=-1)
            logits = jax.nn.leaky_relu(a_s[src] + a_d[dst], NEG_SLOPE)
            m = jax.ops.segment_max(logits, dst, num_segments=n)
            e = jnp.exp(logits - m[dst])
            den = jax.ops.segment_sum(e, dst, num_segments=n)
            alpha = e / (den[dst] + 1e-16)
            out = jax.ops.segment_sum(alpha[:, :, None] * h[src], dst, num_segments=n)
            out = out.reshape(n, heads * out_dim) if concat else out.mean(axis=1)
            return out + bias
        n = x.shape[0]
        loop = jnp.arange(n, dtype=edge_index.dtype)
        ei = jnp.concatenate([edge_index, jnp.stack([loop, loop])], axis=1)
        src, dst = (ei[0], ei[1])
        out1 = jax.nn.elu(_gat_conv(x, src, dst, W0, att_src0, att_dst0, b0, HEADS, HID, True))
        _ = _gat_conv(out1, src, dst, W1, att_src1, att_dst1, b1, 1, D_OUT, False)
        return out1

    def _L2_gnn_ref(h, e_feat, W, A, src, dst):
        import jax, jax.numpy as jnp
        import numpy as np
        ALPHA = 0.2
        N = h.shape[0]
        F_OUT = W.shape[0]
        z = h @ W.T
        z_src = z[src]
        z_dst = z[dst]
        a_src, a_dst, a_e = (A[0, :F_OUT], A[0, F_OUT:2 * F_OUT], A[0, 2 * F_OUT:])
        logits = z_src @ a_src + z_dst @ a_dst + e_feat @ a_e
        e = jax.nn.leaky_relu(logits, ALPHA)
        m = jax.ops.segment_max(e, dst, num_segments=N)
        ex = jnp.exp(e - m[dst])
        denom = jax.ops.segment_sum(ex, dst, num_segments=N)
        alpha = ex / denom[dst]
        h_out = jax.ops.segment_sum(alpha[:, None] * z_src, dst, num_segments=N)
        return h_out

    def _L3_gnn_ref(h, relvectors, w_ih, w_hh, b_ih, b_hh, edge_src, edge_dst, edge_rel):
        import jax, jax.numpy as jnp
        import numpy as np
        N_NODES = 50000
        N_EDGES = 25000
        HDIM = 256
        NUMRELS = 16

        def _gru_cell(x, h, w_ih, w_hh, b_ih, b_hh):
            gi = x @ w_ih.T + b_ih
            gh = h @ w_hh.T + b_hh
            i_r, i_z, i_n = jnp.split(gi, 3, axis=-1)
            h_r, h_z, h_n = jnp.split(gh, 3, axis=-1)
            r = jax.nn.sigmoid(i_r + h_r)
            z = jax.nn.sigmoid(i_z + h_z)
            n = jnp.tanh(i_n + r * h_n)
            return (1.0 - z) * n + z * h
        msg = h[edge_src] + relvectors[edge_rel]
        red = jax.ops.segment_sum(msg, edge_dst, num_segments=h.shape[0])
        return _gru_cell(red, h, w_ih, w_hh, b_ih, b_hh)
    edge_index = jnp.stack([src, dst])
    x = _layernorm(x + _L0_gnn_ref(x, edge_index, edge_weight, L0_gnn_node_lock, L0_gnn_W, L0_gnn_b), axis=-1)
    x = _layernorm(x + _L1_gnn_ref(x, edge_index, L1_gnn_W0, L1_gnn_att_src0, L1_gnn_att_dst0, L1_gnn_b0, L1_gnn_W1, L1_gnn_att_src1, L1_gnn_att_dst1, L1_gnn_b1), axis=-1)
    x = _layernorm(x + _L2_gnn_ref(x, edge_attr_64, L2_gnn_W, L2_gnn_A, src, dst), axis=-1)
    x = _layernorm(x + _L3_gnn_ref(x, L3_gnn_relvectors, L3_gnn_w_ih, L3_gnn_w_hh, L3_gnn_b_ih, L3_gnn_b_hh, src, dst, edge_type_16), axis=-1)
    return x

_drawn_inputs = setup_inputs


def setup_inputs(seed=0):
    import zlib

    import numpy as np

    out = dict(_drawn_inputs(seed))
    spreads = {'L1_gnn_b0': (0.0, 0.1), 'L1_gnn_b1': (0.0, 0.1)}
    factors = {'L0_gnn_b': 4.89, 'L3_gnn_b_ih': 4.825, 'L3_gnn_b_hh': 7.264}
    for name, (base, spread) in spreads.items():
        noise = np.random.default_rng([zlib.crc32(name.encode()), seed]).standard_normal(out[name].shape)
        drawn = base * np.exp(spread * noise) if base else spread * noise
        out[name] = jnp.asarray(drawn.astype(out[name].dtype))
    for name, factor in factors.items():
        out[name] = (out[name] * factor).astype(out[name].dtype)
    return out
```

```python
from contextlib import ExitStack

import concourse.bass as bass
from concourse import mybir
from concourse.alu_op_type import AluOpType as ALU

ACT = mybir.ActivationFunctionType
AX = mybir.AxisListType
F32 = mybir.dt.float32
BF16 = mybir.dt.bfloat16
I32 = mybir.dt.int32

P = 128
D = 256
KC = D // P
HEADS = 8
HID = D // HEADS
RELS = 16
EDIM = 64
SLOT_EDGES = P - 1
EPS = 1e-5
THR_A = 0.1
THR_W = 0.1
SLOPE = 0.2
FAR = 1 << 20
NONE = -1e30


class Steps:

    def __init__(self, sem, stages, slots, main=None, rounds=0):
        self.sem, self.slots, self.main, self.rounds = sem, slots, main, rounds
        self.order = {}
        for stage in stages:
            for s in slots:
                for name in stage.split():
                    self.order[s, name] = len(self.order)
        self.n = len(self.order)
        self.lead = self.n if main is None else main.lead + rounds * main.n
        if main is not None:
            self.lead -= rounds * self.n

    def at(self, k, s, name):
        return self.sem, k * self.n + (self.lead + self.order[s, name] + 1)

    def before(self, k, s, name):
        if self.main is not None:
            return self.main.at(self.rounds - 1, s, name)
        return self.sem, k * self.n + (self.order[s, name] + 1)


def bcast_rows(ap, rows, cols):
    return bass.AP(ap.tensor, ap.offset, [[0, rows], [1, cols]])


def gnn(nc, x, src, dst, dst_next, dst_cols, dst_prev, attr, etype, ew, node_lock, W0e_T, b0e, W1_T, W1n, att1, b1,
        W2_T, W2n, A2, a2_T, rel_T, wih_T, whh_T, b_ih, b_hh, out, X1, X2, X3, MSG):
    N = x.shape[0]
    NB = src.shape[1]
    NEDGE = NB_EDGES[0]
    L = node_lock.shape[1]
    PAIR = 2 * P
    PAIRS = N // PAIR
    REST = N - PAIRS * PAIR
    assert 0 < REST <= P
    U = 3
    assert PAIRS % U == 0 and NB % U == 0
    es = ExitStack()
    with es:
        def sb(name, shape, dt=F32, ctx=es):
            return ctx.enter_context(nc.sbuf_tensor(name, shape, dt))

        def ps(name, shape, ctx, dt=F32):
            return ctx.enter_context(nc.psum_tensor(name, shape, dt))

        def sm(name, ctx=es):
            return ctx.enter_context(nc.semaphore(name))

        ident = sb("ident", [P, P])
        ones_b = sb("ones_b", [P, P], BF16)
        eps_c = sb("eps_c", [P, 2])
        mhalf = sb("mhalf", [P, 2])
        src_f = sb("src_f", [P, NB])
        dst_f = sb("dst_f", [P, NB])
        type_f = sb("type_f", [P, NB])
        w_e = sb("w_e", [P, NB])
        src_i = sb("src_i", [P, NB], I32)
        dst_i = sb("dst_i", [P, NB], I32)
        put_i = sb("put_i", [P, NB], I32)
        efeat = sb("efeat", [P, NB])
        keep = sb("keep", [P, NB])
        Weff_T = sb("Weff_T", [P, KC, D])
        b0e_r = sb("b0e_r", [P, D])
        W1x = sb("W1x", [P, KC, D + 2 * HEADS])
        b1m1_r = sb("b1m1_r", [P, D])
        W2T = sb("W2T", [P, KC, D])
        us_r = sb("us_r", [P, D])
        ud_r = sb("ud_r", [P, D])
        whhT = sb("whhT", [P, KC, 3 * D])
        wihT = sb("wihT", [P, KC, 3 * D])
        relw = sb("relw", [RELS, 3 * D])
        bias3 = sb("bias3", [P, 3 * D], BF16)
        bin_r = sb("bin_r", [P, D])

        prepare(nc, locals())
        dense(nc, locals())
        edge_norms(nc, locals())
        edge_sum(nc, locals())
        edge_heads(nc, locals())
        edge_attention(nc, locals())
        edge_gru(nc, locals())


def prepare(nc, g):
    (N, NB, L, sb, ps, sm) = (g[n] for n in ("N", "NB", "L", "sb", "ps", "sm"))
    x = g["x"]
    with ExitStack() as c:
        loaded = sm("loaded", c)
        dve_done = sm("dve_done", c)
        pe_done = sm("pe_done", c)
        act_done = sm("act_done", c)
        pool_done = sm("pool_done", c)
        attr_loaded = [sm(f"attr_loaded{s}", c) for s in range(2)]
        attr_used = sm("attr_used", c)
        x_loaded = [sm(f"x_loaded{s}", c) for s in range(2)]
        x_squared = sm("x_squared", c)
        sq_added = sm("sq_added", c)
        lead_done = sm("lead_done", c)
        W0r = sb("W0r", [P, KC, D], F32, c)
        W1n = sb("W1n", [P, KC, D], F32, c)
        W2n = sb("W2n", [P, KC, D], F32, c)
        att = sb("att", [P, KC, 2 * HEADS], F32, c)
        a2 = sb("a2", [P, KC, 2], F32, c)
        a2b = sb("a2b", [P, KC, 2, P], F32, c)
        ae_r = sb("ae_r", [P, EDIM], F32, c)
        relT = sb("relT", [P, KC, RELS], F32, c)
        nxt_f = sb("nxt_f", [P, NB], I32, c)
        type_i = sb("type_i", [P, NB], I32, c)
        bi_r = sb("bi_r", [P, 3 * D], F32, c)
        bh_r = sb("bh_r", [P, 3 * D], F32, c)
        bsum = sb("bsum", [P, 3 * D], F32, c)
        bsum2 = sb("bsum2", [P, 3 * D], F32, c)
        bh = sb("bh", [P, 3 * D], BF16, c)
        tmp = sb("tmp", [P, NB], F32, c)
        tmp2 = sb("tmp2", [P, NB], F32, c)
        src0 = sb("src0", [P, NB], I32, c)
        dst0 = sb("dst0", [P, NB], I32, c)
        AB = NB // 6 if NB % 6 == 0 else NB
        at_sb = [sb(f"at_sb{s}", [P, AB, EDIM], F32, c) for s in range(2)]
        NROW = N // P
        NG = 13 if NROW % 13 == 0 else 6
        xg = [sb(f"xg{s}", [P, NG, D], F32, c) for s in range(2)]
        sq = [sb(f"sq{s}", [P, NG, D], F32, c) for s in range(2)]
        acc = sb("acc", [P, NG, D], F32, c)
        xtail = sb("xtail", [P, D], F32, c)
        onesf = sb("onesf", [P, P], F32, c)
        accr = sb("accr", [P, D], F32, c)
        nk = sb("nk", [P, KC], F32, c)
        nk2 = sb("nk2", [P, KC], F32, c)
        na = sb("na", [P, 1], F32, c)
        thr = sb("thr", [P, KC], F32, c)
        flag = sb("flag", [P, 1], F32, c)
        absw = sb("absw", [P, KC, D], F32, c)
        pv = ps("pv", [P, KC, 2 * HEADS], c)
        pu = ps("pu", [P, 2, D], c)
        pr = ps("pr", [RELS, 512], c)
        pr2 = ps("pr2", [RELS, D], c)
        pn = ps("pn", [P, KC + 1], c)
        TAIL = N - NROW * P
        STEPS = NROW // NG
        assert STEPS * NG == NROW and STEPS % 2 == 0
        block = c.enter_context(nc.Block())

        @block.sync
        def _(sp):
            kview = lambda a: a.rearrange("(c p) n -> p c n", p=P)
            loads = [
                (W0r[:, :, :], kview(g["W0e_T"])), (g["W1x"][:, :, 0:D], kview(g["W1_T"])),
                (W1n[:, :, :], kview(g["W1n"])), (W2n[:, :, :], kview(g["W2n"])),
                (g["W2T"][:, :, :], kview(g["W2_T"])), (att[:, :, :], kview(g["att1"])),
                (a2[:, :, :], kview(g["a2_T"])),
                (ae_r[:, :], bcast_rows(g["A2"][0:1, 2 * D:], P, EDIM)),
                (relT[:, :, :], kview(g["rel_T"])), (g["wihT"][:, :, :], kview(g["wih_T"])),
                (g["whhT"][:, :, :], kview(g["whh_T"])),
                (g["b0e_r"][:, :], bcast_rows(g["b0e"], P, D)), (g["b1m1_r"][:, :], bcast_rows(g["b1"], P, D)),
                (bi_r[:, :], bcast_rows(g["b_ih"], P, 3 * D)), (bh_r[:, :], bcast_rows(g["b_hh"], P, 3 * D)),
                (src0[:, :], g["src"]), (dst0[:, :], g["dst"]), (nxt_f[:, :], g["dst_next"]),
                (type_i[:, :], g["etype"]), (g["w_e"][:, :], g["ew"]),
                (xtail[0:TAIL, :], x[NROW * P:N, :]),
            ]
            for dst_ap, src_ap in loads:
                sp.dma_start(dst_ap, src_ap).then_inc(loaded, 16)
            g["N_LOADS"] = len(loads)
            for a in range(NB // AB):
                if a >= 2:
                    sp.wait_ge(attr_used, a - 1)
                sp.dma_start(at_sb[a % 2][:, :, :], g["attr"][:, a * AB:(a + 1) * AB, :]).then_inc(attr_loaded[a % 2], 16)

        NLOAD = 21

        @block.scalar
        def _(act):
            xv = x[0:NROW * P, :].rearrange("(i p g) d -> i p g d", p=P, g=NG)
            for s in range(2):
                act.dma_start(xg[s][:, :, :], xv[s]).then_inc(x_loaded[s], 16)
            for i in range(STEPS):
                s = i % 2
                act.wait_ge(x_loaded[s], 16 * (i // 2 + 1))
                if i >= 2:
                    act.wait_ge(sq_added, i - 1)
                nc.scalar.activation(sq[s][:, :, :], xg[s][:, :, :], ACT.Square).then_inc(x_squared, 1)
                if i + 2 < STEPS:
                    act.wait_ge(x_squared, i + 1)
                    act.dma_start(xg[s][:, :, :], xv[i + 2]).then_inc(x_loaded[s], 16)
            act.wait_ge(loaded, 16 * NLOAD)
            nc.scalar.activation(xtail[0:TAIL, :], xtail[0:TAIL, :], ACT.Square).then_inc(x_squared, 1)
            act.wait_ge(pe_done, 2)
            nc.scalar.activation(nk[:, :], pn[:, 0:KC], ACT.Sqrt).then_inc(act_done, 1)
            act.wait_ge(pe_done, 3)
            nc.scalar.activation(na[:, :], pn[:, KC:KC + 1], ACT.Sqrt).then_inc(act_done, 1)

        @block.gpsimd
        def _(pool):
            nc.gpsimd.memset(g["ident"][:, :], 0.0).then_inc(pool_done, 1)
            pool.wait_ge(pool_done, 1)
            nc.gpsimd.affine_select(out=g["ident"][:, :], in_=g["ident"][:, :], compare_op=ALU.not_equal, fill=1.0,
                                    base=0, pattern=[[-1, P]], channel_multiplier=1).then_inc(pool_done, 1)
            nc.gpsimd.memset(g["ones_b"][:, :], 1.0)
            nc.gpsimd.memset(onesf[:, :], 1.0)
            nc.gpsimd.memset(g["eps_c"][:, :], EPS)
            nc.gpsimd.memset(g["mhalf"][:, :], -0.5)
            nc.gpsimd.memset(g["bias3"][:, :], 0.0).then_inc(pool_done, 1)

        @block.vector
        def _(dve):
            count = [0]

            def done(ins):
                count[0] += 1
                ins.then_inc(dve_done, 1)
                dve.wait_ge(dve_done, count[0])

            done(nc.vector.memset(acc[:, :, :], 0.0))
            for i in range(STEPS):
                dve.wait_ge(x_squared, i + 1)
                nc.vector.tensor_tensor(acc[:, :, :], acc[:, :, :], sq[i % 2][:, :, :], ALU.add).then_inc(sq_added, 1)
                dve.wait_ge(sq_added, i + 1)
            dve.wait_ge(loaded, 16 * NLOAD)
            done(nc.vector.tensor_reduce(accr[:, :], acc[:, :, :].rearrange("p g d -> p d g"), AX.X, ALU.add))
            dve.wait_ge(x_squared, STEPS + 1)
            done(nc.vector.tensor_tensor(accr[0:TAIL, :], accr[0:TAIL, :], xtail[0:TAIL, :], ALU.add))
            count_sq = count[0]
            g["count_sq"] = count_sq
            done(nc.vector.tensor_copy(g["src_f"][:, :], src0[:, :]))
            done(nc.vector.tensor_copy(g["dst_f"][:, :], dst0[:, :]))
            nc.vector.tensor_scalar(g["src_i"][:, :], g["src_f"][:, :], 0.0, float(N - 1), ALU.max, ALU.min)
            nc.vector.tensor_scalar(g["dst_i"][:, :], g["dst_f"][:, :], 0.0, float(N - 1), ALU.max, ALU.min)
            nc.vector.tensor_copy(g["type_f"][:, :], type_i[:, :])
            done(nc.vector.tensor_tensor(tmp[:, :], g["dst_f"][:, :], nxt_f[:, :], ALU.is_equal))
            done(nc.vector.scalar_tensor_tensor(tmp2[:, :], tmp[:, :], float(FAR), g["dst_f"][:, :], ALU.mult, ALU.add))
            done(nc.vector.tensor_copy(g["put_i"][:, :], tmp2[:, :]))
            for a in range(NB // AB):
                t = at_sb[a % 2]
                dve.wait_ge(attr_loaded[a % 2], 16 * (a // 2 + 1))
                done(nc.vector.tensor_tensor(t[:, :, :], t[:, :, :],
                                             ae_r[:, :].unsqueeze(1).to_broadcast([P, AB, EDIM]), ALU.mult))
                nc.vector.tensor_reduce(g["efeat"][:, a * AB:(a + 1) * AB], t[:, :, :], AX.X, ALU.add)\
                    .then_inc(attr_used, 1)
            done(nc.vector.tensor_scalar(g["b1m1_r"][:, :], g["b1m1_r"][:, :], -1.0, None, ALU.add))
            nc.vector.tensor_copy(g["bin_r"][:, :], bi_r[:, 2 * D:3 * D])
            nc.vector.tensor_scalar(bsum[:, 2 * D:3 * D], bh_r[:, 2 * D:3 * D], 0.5, None, ALU.mult)
            nc.vector.tensor_scalar(g["whhT"][:, :, 2 * D:3 * D], g["whhT"][:, :, 2 * D:3 * D], 0.5, None, ALU.mult)
            done(nc.vector.tensor_tensor(bsum[:, 0:2 * D], bi_r[:, 0:2 * D], bh_r[:, 0:2 * D], ALU.add))
            dve.wait_ge(pool_done, 3)
            a, b = bsum, bsum2
            for part in range(3):
                done(nc.vector.tensor_copy(bh[:, :], a[:, :]))
                nc.vector.tensor_copy(g["bias3"][32 * part:32 * part + 1, :], bh[32 * part:32 * part + 1, :])
                done(nc.vector.tensor_tensor(b[:, :], a[:, :], bh[:, :], ALU.subtract))
                a, b = b, a
            for j in range(2):
                done(nc.vector.tensor_copy(a2b[:, :, j, :], a2[:, :, j:j + 1].to_broadcast([P, KC, P])))
            g["count_a2b"] = count[0]
            dve.wait_ge(pe_done, 1)
            nc.vector.tensor_copy(g["W1x"][:, :, D:D + 2 * HEADS], pv[:, :, :])
            nc.vector.tensor_copy(g["us_r"][:, :], pu[:, 0, :])
            nc.vector.tensor_copy(g["ud_r"][:, :], pu[:, 1, :])
            nc.vector.tensor_copy(g["relw"][:, 0:512], pr[:, :])
            done(nc.vector.tensor_copy(g["relw"][:, 512:3 * D], pr2[:, :]))
            dve.wait_ge(act_done, 1)
            done(nc.vector.tensor_copy(nk2[:, :], pn[:, 0:KC]))
            done(nc.vector.tensor_tensor(nk2[:, 0:1], nk2[:, 0:1], nk2[:, 1:2], ALU.add))
            g["count_nk"] = count[0]
            dve.wait_ge(act_done, 2)
            done(nc.vector.reciprocal(thr[:, :], nk[:, :]))
            done(nc.vector.tensor_scalar(na[:, :], na[:, :], 1.0 / D, None, ALU.mult))
            done(nc.vector.tensor_scalar(flag[:, :], na[:, :], 1e-8, None, ALU.is_gt))
            done(nc.vector.tensor_scalar(na[:, :], na[:, :], THR_W, None, ALU.mult))
            done(nc.vector.tensor_scalar(thr[:, :], thr[:, :], na[:, :], None, ALU.mult))
            done(nc.vector.scalar_tensor_tensor(absw[:, :, :], W0r[:, :, :], -1.0, W0r[:, :, :], ALU.mult, ALU.max))
            for k in range(KC):
                done(nc.vector.tensor_scalar(absw[:, k, :], absw[:, k, :], thr[:, k:k + 1], flag[:, :],
                                             ALU.is_lt, ALU.mult))
            done(nc.vector.tensor_tensor(absw[:, :, :], absw[:, :, :], W0r[:, :, :], ALU.mult))
            done(nc.vector.tensor_tensor(g["Weff_T"][:, :, :], W0r[:, :, :], absw[:, :, :], ALU.subtract))

        @block.tensor
        def _(pe):
            pe.wait_ge(loaded, 16 * NLOAD)
            for k in range(KC):
                for o in range(KC):
                    nc.tensor.matmul(pv[:, k, :], W1n[:, o, k * P:(k + 1) * P], att[:, o, :],
                                     start=(o == 0), stop=(o == KC - 1))
            pe.wait_ge(dve_done, g["count_a2b"])
            for j in range(2):
                for o in range(KC):
                    nc.tensor.matmul(pu[:, j, :], a2b[:, o, j, :], W2n[:, o, :], start=(o == 0), stop=(o == KC - 1))
            for o in range(KC):
                nc.tensor.matmul(pr[:, :], relT[:, o, :], g["wihT"][:, o, 0:512], start=(o == 0), stop=(o == KC - 1))
            for o in range(KC):
                last = nc.tensor.matmul(pr2[:, :], relT[:, o, :], g["wihT"][:, o, 512:3 * D],
                                        start=(o == 0), stop=(o == KC - 1))
            last.then_inc(pe_done, 1)
            pe.wait_ge(pool_done, 3)
            pe.wait_ge(dve_done, g["count_sq"])
            for k in range(KC):
                last = nc.tensor.matmul(pn[:, k:k + 1], accr[:, k * P:(k + 1) * P], onesf[:, 0:1], start=True, stop=True)
            last.then_inc(pe_done, 1)
            pe.wait_ge(dve_done, g["count_nk"])
            nc.tensor.matmul(pn[:, KC:KC + 1], onesf[:, :], nk2[:, 0:1], start=True, stop=True).then_inc(pe_done, 1)


def dense(nc, g):
    sb, ps, sm, N, PAIRS, REST, U, x = (g[n] for n in ("sb", "ps", "sm", "N", "PAIRS", "REST", "U", "x"))
    PAIR = 2 * P
    with ExitStack() as c:
        ROUNDS = PAIRS // U
        slots = list(range(U))
        load_sem = [sm(f"nodes_loaded{s}", c) for s in slots]
        store_sem = {n: [sm(f"{n}_stored{s}", c) for s in slots] for n in ("x1", "x2", "x3", "x4")}
        stages = {
            "vec": ["v0 st0 ag0", "x1", "tb u", "v1 st1 ag1", "x2 st2 ag2", "x3", "q", "w v3 st3 ag3", "x4"],
            "pool": ["e0 r0", "e1 r1", "e2 r2", "q2", "d s", "e3 r3"],
            "scal": ["x1T", "ex", "x3T", "rz0 rz1", "n"],
            "mat": ["t1", "h", "t3", "gru0 gru1"],
        }
        sems = {e: sm(f"dense_{e}", c) for e in stages}
        main = {e: Steps(sems[e], stages[e], slots) for e in stages}
        rest = {e: Steps(sems[e], [n.replace(" rz1", "").replace(" gru1", "") for n in stages[e]], [0], main[e], ROUNDS)
                for e in stages}
        t = {}
        for n in ("x", "v", "x1", "x1T", "tb", "ex", "u", "x2", "x3", "x3T", "q", "q2", "n", "d", "s", "w", "x4"):
            t[n] = [sb(f"d_{n}{s}", [P, 2, D], F32, c) for s in slots]
        rz = [sb(f"d_rz{s}", [P, 2, 2 * D], F32, c) for s in slots]
        st = [sb(f"d_st{s}", [P, 2, 6], F32, c) for s in slots]
        mv = [sb(f"d_mv{s}", [P, 4, 2, 2], F32, c) for s in slots]
        ve = [sb(f"d_ve{s}", [P, 4, 2], F32, c) for s in slots]
        rs = [sb(f"d_rs{s}", [P, 4, 2], F32, c) for s in slots]
        pT = [ps(f"d_pT{i}", [P, 2 * D], c) for i in range(2)]
        pH = [ps(f"d_pH{i}", [P, 2, D], c) for i in range(2)]
        pRZ = [ps(f"d_pRZ{i}", [P, 2 * D], c) for i in range(2)]
        pN = [ps(f"d_pN{i}", [P, 2, D], c) for i in range(2)]
        block = c.enter_context(nc.Block())

        def rows_of(a, k, s, R, G):
            if G == 1:
                return a[PAIRS * PAIR:N, :].rearrange("(p g) d -> p g d", g=1)
            return a[bass.ds((k * U + s) * PAIR, PAIR), :].rearrange("(p g) d -> p g d", g=2)

        def rounds(eng, body):
            with eng.Fori(0, ROUNDS) as k:
                body(k, slots, P, 2, main)
            body(ROUNDS, [0], REST, 1, rest)

        @block.sync
        def _(sp):
            for n in store_sem:
                for s in slots:
                    sp.sem_inc(store_sem[n][s], 16)

            def body(k, ss, R, G, S):
                for s in ss:
                    sp.wait_ge(*S["vec"].before(k, s, "v0"))
                    sp.dma_start(t["x"][s][0:R, 0:G, :], rows_of(x, k, s, R, G)).then_inc(load_sem[s], 16)
                for n, a in (("x1", g["X1"]), ("x2", g["X2"]), ("x3", g["X3"]), ("x4", g["out"])):
                    for s in ss:
                        sp.wait_ge(*S["vec"].at(k, s, n))
                        sp.dma_start(rows_of(a, k, s, R, G), t[n][s][0:R, 0:G, :]).then_inc(store_sem[n][s], 16)
            rounds(sp, body)
            for n in store_sem:
                for s in slots:
                    sp.wait_ge(store_sem[n][s], 16 * (ROUNDS + 1 + (s == 0)))

        def norm(dve, S, k, s, R, G, i, into, frm):
            dve.wait_ge(*S["pool"].at(k, s, f"r{i}"))
            for j in range(G):
                last = nc.vector.tensor_scalar(t[into][s][0:R, j, :], t[frm][s][0:R, j, :], mv[s][0:R, i, j, 0:1],
                                               rs[s][0:R, i, j:j + 1], ALU.subtract, ALU.mult)
            return last

        @block.vector
        def _(dve):
            nc.vector.sem_inc(main["vec"].sem, main["vec"].lead)

            def body(k, ss, R, G, S):
                V, O, A, M = S["vec"], S["pool"], S["scal"], S["mat"]

                def stats(s, i, frm, wait):
                    dve.wait_ge(*V.at(k, s, wait))
                    for j in range(G):
                        last = nc.vector.bn_stats(st[s][0:R, j, :], t[frm][s][0:R, j, :])
                    last.then_inc(V.sem, 1)
                    dve.wait_ge(*V.at(k, s, f"st{i}"))
                    nc.vector.nop(nofuse=True)
                    for j in range(G):
                        last = nc.vector.bn_aggr(mv[s][0:R, i, j, :], st[s][0:R, j, :])
                    last.then_inc(V.sem, 1)

                for s in ss:
                    b = g["b0e_r"][0:R, :].unsqueeze(1).to_broadcast([R, G, D])
                    dve.wait_ge(load_sem[s], (k + 1) * 16)
                    nc.vector.tensor_tensor(t["v"][s][0:R, 0:G, :], t["x"][s][0:R, 0:G, :], b, ALU.add).then_inc(V.sem, 1)
                    stats(s, 0, "v", "v0")
                for s in ss:
                    dve.wait_ge(store_sem["x1"][s], k * 16 + 16)
                    norm(dve, S, k, s, R, G, 0, "x1", "v").then_inc(V.sem, 1)
                for s in ss:
                    dve.wait_ge(*M.at(k, s, "h"))
                    b = g["b1m1_r"][0:R, :].unsqueeze(1).to_broadcast([R, G, D])
                    nc.vector.tensor_tensor(t["tb"][s][0:R, 0:G, :], pH[s % 2][0:R, 0:G, :], b, ALU.add)\
                        .then_inc(V.sem, 1)
                    dve.wait_ge(*V.at(k, s, "tb"))
                    nc.vector.scalar_tensor_tensor(t["u"][s][0:R, 0:G, :], t["tb"][s][0:R, 0:G, :], -1.0,
                                                   t["x1"][s][0:R, 0:G, :], ALU.max, ALU.add).then_inc(V.sem, 1)
                for s in ss:
                    dve.wait_ge(*A.at(k, s, "ex"))
                    dve.wait_ge(*V.at(k, s, "u"))
                    nc.vector.scalar_tensor_tensor(t["v"][s][0:R, 0:G, :], t["ex"][s][0:R, 0:G, :], 1.0,
                                                   t["u"][s][0:R, 0:G, :], ALU.min, ALU.add).then_inc(V.sem, 1)
                    stats(s, 1, "v", "v1")
                for s in ss:
                    dve.wait_ge(store_sem["x2"][s], k * 16 + 16)
                    norm(dve, S, k, s, R, G, 1, "x2", "v").then_inc(V.sem, 1)
                    stats(s, 2, "x2", "x2")
                for s in ss:
                    dve.wait_ge(store_sem["x3"][s], k * 16 + 16)
                    dve.wait_ge(*O.before(k, s, "s"))
                    norm(dve, S, k, s, R, G, 2, "x3", "x2").then_inc(V.sem, 1)
                for s in ss:
                    dve.wait_ge(*M.at(k, s, f"gru{G - 1}"))
                    dve.wait_ge(*A.at(k, s, f"rz{G - 1}"))
                    nc.vector.scalar_tensor_tensor(t["q"][s][0:R, 0:G, :], rz[s][0:R, 0:G, 0:D], 1.0,
                                                   pN[s % 2][0:R, 0:G, :], ALU.add, ALU.mult).then_inc(V.sem, 1)
                for s in ss:
                    dve.wait_ge(*O.at(k, s, "s"))
                    nc.vector.scalar_tensor_tensor(t["w"][s][0:R, 0:G, :], rz[s][0:R, 0:G, D:2 * D], 1.0,
                                                   t["d"][s][0:R, 0:G, :], ALU.add, ALU.mult).then_inc(V.sem, 1)
                    dve.wait_ge(*V.at(k, s, "w"))
                    nc.vector.scalar_tensor_tensor(t["v"][s][0:R, 0:G, :], t["w"][s][0:R, 0:G, :], 0.5,
                                                   t["s"][s][0:R, 0:G, :], ALU.mult, ALU.add).then_inc(V.sem, 1)
                    stats(s, 3, "v", "v3")
                for s in ss:
                    dve.wait_ge(store_sem["x4"][s], k * 16 + 16)
                    norm(dve, S, k, s, R, G, 3, "x4", "v").then_inc(V.sem, 1)
            rounds(dve, body)

        @block.gpsimd
        def _(pool):
            nc.gpsimd.sem_inc(main["pool"].sem, main["pool"].lead)

            def body(k, ss, R, G, S):
                V, O, A = S["vec"], S["pool"], S["scal"]

                def rstd(s, i):
                    pool.wait_ge(*V.at(k, s, f"ag{i}"))
                    nc.gpsimd.tensor_tensor(ve[s][0:R, i, 0:G], mv[s][0:R, i, 0:G, 1], g["eps_c"][0:R, 0:G], ALU.add)\
                        .then_inc(O.sem, 1)
                    pool.wait_ge(*O.at(k, s, f"e{i}"))
                    nc.gpsimd.tensor_tensor(rs[s][0:R, i, 0:G], ve[s][0:R, i, 0:G], g["mhalf"][0:R, 0:G], ALU.pow)\
                        .then_inc(O.sem, 1)

                for i in range(3):
                    for s in ss:
                        rstd(s, i)
                for s in ss:
                    pool.wait_ge(*V.at(k, s, "q"))
                    b = g["bin_r"][0:R, :].unsqueeze(1).to_broadcast([R, G, D])
                    nc.gpsimd.tensor_tensor(t["q2"][s][0:R, 0:G, :], t["q"][s][0:R, 0:G, :], b, ALU.add)\
                        .then_inc(O.sem, 1)
                for s in ss:
                    pool.wait_ge(*A.at(k, s, "n"))
                    nc.gpsimd.tensor_tensor(t["d"][s][0:R, 0:G, :], t["x3"][s][0:R, 0:G, :], t["n"][s][0:R, 0:G, :],
                                            ALU.subtract).then_inc(O.sem, 1)
                    nc.gpsimd.tensor_tensor(t["s"][s][0:R, 0:G, :], t["x3"][s][0:R, 0:G, :], t["n"][s][0:R, 0:G, :],
                                            ALU.add).then_inc(O.sem, 1)
                for s in ss:
                    rstd(s, 3)
            rounds(pool, body)

        @block.scalar
        def _(act):
            nc.scalar.sem_inc(main["scal"].sem, main["scal"].lead)

            def body(k, ss, R, G, S):
                V, O, A, M = S["vec"], S["pool"], S["scal"], S["mat"]
                W = G * KC * R
                for s in ss:
                    act.wait_ge(*M.at(k, s, "t1"))
                    nc.scalar.activation(t["x1T"][s][:, :, :].rearrange("p a b -> p (a b)")[:, 0:W],
                                         pT[s % 2][:, 0:W], ACT.Copy).then_inc(A.sem, 1)
                for s in ss:
                    act.wait_ge(*V.at(k, s, "tb"))
                    nc.scalar.activation(t["ex"][s][0:R, 0:G, :], t["tb"][s][0:R, 0:G, :], ACT.Exp, bias=1.0)\
                        .then_inc(A.sem, 1)
                for s in ss:
                    act.wait_ge(*M.at(k, s, "t3"))
                    nc.scalar.activation(t["x3T"][s][:, :, :].rearrange("p a b -> p (a b)")[:, 0:W],
                                         pT[s % 2][:, 0:W], ACT.Copy).then_inc(A.sem, 1)
                for s in ss:
                    act.wait_ge(*V.before(k, s, "w"))
                    for j in range(G):
                        act.wait_ge(*M.at(k, s, f"gru{j}"))
                        nc.scalar.activation(rz[s][0:R, j, :], pRZ[j][0:R, :], ACT.Tanh, scale=0.5)\
                            .then_inc(A.sem, 1)
                for s in ss:
                    act.wait_ge(*O.at(k, s, "q2"))
                    nc.scalar.activation(t["n"][s][0:R, 0:G, :], t["q2"][s][0:R, 0:G, :], ACT.Tanh).then_inc(A.sem, 1)
            rounds(act, body)

        @block.tensor
        def _(pe):
            nc.tensor.sem_inc(main["mat"].sem, main["mat"].lead)

            def body(k, ss, R, G, S):
                V, A, M = S["vec"], S["scal"], S["mat"]

                def flip(s, frm):
                    for j in range(G):
                        for c_ in range(KC):
                            o = (j * KC + c_) * R
                            last = nc.tensor.transpose(pT[s % 2][:, o:o + R], t[frm][s][0:R, j, c_ * P:(c_ + 1) * P],
                                                       g["ident"][0:R, 0:R])
                    return last

                def lhs(name, s, j, c_):
                    o = (j * KC + c_) * R
                    return t[name][s][:, :, :].rearrange("p a b -> p (a b)")[:, o:o + R]

                for s in ss:
                    pe.wait_ge(*V.at(k, s, "x1"))
                    if s < 2:
                        pe.wait_ge(*A.before(k, U - 1, "x3T"))
                    else:
                        pe.wait_ge(*A.at(k, s - 2, "x1T"))
                    flip(s, "x1").then_inc(M.sem, 1)
                for s in ss:
                    pe.wait_ge(*A.at(k, s, "x1T"))
                    if s >= 2:
                        pe.wait_ge(*V.at(k, s - 2, "tb"))
                    for j in range(G):
                        for c_ in range(KC):
                            last = nc.tensor.matmul(pH[s % 2][0:R, j, :], lhs("x1T", s, j, c_), g["W1x"][:, c_, 0:D],
                                                    start=(c_ == 0), stop=(c_ == KC - 1))
                    last.then_inc(M.sem, 1)
                for s in ss:
                    pe.wait_ge(*V.at(k, s, "x3"))
                    if s >= 2:
                        pe.wait_ge(*A.at(k, s - 2, "x3T"))
                    elif len(ss) > 1:
                        pe.wait_ge(*A.at(k, 2, "x1T"))
                    flip(s, "x3").then_inc(M.sem, 1)
                for s in ss:
                    pe.wait_ge(*A.at(k, s, "x3T"))
                    if s >= 2:
                        pe.wait_ge(*V.at(k, s - 2, "q"))
                    for j in range(G):
                        if s >= 1:
                            pe.wait_ge(*A.at(k, s - 1, f"rz{j}"))
                        nc.tensor.matmul(pRZ[j][0:R, :], g["ones_b"][:, 0:R], g["bias3"][:, 0:2 * D],
                                         start=True, stop=False)
                        for c_ in range(KC):
                            nc.tensor.matmul(pRZ[j][0:R, :], lhs("x3T", s, j, c_), g["whhT"][:, c_, 0:2 * D],
                                             start=False, stop=(c_ == KC - 1))
                        nc.tensor.matmul(pN[s % 2][0:R, j, :], g["ones_b"][:, 0:R], g["bias3"][:, 2 * D:3 * D],
                                         start=True, stop=False)
                        for c_ in range(KC):
                            last = nc.tensor.matmul(pN[s % 2][0:R, j, :], lhs("x3T", s, j, c_),
                                                    g["whhT"][:, c_, 2 * D:3 * D], start=False, stop=(c_ == KC - 1))
                        last.then_inc(M.sem, 1)
            rounds(pe, body)


def slot_steps(sm, c, name, stages, slots):
    return {e: Steps(sm(f"{name}_{e}", c), stages[e], slots) for e in stages}


def edge_norms(nc, g):
    sb, ps, sm, NB, U, L, x = (g[n] for n in ("sb", "ps", "sm", "NB", "U", "L", "x"))
    with ExitStack() as c:
        slots = list(range(U))
        stages = {"pool": ["ix"], "mat": ["t", "h"], "scal": ["T", "msg", "sq"], "vec": ["lk"]}
        S = slot_steps(sm, c, "norms", stages, slots)
        O, M, A, V = S["pool"], S["mat"], S["scal"], S["vec"]
        gathered = [sm(f"n_gathered{s}", c) for s in slots]
        stored = [sm(f"n_stored{s}", c) for s in slots]
        lock_loaded = sm("lock_loaded", c)
        ready = sm("n_ready", c)
        lock_i = sb("lock_i", [P, L], I32, c)
        lock_f = sb("lock_f", [P, L], F32, c)
        hit = [sb(f"hit{s}", [P, L], F32, c) for s in slots]
        lockc = sb("lockc", [P, NB], F32, c)
        n2 = sb("n2", [P, NB], F32, c)
        ix = [sb(f"n_ix{s}", [P, 1], I32, c) for s in slots]
        Xs = [sb(f"n_Xs{s}", [P, D], F32, c) for s in slots]
        XT = [sb(f"n_XT{s}", [P, KC, P], F32, c) for s in slots]
        msg = [sb(f"n_msg{s}", [P, D], F32, c) for s in slots]
        msq = [sb(f"n_msq{s}", [P, D], F32, c) for s in slots]
        pT = [ps(f"n_pT{i}", [P, KC, P], c) for i in range(U)]
        pH = [ps(f"n_pH{i}", [P, D], c) for i in range(U)]
        ROUNDS = NB // U
        with nc.Block() as block:
            @block.gpsimd
            def _(pool):
                nc.gpsimd.sem_inc(O.sem, O.lead)
                with pool.Fori(0, ROUNDS) as k:
                    for s in slots:
                        pool.wait_ge(*M.before(k, s, "t"))
                        nc.gpsimd.tensor_copy(ix[s][:, :], g["src_i"][:, bass.ds(k * U + s, 1)]).then_inc(O.sem, 1)
                        pool.wait_ge(*O.at(k, s, "ix"))
                        nc.gpsimd.nop(nofuse=True)
                        nc.gpsimd.indirect_dma_start(
                            out=Xs[s][:, :], out_offset=None, in_=x[:, :],
                            in_offset=bass.IndirectOffsetOnAxis(ap=ix[s][:, 0:1], axis=0)).then_inc(gathered[s], 16)

            @block.tensor
            def _(pe):
                nc.tensor.sem_inc(M.sem, M.lead)
                with pe.Fori(0, ROUNDS) as k:
                    for s in slots:
                        pe.wait_ge(gathered[s], (k + 1) * 16)
                        pe.wait_ge(*A.before(k, s, "T"))
                        for j in range(KC):
                            last = nc.tensor.transpose(pT[s][:, j, :], Xs[s][:, j * P:(j + 1) * P], g["ident"][:, :])
                        last.then_inc(M.sem, 1)
                    for s in slots:
                        pe.wait_ge(*A.at(k, s, "T"))
                        for j in range(KC):
                            last = nc.tensor.matmul(pH[s][:, :], XT[s][:, j, :], g["Weff_T"][:, j, :],
                                                    start=(j == 0), stop=(j == KC - 1))
                        last.then_inc(M.sem, 1)

            @block.scalar
            def _(act):
                nc.scalar.sem_inc(A.sem, A.lead)
                with act.Fori(0, ROUNDS) as k:
                    for s in slots:
                        act.wait_ge(*M.at(k, s, "t"))
                        nc.scalar.activation(XT[s][:, :, :], pT[s][:, :, :], ACT.Copy).then_inc(A.sem, 1)
                    for s in slots:
                        act.wait_ge(*M.at(k, s, "h"))
                        act.wait_ge(stored[s], k * 16 + 16)
                        nc.scalar.activation(msg[s][:, :], pH[s][:, :], ACT.Copy,
                                             scale=g["w_e"][:, bass.ds(k * U + s, 1)]).then_inc(A.sem, 1)
                    for s in slots:
                        act.wait_ge(*A.at(k, s, "msg"))
                        nc.scalar.activation(msq[s][:, :], msg[s][:, :], ACT.Square,
                                             accum_out=n2[:, bass.ds(k * U + s, 1)]).then_inc(A.sem, 1)

            @block.sync
            def _(sp):
                for s in slots:
                    sp.sem_inc(stored[s], 16)
                sp.dma_start(lock_i[:, :], bcast_rows(g["node_lock"], P, L)).then_inc(lock_loaded, 16)
                with sp.Fori(0, ROUNDS) as k:
                    for s in slots:
                        sp.wait_ge(*A.at(k, s, "msg"))
                        sp.dma_start(g["MSG"][bass.ds((k * U + s) * P, P), :], msg[s][:, :]).then_inc(stored[s], 16)
                for s in slots:
                    sp.wait_ge(stored[s], 16 * ROUNDS + 16)

            @block.vector
            def _(dve):
                nc.vector.sem_inc(V.sem, V.lead)
                dve.wait_ge(lock_loaded, 16)
                nc.vector.tensor_copy(lock_f[:, :], lock_i[:, :]).then_inc(ready, 1)
                dve.wait_ge(ready, 1)
                with dve.Fori(0, ROUNDS) as k:
                    for s in slots:
                        dve.wait_ge(*V.before(k, s, "lk"))
                        nc.vector.tensor_scalar(hit[s][:, :], lock_f[:, :], g["dst_f"][:, bass.ds(k * U + s, 1)], 0.0,
                                                ALU.is_equal, ALU.add, accum_out=lockc[:, bass.ds(k * U + s, 1)])\
                            .then_inc(V.sem, 1)

        tot = sb("n_tot", [P, 1], F32, c)
        thr = sb("n_thr", [P, 1], F32, c)
        norm = sb("n_norm", [P, NB], F32, c)
        m0 = sb("n_m0", [P, NB], F32, c)
        m1 = sb("n_m1", [P, NB], F32, c)
        lk = sb("n_lk", [P, NB], F32, c)
        eq = sb("n_eq", [P, NB], F32, c)
        onesf = sb("n_ones", [P, P], F32, c)
        pX = ps("n_pX", [P, 1], c)
        sqrt_done, dve_done, total_done = sm("sqrt_done", c), sm("keep_dve", c), sm("total_done", c)
        with nc.Block() as block:
            @block.scalar
            def _(act):
                nc.scalar.activation(norm[:, :], n2[:, :], ACT.Sqrt).then_inc(sqrt_done, 1)

            @block.tensor
            def _(pe):
                pe.wait_ge(dve_done, 2)
                nc.tensor.matmul(pX[:, :], onesf[:, :], tot[:, :], start=True, stop=True).then_inc(total_done, 1)

            @block.vector
            def _(dve):
                count = [0]

                def done(ins):
                    count[0] += 1
                    ins.then_inc(dve_done, 1)
                    dve.wait_ge(dve_done, count[0])

                done(nc.vector.memset(onesf[:, :], 1.0))
                dve.wait_ge(sqrt_done, 1)
                done(nc.vector.tensor_reduce(tot[:, :], norm[:, :], AX.X, ALU.add))
                dve.wait_ge(total_done, 1)
                done(nc.vector.tensor_scalar(thr[:, :], pX[:, :], 1.0 / g["NEDGE"], THR_A, ALU.mult, ALU.mult))
                nc.vector.tensor_tensor(eq[:, :], g["src_f"][:, :], g["dst_f"][:, :], ALU.is_equal)
                nc.vector.tensor_scalar(lk[:, :], lockc[:, :], 0.5, None, ALU.is_gt)
                done(nc.vector.tensor_scalar(m0[:, :], norm[:, :], thr[:, :], None, ALU.is_lt))
                done(nc.vector.tensor_scalar(m1[:, :], m0[:, :], -1.0, 1.0, ALU.mult, ALU.add))
                done(nc.vector.tensor_tensor(lk[:, :], lk[:, :], eq[:, :], ALU.max))
                done(nc.vector.tensor_tensor(g["keep"][:, :], m1[:, :], lk[:, :], ALU.max))


class EdgePass:

    def __init__(self, nc, g, c, name, stages, table, into):
        self.nc, self.g, self.c, self.name, self.table, self.into = nc, g, c, name, table, into
        self.NB, self.U = g["NB"], g["U"]
        self.N = g["N"]
        self.slots = list(range(self.U))
        self.ROUNDS = self.NB // self.U
        S = slot_steps(g["sm"], c, name, stages, self.slots)
        self.V, self.O, self.A, self.M = S["vec"], S["pool"], S["scal"], S["mat"]
        self.Xd = self.tiles("Xd", [P, D])
        self.v = self.tiles("v", [P, D])
        self.xn = self.tiles("xn", [P, D])
        self.st = self.tiles("st", [P, 6])
        self.mv = self.tiles("mv", [P, 2])
        self.ve = self.tiles("ve", [P, 1])
        self.rs = self.tiles("rs", [P, 1])
        self.dc = self.tiles("dc", [P, P], I32)
        self.eq = self.tiles("eq", [P, P])
        self.ixs = self.tiles("ixs", [P, 1], I32)
        self.ixd = self.tiles("ixd", [P, 1], I32)
        self.ixp = self.tiles("ixp", [P, 1], I32)
        self.src_in, self.dst_in, self.cols_in, self.put_out = (
            [g["sm"](f"{name}_{n}{s}", c) for s in self.slots] for n in ("src_in", "dst_in", "cols_in", "put_out"))

    def tiles(self, n, shape, dt=F32):
        return [self.g["sb"](f"{self.name}_{n}{s}", shape, dt, self.c) for s in self.slots]

    def banks(self, n, shape, count):
        return [self.g["ps"](f"{self.name}_{n}{i}", shape, self.c) for i in range(count)]

    def block_of(self, k, s):
        return bass.ds(k * self.U + s, 1)

    def carry_from(self, k, s, steps, name):
        return steps.at(k, s - 1, name) if s else steps.before(k, self.U - 1, name)

    def gather(self, pool, k, s, ix, index, into, sem):
        nc, O = self.nc, self.O
        nc.gpsimd.tensor_copy(ix[s][:, :], self.g[index][:, self.block_of(k, s)]).then_inc(O.sem, 1)
        pool.wait_ge(*O.at(k, s, index))
        nc.gpsimd.nop(nofuse=True)
        nc.gpsimd.indirect_dma_start(out=into, out_offset=None, in_=self.table[:, :],
                                     in_offset=bass.IndirectOffsetOnAxis(ap=ix[s][:, 0:1], axis=0)).then_inc(sem[s], 16)

    def scatter(self, pool, k, s):
        nc, O = self.nc, self.O
        pool.wait_ge(self.put_out[s], k * 16 + 16)
        nc.gpsimd.tensor_copy(self.ixp[s][:, :], self.g["put_i"][:, self.block_of(k, s)]).then_inc(O.sem, 1)
        pool.wait_ge(*O.at(k, s, "put"))
        pool.wait_ge(*self.V.at(k, s, "xn"))
        nc.gpsimd.nop(nofuse=True)
        nc.gpsimd.indirect_dma_start(out=self.into[:, :],
                                     out_offset=bass.IndirectOffsetOnAxis(ap=self.ixp[s][:, 0:1], axis=0),
                                     in_=self.xn[s][:, :], in_offset=None, bounds_check=self.N - 1,
                                     oob_is_err=False).then_inc(self.put_out[s], 16)

    def rstd(self, pool, k, s):
        nc, O = self.nc, self.O
        pool.wait_ge(*self.V.at(k, s, "ag"))
        nc.gpsimd.tensor_tensor(self.ve[s][:, :], self.mv[s][:, 1:2], self.g["eps_c"][:, 0:1], ALU.add)\
            .then_inc(O.sem, 1)
        pool.wait_ge(*O.at(k, s, "e"))
        nc.gpsimd.tensor_tensor(self.rs[s][:, :], self.ve[s][:, :], self.g["mhalf"][:, 0:1], ALU.pow)\
            .then_inc(O.sem, 1)

    def stats(self, dve, k, s):
        nc, V = self.nc, self.V
        nc.vector.bn_stats(self.st[s][:, :], self.v[s][:, :]).then_inc(V.sem, 1)
        dve.wait_ge(*V.at(k, s, "st"))
        nc.vector.nop(nofuse=True)
        nc.vector.bn_aggr(self.mv[s][:, :], self.st[s][:, :]).then_inc(V.sem, 1)

    def normalise(self, dve, k, s):
        dve.wait_ge(*self.O.at(k, s, "r"))
        dve.wait_ge(self.put_out[s], k * 16 + 16)
        self.nc.vector.tensor_scalar(self.xn[s][:, :], self.v[s][:, :], self.mv[s][:, 0:1], self.rs[s][:, :],
                                     ALU.subtract, ALU.mult).then_inc(self.V.sem, 1)

    def load_cols(self, sp, k, s):
        a = self.g["dst_cols"][self.block_of(k, s), :]
        sp.dma_start(self.dc[s][:, :], a.to_broadcast([P, P])).then_inc(self.cols_in[s], 16)

    def lead_out(self, pool):
        for s in self.slots:
            pool.dma_start(self.xn[s][:, :], self.table[0:P, :]).then_inc(self.put_out[s], 16)

    def wait_out(self, sp):
        for s in self.slots:
            sp.wait_ge(self.put_out[s], 16 * self.ROUNDS + 16)


def edge_sum(nc, g):
    with ExitStack() as c:
        stages = {"pool": ["dst_i", "vb", "e r", "put"], "mat": ["ag"], "scal": [], "vec": ["eq", "cy", "v", "st ag", "xn"]}
        E = EdgePass(nc, g, c, "sum", stages, g["x"], g["X1"])
        V, O, M, slots, ROUNDS = E.V, E.O, E.M, E.slots, E.ROUNDS
        m = E.tiles("m", [P, D])
        v0 = E.tiles("v0", [P, D])
        m_in = [g["sm"](f"sum_m_in{s}", c) for s in slots]
        cleared = g["sm"]("sum_cleared", c)
        pA = E.banks("pA", [P, D], E.U)
        with nc.Block() as block:
            @block.sync
            def _(sp):
                with sp.Fori(0, ROUNDS) as k:
                    for s in slots:
                        sp.wait_ge(*M.before(k, s, "ag"))
                        sp.dma_start(m[s][:, :], g["MSG"][bass.ds((k * E.U + s) * P, P), :]).then_inc(m_in[s], 16)
                        E.load_cols(sp, k, s)
                E.wait_out(sp)

            @block.gpsimd
            def _(pool):
                nc.gpsimd.sem_inc(O.sem, O.lead)
                E.lead_out(pool)
                with pool.Fori(0, ROUNDS) as k:
                    for s in slots:
                        pool.wait_ge(*V.before(k, s, "v"))
                        E.gather(pool, k, s, E.ixd, "dst_i", E.Xd[s][:, :], E.dst_in)
                    for s in slots:
                        pool.wait_ge(*V.at(k, s, "v"))
                        nc.gpsimd.tensor_tensor(E.v[s][:, :], v0[s][:, :], g["b0e_r"][:, :], ALU.add)\
                            .then_inc(O.sem, 1)
                    for s in slots:
                        E.rstd(pool, k, s)
                    for s in slots:
                        E.scatter(pool, k, s)

            @block.tensor
            def _(pe):
                nc.tensor.sem_inc(M.sem, M.lead)
                pe.wait_ge(cleared, 1)
                with pe.Fori(0, ROUNDS) as k:
                    for s in slots:
                        pe.wait_ge(*V.at(k, s, "cy"))
                        nc.tensor.matmul(pA[s][:, :], E.eq[s][:, :], m[s][:, :], start=True, stop=True)\
                            .then_inc(M.sem, 1)

            @block.vector
            def _(dve):
                nc.vector.sem_inc(V.sem, V.lead)
                nc.vector.memset(pA[E.U - 1][:, :], 0.0).then_inc(cleared, 1)
                dve.wait_ge(cleared, 1)
                with dve.Fori(0, ROUNDS) as k:
                    for s in slots:
                        dve.wait_ge(E.cols_in[s], (k + 1) * 16)
                        nc.vector.tensor_scalar(E.eq[s][:, :], E.dc[s][:, :], g["dst_f"][:, E.block_of(k, s)],
                                                g["keep"][:, E.block_of(k, s)], ALU.is_equal, ALU.mult)\
                            .then_inc(V.sem, 1)
                    for s in slots:
                        dve.wait_ge(m_in[s], (k + 1) * 16)
                        dve.wait_ge(*E.carry_from(k, s, M, "ag"))
                        nc.vector.tensor_copy(m[s][0:1, :], pA[s - 1][0:1, :]).then_inc(V.sem, 1)
                    for s in slots:
                        dve.wait_ge(*M.at(k, s, "ag"))
                        dve.wait_ge(E.dst_in[s], (k + 1) * 16)
                        nc.vector.tensor_tensor(v0[s][:, :], pA[s][:, :], E.Xd[s][:, :], ALU.add).then_inc(V.sem, 1)
                    for s in slots:
                        dve.wait_ge(*O.at(k, s, "vb"))
                        E.stats(dve, k, s)
                    for s in slots:
                        E.normalise(dve, k, s)


class SegmentMax:

    STEPS = "ne kl LT fw bw"

    def __init__(self, E, H, own):
        self.E, self.H, self.own = E, H, own
        self.dv = E.tiles("dv", [H, P], I32)
        self.prev_in = [E.g["sm"](f"{E.name}_prev_in{s}", E.c) for s in E.slots]
        self.ne = E.tiles("ne", [H, P])
        self.kl = E.tiles("kl", [H, P + 1])
        self.LT = E.tiles("LT", [H, 2 * P])
        self.F = E.tiles("F", [H, P])
        self.B = E.tiles("B", [H, P])
        self.m = E.tiles("m", [H, P]) if own else self.B
        self.dl = E.tiles("dl", [H, 2 * P])
        self.ET = E.tiles("ET", [H, 2 * P])

    def load(self, sp, k, s):
        a = self.E.g["dst_prev"][self.E.block_of(k, s), :]
        sp.dma_start(self.dv[s][:, :], a.to_broadcast([self.H, P])).then_inc(self.prev_in[s], 16)

    def start(self, nc, done):
        for s in self.E.slots:
            done(nc.vector.memset(self.kl[s][:, P:P + 1], NONE))
            done(nc.vector.memset(self.dl[s][:, :], 0.0))
        done(nc.vector.memset(self.m[self.E.U - 1][:, :], NONE))

    def breaks(self, dve, k, s):
        nc, V, H = self.E.nc, self.E.V, self.H
        dve.wait_ge(self.prev_in[s], (k + 1) * 16)
        dve.wait_ge(self.E.cols_in[s], (k + 1) * 16)
        nc.vector.tensor_tensor(self.ne[s][:, :], self.dv[s][:, :], self.E.dc[s][0:H, :], ALU.not_equal)\
            .then_inc(V.sem, 1)
        dve.wait_ge(*V.at(k, s, "ne"))
        nc.vector.tensor_scalar(self.kl[s][:, 0:P], self.ne[s][:, :], NONE, None, ALU.mult).then_inc(V.sem, 1)

    def maxima(self, dve, k, s):
        nc, V = self.E.nc, self.E.V
        kl, F, B, m, LT, dl = self.kl[s], self.F[s], self.B[s], self.m[s], self.LT[s], self.dl[s]
        before = self.m[s - 1][:, P - 1:P]
        dve.wait_ge(*V.at(k, s, "LT"))
        nc.vector.tensor_tensor_scan(F[:, 1:P], kl[:, 1:P], LT[:, 1:P], before, ALU.add, ALU.max).then_inc(V.sem, 1)
        dve.wait_ge(*V.at(k, s, "fw"))
        nc.vector.tensor_tensor_scan(B[:, P - 1:0:-1], kl[:, P:1:-1], F[:, P - 1:0:-1], NONE, ALU.add, ALU.max)\
            .then_inc(V.sem, 1)
        dve.wait_ge(*V.at(k, s, "bw"))
        if self.own:
            nc.vector.tensor_tensor(m[:, 1:P], B[:, 1:P], LT[:, P + 1:2 * P], ALU.max).then_inc(V.sem, 1)
            dve.wait_ge(*V.at(k, s, "mx"))
            nc.vector.tensor_tensor(dl[:, P + 1:2 * P], LT[:, P + 1:2 * P], m[:, 1:P], ALU.subtract)
        nc.vector.tensor_tensor(dl[:, 1:P], LT[:, 1:P], m[:, 1:P], ALU.subtract)
        nc.vector.tensor_scalar(dl[:, 0:1], before, m[:, 1:2], 0.0, ALU.subtract, ALU.min).then_inc(V.sem, 1)


def edge_heads(nc, g):
    with ExitStack() as c:
        stages = {
            "pool": ["src_i dst_i", "t1", "t4", "e r", "put"],
            "mat": ["t", "hs hd", "lt", "xr", "ag"],
            "scal": ["T", "hx hd", "ET", "ex"],
            "vec": ["eq ne kl", "lg lr", "LT", "fw bw mx dl", "x hw", "cy", "t2 de rd t3", "u v st ag", "xn"],
        }
        E = EdgePass(nc, g, c, "heads", stages, g["X1"], g["X2"])
        V, O, M, A, slots, ROUNDS = E.V, E.O, E.M, E.A, E.slots, E.ROUNDS
        W = HID + 1
        SM = SegmentMax(E, HEADS, True)
        Xs = E.tiles("Xs", [P, D])
        XT = E.tiles("XT", [P, 2 * KC, P])
        Hx = E.tiles("Hx", [P, HEADS, W])
        Hw = E.tiles("Hw", [P, HEADS, W])
        Hd = E.tiles("Hd", [P, D + 2 * HEADS])
        as_ = E.tiles("as", [P, HEADS])
        lg = E.tiles("lg", [P, 2, HEADS])
        lr = E.tiles("lr", [P, 2, HEADS])
        xw = E.tiles("xw", [P, 2, HEADS])
        t1, t2, t3, t4, ex, u = (E.tiles(n, [P, D]) for n in ("t1", "t2", "t3", "t4", "ex", "u"))
        de = E.tiles("de", [P, HEADS])
        rd = E.tiles("rd", [P, HEADS])
        started = g["sm"]("heads_started", c)
        pT = E.banks("pT", [P, 2 * KC, P], 1)[0]
        pHs = E.banks("pHs", [P, D + HEADS], 2)
        pHd = E.banks("pHd", [P, D + 2 * HEADS], 2)
        pA = E.banks("pA", [P, HEADS, W], 2)
        pS = E.banks("pS", [P, 512], 1)[0]
        head = lambda a: a.rearrange("p (h c) -> p h c", h=HEADS)
        per_head = lambda a, n: a.unsqueeze(2).to_broadcast([a.shape[0], HEADS, n])
        start_count = []

        with nc.Block() as block:
            @block.sync
            def _(sp):
                with sp.Fori(0, ROUNDS) as k:
                    for s in slots:
                        sp.wait_ge(*V.before(k, s, "kl"))
                        E.load_cols(sp, k, s)
                        SM.load(sp, k, s)
                E.wait_out(sp)

            @block.gpsimd
            def _(pool):
                nc.gpsimd.sem_inc(O.sem, O.lead)
                E.lead_out(pool)
                with pool.Fori(0, ROUNDS) as k:
                    for s in slots:
                        pool.wait_ge(*M.before(k, s, "t"))
                        E.gather(pool, k, s, E.ixs, "src_i", Xs[s][:, :], E.src_in)
                        pool.wait_ge(*V.before(k, s, "v"))
                        E.gather(pool, k, s, E.ixd, "dst_i", E.Xd[s][:, :], E.dst_in)
                    for s in slots:
                        pool.wait_ge(*V.at(k, s, "x"))
                        nc.gpsimd.tensor_tensor(head(t1[s][:, :]), head(Hd[s][:, 0:D]), per_head(xw[s][:, 1, :], HID),
                                                ALU.mult).then_inc(O.sem, 1)
                    for s in slots:
                        pool.wait_ge(*V.at(k, s, "t3"))
                        nc.gpsimd.tensor_tensor(t4[s][:, :], t3[s][:, :], g["b1m1_r"][:, :], ALU.add)\
                            .then_inc(O.sem, 1)
                    for s in slots:
                        E.rstd(pool, k, s)
                    for s in slots:
                        E.scatter(pool, k, s)

            @block.vector
            def _(dve):
                count = [0]

                def done(ins):
                    count[0] += 1
                    ins.then_inc(started, 1)
                    dve.wait_ge(started, count[0])

                nc.vector.sem_inc(V.sem, V.lead)
                SM.start(nc, done)
                for s in slots:
                    done(nc.vector.memset(Hx[s][:, :, :], 1.0))
                done(nc.vector.memset(pA[(E.U - 1) % 2][:, :, :], 0.0))
                start_count.append(count[0])
                with dve.Fori(0, ROUNDS) as k:
                    for s in slots:
                        dve.wait_ge(E.cols_in[s], (k + 1) * 16)
                        nc.vector.tensor_scalar(E.eq[s][:, :], E.dc[s][:, :], g["dst_f"][:, E.block_of(k, s)], None,
                                                ALU.is_equal).then_inc(V.sem, 1)
                        SM.breaks(dve, k, s)
                    for s in slots:
                        dve.wait_ge(*A.at(k, s, "hd"))
                        nc.vector.tensor_tensor(lg[s][:, 0, :], as_[s][:, :], Hd[s][:, D + HEADS:D + 2 * HEADS], ALU.add)
                        nc.vector.tensor_tensor(lg[s][:, 1, :], Hd[s][:, D:D + HEADS],
                                                Hd[s][:, D + HEADS:D + 2 * HEADS], ALU.add).then_inc(V.sem, 1)
                        dve.wait_ge(*V.at(k, s, "lg"))
                        nc.vector.scalar_tensor_tensor(lr[s][:, :, :], lg[s][:, :, :], SLOPE, lg[s][:, :, :],
                                                       ALU.mult, ALU.max).then_inc(V.sem, 1)
                    for s in slots:
                        dve.wait_ge(*M.at(k, s, "lt"))
                        nc.vector.tensor_copy(SM.LT[s][:, :], pS[0:HEADS, 0:2 * P]).then_inc(V.sem, 1)
                    for s in slots:
                        SM.maxima(dve, k, s)
                    for s in slots:
                        dve.wait_ge(*M.at(k, s, "xr"))
                        nc.vector.tensor_copy(xw[s][:, :, :].rearrange("p a h -> p (a h)"), pS[:, 2 * P:2 * P + 2 * HEADS])\
                            .then_inc(V.sem, 1)
                        dve.wait_ge(*V.at(k, s, "x"))
                        nc.vector.tensor_tensor(Hw[s][:, :, :], Hx[s][:, :, :], per_head(xw[s][:, 0, :], W), ALU.mult)\
                            .then_inc(V.sem, 1)
                    for s in slots:
                        dve.wait_ge(*V.at(k, s, "hw"))
                        dve.wait_ge(*E.carry_from(k, s, M, "ag"))
                        prev = pA[((s - 1) % E.U) % 2]
                        nc.vector.tensor_tensor(Hw[s][0:1, :, :], prev[0:1, :, :], per_head(xw[s][0:1, 0, :], W),
                                                ALU.mult).then_inc(V.sem, 1)
                    for s in slots:
                        dve.wait_ge(*M.at(k, s, "ag"))
                        dve.wait_ge(*O.at(k, s, "t1"))
                        nc.vector.tensor_tensor(head(t2[s][:, :]), pA[s % 2][:, :, 0:HID], head(t1[s][:, :]), ALU.add)\
                            .then_inc(V.sem, 1)
                        nc.vector.scalar_tensor_tensor(de[s][:, :], pA[s % 2][:, :, HID], 1e-16, xw[s][:, 1, :],
                                                       ALU.add, ALU.add).then_inc(V.sem, 1)
                        dve.wait_ge(*V.at(k, s, "de"))
                        nc.vector.reciprocal(rd[s][:, :], de[s][:, :]).then_inc(V.sem, 1)
                        dve.wait_ge(*V.at(k, s, "rd"))
                        nc.vector.tensor_tensor(head(t3[s][:, :]), head(t2[s][:, :]), per_head(rd[s][:, :], HID),
                                                ALU.mult).then_inc(V.sem, 1)
                    for s in slots:
                        dve.wait_ge(*O.at(k, s, "t4"))
                        nc.vector.scalar_tensor_tensor(u[s][:, :], t4[s][:, :], -1.0, E.Xd[s][:, :], ALU.max, ALU.add)\
                            .then_inc(V.sem, 1)
                        dve.wait_ge(*A.at(k, s, "ex"))
                        dve.wait_ge(*V.at(k, s, "u"))
                        nc.vector.scalar_tensor_tensor(E.v[s][:, :], ex[s][:, :], 1.0, u[s][:, :], ALU.min, ALU.add)\
                            .then_inc(V.sem, 1)
                        dve.wait_ge(*V.at(k, s, "v"))
                        E.stats(dve, k, s)
                    for s in slots:
                        E.normalise(dve, k, s)

            @block.tensor
            def _(pe):
                nc.tensor.sem_inc(M.sem, M.lead)
                pe.wait_ge(started, start_count[0])
                with pe.Fori(0, ROUNDS) as k:
                    for s in slots:
                        pe.wait_ge(E.src_in[s], (k + 1) * 16)
                        pe.wait_ge(E.dst_in[s], (k + 1) * 16)
                        pe.wait_ge(*E.carry_from(k, s, A, "T"))
                        for a, rows in enumerate((Xs, E.Xd)):
                            for j in range(KC):
                                last = nc.tensor.transpose(pT[:, a * KC + j, :], rows[s][:, j * P:(j + 1) * P],
                                                           g["ident"][:, :])
                        last.then_inc(M.sem, 1)
                    for s in slots:
                        pe.wait_ge(*A.at(k, s, "T"))
                        if s >= 2:
                            pe.wait_ge(*A.at(k, s - 2, "hd"))
                        for j in range(KC):
                            last = nc.tensor.matmul(pHs[s % 2][:, :], XT[s][:, j, :], g["W1x"][:, j, 0:D + HEADS],
                                                    start=(j == 0), stop=(j == KC - 1))
                        last.then_inc(M.sem, 1)
                        for j in range(KC):
                            last = nc.tensor.matmul(pHd[s % 2][:, :], XT[s][:, KC + j, :], g["W1x"][:, j, :],
                                                    start=(j == 0), stop=(j == KC - 1))
                        last.then_inc(M.sem, 1)
                    for s in slots:
                        pe.wait_ge(*V.at(k, s, "lr"))
                        if s:
                            pe.wait_ge(*V.at(k, s - 1, "LT"))
                        for a in range(2):
                            last = nc.tensor.transpose(pS[0:HEADS, a * P:(a + 1) * P], lr[s][:, a, :], g["ident"][:, :])
                        last.then_inc(M.sem, 1)
                    for s in slots:
                        pe.wait_ge(*A.at(k, s, "ET"))
                        pe.wait_ge(*(V.at(k, s - 1, "x") if s else V.at(k, E.U - 1, "LT")))
                        for a in range(2):
                            last = nc.tensor.matmul(pS[:, 2 * P + a * HEADS:2 * P + (a + 1) * HEADS],
                                                    SM.ET[s][:, a * P:(a + 1) * P], g["ident"][0:HEADS, 0:HEADS],
                                                    start=True, stop=True)
                        last.then_inc(M.sem, 1)
                    for s in slots:
                        pe.wait_ge(*V.at(k, s, "cy"))
                        if s >= 2:
                            pe.wait_ge(*V.at(k, s - 2, "de"))
                        nc.tensor.matmul(pA[s % 2][:, :, :].rearrange("p h c -> p (h c)"), E.eq[s][:, :],
                                         Hw[s][:, :, :].rearrange("p h c -> p (h c)"), start=True, stop=True)\
                            .then_inc(M.sem, 1)

            @block.scalar
            def _(act):
                nc.scalar.sem_inc(A.sem, A.lead)
                act.wait_ge(started, start_count[0])
                with act.Fori(0, ROUNDS) as k:
                    for s in slots:
                        act.wait_ge(*M.at(k, s, "t"))
                        nc.scalar.activation(XT[s][:, :, :], pT[:, :, :], ACT.Copy).then_inc(A.sem, 1)
                    for s in slots:
                        act.wait_ge(*M.at(k, s, "hs"))
                        nc.scalar.activation(Hx[s][:, :, 0:HID], head(pHs[s % 2][:, 0:D]), ACT.Copy)
                        nc.scalar.activation(as_[s][:, :], pHs[s % 2][:, D:D + HEADS], ACT.Copy).then_inc(A.sem, 1)
                        act.wait_ge(*M.at(k, s, "hd"))
                        act.wait_ge(*O.before(k, s, "t1"))
                        nc.scalar.activation(Hd[s][:, :], pHd[s % 2][:, :], ACT.Copy).then_inc(A.sem, 1)
                    for s in slots:
                        act.wait_ge(*V.at(k, s, "dl"))
                        nc.scalar.activation(SM.ET[s][:, :], SM.dl[s][:, :], ACT.Exp).then_inc(A.sem, 1)
                    for s in slots:
                        act.wait_ge(*O.at(k, s, "t4"))
                        nc.scalar.activation(ex[s][:, :], t4[s][:, :], ACT.Exp, bias=1.0).then_inc(A.sem, 1)


def edge_attention(nc, g):
    with ExitStack() as c:
        stages = {
            "pool": ["src_i dst_i", "e r", "put"],
            "mat": ["lt", "xr", "ag", "t", "h"],
            "scal": ["ET", "T"],
            "vec": ["s1 s2 lg lr", "ne kl", "LT", "fw bw dl", "x eq", "cy", "A rd", "v st ag", "xn"],
        }
        E = EdgePass(nc, g, c, "att", stages, g["X2"], g["X3"])
        V, O, M, A, slots, ROUNDS = E.V, E.O, E.M, E.A, E.slots, E.ROUNDS
        W = D + 1
        SM = SegmentMax(E, 1, False)
        Xs = E.tiles("Xs", [P, W])
        junk = E.tiles("junk", [P, D])
        junk2 = E.tiles("junk2", [P, D])
        sc = E.tiles("sc", [P, 2])
        lg = E.tiles("lg", [P, 1])
        lr = E.tiles("lr", [P, 1])
        xw = E.tiles("xw", [P, 1])
        As = E.tiles("As", [P, W])
        AT = E.tiles("AT", [P, KC, P])
        rd = E.tiles("rd", [P, 1])
        started = g["sm"]("att_started", c)
        pT = E.banks("pT", [P, KC, P], 1)[0]
        pH = E.banks("pH", [P, D], 2)
        pA = E.banks("pA", [P, W], E.U)
        pS = E.banks("pS", [P, 512], 1)[0]
        start_count = []

        with nc.Block() as block:
            @block.sync
            def _(sp):
                with sp.Fori(0, ROUNDS) as k:
                    for s in slots:
                        sp.wait_ge(*V.before(k, s, "eq"))
                        E.load_cols(sp, k, s)
                        SM.load(sp, k, s)
                E.wait_out(sp)

            @block.gpsimd
            def _(pool):
                nc.gpsimd.sem_inc(O.sem, O.lead)
                E.lead_out(pool)
                with pool.Fori(0, ROUNDS) as k:
                    for s in slots:
                        pool.wait_ge(*M.before(k, s, "ag"))
                        E.gather(pool, k, s, E.ixs, "src_i", Xs[s][:, 0:D], E.src_in)
                        pool.wait_ge(*V.before(k, s, "v"))
                        E.gather(pool, k, s, E.ixd, "dst_i", E.Xd[s][:, :], E.dst_in)
                    for s in slots:
                        E.rstd(pool, k, s)
                    for s in slots:
                        E.scatter(pool, k, s)

            @block.vector
            def _(dve):
                count = [0]

                def done(ins):
                    count[0] += 1
                    ins.then_inc(started, 1)
                    dve.wait_ge(started, count[0])

                nc.vector.sem_inc(V.sem, V.lead)
                SM.start(nc, done)
                for s in slots:
                    done(nc.vector.memset(Xs[s][:, D:W], 1.0))
                done(nc.vector.memset(pA[E.U - 1][:, :], 0.0))
                start_count.append(count[0])
                with dve.Fori(0, ROUNDS) as k:
                    for s in slots:
                        dve.wait_ge(E.src_in[s], (k + 1) * 16)
                        nc.vector.tensor_tensor_reduce(out=junk[s][:, :], in0=Xs[s][:, 0:D], in1=g["us_r"][:, :],
                                                       scale=1.0, scalar=0.0, op0=ALU.mult, op1=ALU.add,
                                                       accum_out=sc[s][:, 0:1]).then_inc(V.sem, 1)
                        dve.wait_ge(E.dst_in[s], (k + 1) * 16)
                        nc.vector.tensor_tensor_reduce(out=junk2[s][:, :], in0=E.Xd[s][:, :], in1=g["ud_r"][:, :],
                                                       scale=1.0, scalar=0.0, op0=ALU.mult, op1=ALU.add,
                                                       accum_out=sc[s][:, 1:2]).then_inc(V.sem, 1)
                        dve.wait_ge(*V.at(k, s, "s2"))
                        nc.vector.scalar_tensor_tensor(lg[s][:, :], sc[s][:, 0:1], sc[s][:, 1:2],
                                                       g["efeat"][:, E.block_of(k, s)], ALU.add, ALU.add)\
                            .then_inc(V.sem, 1)
                        dve.wait_ge(*V.at(k, s, "lg"))
                        nc.vector.scalar_tensor_tensor(lr[s][:, :], lg[s][:, :], SLOPE, lg[s][:, :],
                                                       ALU.mult, ALU.max).then_inc(V.sem, 1)
                    for s in slots:
                        SM.breaks(dve, k, s)
                    for s in slots:
                        dve.wait_ge(*M.at(k, s, "lt"))
                        nc.vector.tensor_copy(SM.LT[s][:, 0:P], pS[0:1, 0:P]).then_inc(V.sem, 1)
                    for s in slots:
                        SM.maxima(dve, k, s)
                    for s in slots:
                        dve.wait_ge(*M.at(k, s, "xr"))
                        nc.vector.tensor_copy(xw[s][:, :], pS[:, 2 * P:2 * P + 1]).then_inc(V.sem, 1)
                        dve.wait_ge(*V.at(k, s, "x"))
                        nc.vector.tensor_scalar(E.eq[s][:, :], E.dc[s][:, :], g["dst_f"][:, E.block_of(k, s)],
                                                xw[s][:, :], ALU.is_equal, ALU.mult).then_inc(V.sem, 1)
                    for s in slots:
                        dve.wait_ge(*E.carry_from(k, s, M, "ag"))
                        nc.vector.tensor_copy(Xs[s][0:1, :], pA[s - 1][0:1, :]).then_inc(V.sem, 1)
                    for s in slots:
                        dve.wait_ge(*M.at(k, s, "ag"))
                        nc.vector.tensor_copy(As[s][:, :], pA[s][:, :]).then_inc(V.sem, 1)
                        dve.wait_ge(*V.at(k, s, "A"))
                        nc.vector.reciprocal(rd[s][:, :], As[s][:, D:W]).then_inc(V.sem, 1)
                    for s in slots:
                        dve.wait_ge(*M.at(k, s, "h"))
                        dve.wait_ge(*V.at(k, s, "rd"))
                        nc.vector.scalar_tensor_tensor(E.v[s][:, :], pH[s % 2][:, :], rd[s][:, :], E.Xd[s][:, :],
                                                       ALU.mult, ALU.add).then_inc(V.sem, 1)
                        dve.wait_ge(*V.at(k, s, "v"))
                        E.stats(dve, k, s)
                    for s in slots:
                        E.normalise(dve, k, s)

            @block.tensor
            def _(pe):
                nc.tensor.sem_inc(M.sem, M.lead)
                pe.wait_ge(started, start_count[0])
                with pe.Fori(0, ROUNDS) as k:
                    for s in slots:
                        pe.wait_ge(*V.at(k, s, "lr"))
                        if s:
                            pe.wait_ge(*V.at(k, s - 1, "LT"))
                        nc.tensor.transpose(pS[0:1, 0:P], lr[s][:, :], g["ident"][:, :]).then_inc(M.sem, 1)
                    for s in slots:
                        pe.wait_ge(*A.at(k, s, "ET"))
                        pe.wait_ge(*(V.at(k, s - 1, "x") if s else V.at(k, E.U - 1, "LT")))
                        nc.tensor.matmul(pS[:, 2 * P:2 * P + 1], SM.ET[s][:, 0:P], g["ident"][0:1, 0:1],
                                         start=True, stop=True)\
                            .then_inc(M.sem, 1)
                    for s in slots:
                        pe.wait_ge(*V.at(k, s, "cy"))
                        nc.tensor.matmul(pA[s][:, :], E.eq[s][:, :], Xs[s][:, :], start=True, stop=True)\
                            .then_inc(M.sem, 1)
                    for s in slots:
                        pe.wait_ge(*V.at(k, s, "A"))
                        pe.wait_ge(*E.carry_from(k, s, A, "T"))
                        for j in range(KC):
                            last = nc.tensor.transpose(pT[:, j, :], As[s][:, j * P:(j + 1) * P], g["ident"][:, :])
                        last.then_inc(M.sem, 1)
                    for s in slots:
                        pe.wait_ge(*A.at(k, s, "T"))
                        if s >= 2:
                            pe.wait_ge(*V.at(k, s - 2, "v"))
                        for j in range(KC):
                            last = nc.tensor.matmul(pH[s % 2][:, :], AT[s][:, j, :], g["W2T"][:, j, :],
                                                    start=(j == 0), stop=(j == KC - 1))
                        last.then_inc(M.sem, 1)

            @block.scalar
            def _(act):
                nc.scalar.sem_inc(A.sem, A.lead)
                with act.Fori(0, ROUNDS) as k:
                    for s in slots:
                        act.wait_ge(*V.at(k, s, "dl"))
                        nc.scalar.activation(SM.ET[s][:, 0:P], SM.dl[s][:, 0:P], ACT.Exp).then_inc(A.sem, 1)
                    for s in slots:
                        act.wait_ge(*M.at(k, s, "t"))
                        nc.scalar.activation(AT[s][:, :, :], pT[:, :, :], ACT.Copy).then_inc(A.sem, 1)


def edge_gru(nc, g):
    with ExitStack() as c:
        stages = {
            "pool": ["src_i dst_i", "q2", "d s", "e r", "put"],
            "mat": ["ag", "ct", "t", "gru"],
            "scal": ["cT", "aT", "rz", "n"],
            "vec": ["oh eq", "cy", "A", "q q1", "w v st ag", "xn"],
        }
        E = EdgePass(nc, g, c, "gru", stages, g["X3"], g["out"])
        V, O, M, A, slots, ROUNDS = E.V, E.O, E.M, E.A, E.slots, E.ROUNDS
        W = D + RELS
        Xs = E.tiles("Xs", [P, W])
        As = E.tiles("As", [P, W])
        aT = E.tiles("aT", [P, 2 * KC, P])
        cT = E.tiles("cT", [RELS, P])
        rz = E.tiles("rz", [P, 2 * D])
        q, q1, q2, n, d, sm_, w = (E.tiles(m, [P, D]) for m in ("q", "q1", "q2", "n", "d", "sm", "w"))
        rel_i = g["sb"]("rel_i", [P, RELS], I32, c)
        rel_f = g["sb"]("rel_f", [P, RELS], F32, c)
        started = g["sm"]("gru_started", c)
        pA = E.banks("pA", [P, W], 2)
        pC = E.banks("pC", [RELS, P], 1)[0]
        pT = E.banks("pT", [P, 2 * KC, P], 1)[0]
        pRZ = E.banks("pRZ", [P, 2 * D], 2)
        pN = E.banks("pN", [P, 2, D], 2)

        with nc.Block() as block:
            @block.sync
            def _(sp):
                with sp.Fori(0, ROUNDS) as k:
                    for s in slots:
                        sp.wait_ge(*V.before(k, s, "eq"))
                        E.load_cols(sp, k, s)
                E.wait_out(sp)

            @block.gpsimd
            def _(pool):
                nc.gpsimd.sem_inc(O.sem, O.lead)
                E.lead_out(pool)
                nc.gpsimd.iota(rel_i[:, :], pattern=[[1, RELS]], base=0, channel_multiplier=0).then_inc(started, 1)
                with pool.Fori(0, ROUNDS) as k:
                    for s in slots:
                        pool.wait_ge(*M.before(k, s, "ag"))
                        E.gather(pool, k, s, E.ixs, "src_i", Xs[s][:, 0:D], E.src_in)
                        pool.wait_ge(*V.before(k, s, "v"))
                        E.gather(pool, k, s, E.ixd, "dst_i", E.Xd[s][:, :], E.dst_in)
                    for s in slots:
                        pool.wait_ge(*V.at(k, s, "q1"))
                        nc.gpsimd.tensor_tensor(q2[s][:, :], q1[s][:, :], g["bin_r"][:, :], ALU.add).then_inc(O.sem, 1)
                    for s in slots:
                        pool.wait_ge(*A.at(k, s, "n"))
                        nc.gpsimd.tensor_tensor(d[s][:, :], E.Xd[s][:, :], n[s][:, :], ALU.subtract).then_inc(O.sem, 1)
                        nc.gpsimd.tensor_tensor(sm_[s][:, :], E.Xd[s][:, :], n[s][:, :], ALU.add).then_inc(O.sem, 1)
                    for s in slots:
                        E.rstd(pool, k, s)
                    for s in slots:
                        E.scatter(pool, k, s)

            @block.vector
            def _(dve):
                nc.vector.sem_inc(V.sem, V.lead)
                dve.wait_ge(started, 1)
                nc.vector.tensor_copy(rel_f[:, :], rel_i[:, :])
                nc.vector.memset(pA[(E.U - 1) % 2][:, :], 0.0).then_inc(started, 1)
                dve.wait_ge(started, 2)
                with dve.Fori(0, ROUNDS) as k:
                    for s in slots:
                        dve.wait_ge(*M.before(k, s, "ag"))
                        nc.vector.tensor_scalar(Xs[s][:, D:W], rel_f[:, :], g["type_f"][:, E.block_of(k, s)], None,
                                                ALU.is_equal).then_inc(V.sem, 1)
                        dve.wait_ge(E.cols_in[s], (k + 1) * 16)
                        nc.vector.tensor_scalar(E.eq[s][:, :], E.dc[s][:, :], g["dst_f"][:, E.block_of(k, s)], None,
                                                ALU.is_equal).then_inc(V.sem, 1)
                    for s in slots:
                        dve.wait_ge(E.src_in[s], (k + 1) * 16)
                        dve.wait_ge(*V.at(k, s, "oh"))
                        dve.wait_ge(*E.carry_from(k, s, M, "ag"))
                        nc.vector.tensor_copy(Xs[s][0:1, :], pA[((s - 1) % E.U) % 2][0:1, :]).then_inc(V.sem, 1)
                    for s in slots:
                        dve.wait_ge(*M.at(k, s, "ag"))
                        nc.vector.tensor_copy(As[s][:, :], pA[s % 2][:, :]).then_inc(V.sem, 1)
                    for s in slots:
                        dve.wait_ge(*A.at(k, s, "rz"))
                        nc.vector.scalar_tensor_tensor(q[s][:, :], rz[s][:, 0:D], 1.0, pN[s % 2][:, 1, :],
                                                       ALU.add, ALU.mult).then_inc(V.sem, 1)
                        dve.wait_ge(*V.at(k, s, "q"))
                        nc.vector.tensor_tensor(q1[s][:, :], q[s][:, :], pN[s % 2][:, 0, :], ALU.add).then_inc(V.sem, 1)
                    for s in slots:
                        dve.wait_ge(*O.at(k, s, "s"))
                        nc.vector.scalar_tensor_tensor(w[s][:, :], rz[s][:, D:2 * D], 1.0, d[s][:, :],
                                                       ALU.add, ALU.mult).then_inc(V.sem, 1)
                        dve.wait_ge(*V.at(k, s, "w"))
                        nc.vector.scalar_tensor_tensor(E.v[s][:, :], w[s][:, :], 0.5, sm_[s][:, :],
                                                       ALU.mult, ALU.add).then_inc(V.sem, 1)
                        dve.wait_ge(*V.at(k, s, "v"))
                        E.stats(dve, k, s)
                    for s in slots:
                        E.normalise(dve, k, s)

            @block.tensor
            def _(pe):
                nc.tensor.sem_inc(M.sem, M.lead)
                with pe.Fori(0, ROUNDS) as k:
                    for s in slots:
                        pe.wait_ge(*V.at(k, s, "cy"))
                        if s >= 2:
                            pe.wait_ge(*V.at(k, s - 2, "A"))
                        nc.tensor.matmul(pA[s % 2][:, :], E.eq[s][:, :], Xs[s][:, :], start=True, stop=True)\
                            .then_inc(M.sem, 1)
                    for s in slots:
                        pe.wait_ge(*V.at(k, s, "A"))
                        pe.wait_ge(*E.carry_from(k, s, A, "cT"))
                        nc.tensor.transpose(pC[:, :], As[s][:, D:W], g["ident"][:, :]).then_inc(M.sem, 1)
                    for s in slots:
                        pe.wait_ge(E.dst_in[s], (k + 1) * 16)
                        pe.wait_ge(*E.carry_from(k, s, A, "aT"))
                        for a, rows in enumerate((As, E.Xd)):
                            for j in range(KC):
                                last = nc.tensor.transpose(pT[:, a * KC + j, :], rows[s][:, j * P:(j + 1) * P],
                                                           g["ident"][:, :])
                        last.then_inc(M.sem, 1)
                    for s in slots:
                        pe.wait_ge(*A.at(k, s, "aT"))
                        if s >= 2:
                            pe.wait_ge(*V.at(k, s - 2, "q1"))
                        for o, lo, hi, bias, ins in ((pRZ[s % 2][:, :], 0, 2 * D, True, (0, 1)),
                                                     (pN[s % 2][:, 0, :], 2 * D, 3 * D, False, (0,)),
                                                     (pN[s % 2][:, 1, :], 2 * D, 3 * D, True, (1,))):
                            terms = [(g["ones_b"][:, :], g["bias3"][:, lo:hi])] if bias else []
                            if 0 in ins:
                                terms.append((cT[s][:, :], g["relw"][:, lo:hi]))
                            for a in ins:
                                wT = g["whhT"] if a else g["wihT"]
                                terms += [(aT[s][:, a * KC + j, :], wT[:, j, lo:hi]) for j in range(KC)]
                            for i, (l, r) in enumerate(terms):
                                last = nc.tensor.matmul(o, l, r, start=(i == 0), stop=(i == len(terms) - 1))
                        last.then_inc(M.sem, 1)

            @block.scalar
            def _(act):
                nc.scalar.sem_inc(A.sem, A.lead)
                with act.Fori(0, ROUNDS) as k:
                    for s in slots:
                        act.wait_ge(*M.at(k, s, "ct"))
                        nc.scalar.activation(cT[s][:, :], pC[:, :], ACT.Copy).then_inc(A.sem, 1)
                    for s in slots:
                        act.wait_ge(*M.at(k, s, "t"))
                        nc.scalar.activation(aT[s][:, :, :], pT[:, :, :], ACT.Copy).then_inc(A.sem, 1)
                    for s in slots:
                        act.wait_ge(*M.at(k, s, "gru"))
                        nc.scalar.activation(rz[s][:, :], pRZ[s % 2][:, :], ACT.Tanh, scale=0.5).then_inc(A.sem, 1)
                    for s in slots:
                        act.wait_ge(*O.at(k, s, "q2"))
                        nc.scalar.activation(n[s][:, :], q2[s][:, :], ACT.Tanh).then_inc(A.sem, 1)


NB_EDGES = [0]


def kernel(x, src, dst, edge_attr_64, edge_type_16, edge_weight, L0_gnn_node_lock, L0_gnn_W, L0_gnn_b, L1_gnn_W0,
           L1_gnn_att_src0, L1_gnn_att_dst0, L1_gnn_b0, L1_gnn_W1, L1_gnn_att_src1, L1_gnn_att_dst1, L1_gnn_b1,
           L2_gnn_W, L2_gnn_A, L3_gnn_relvectors, L3_gnn_w_ih, L3_gnn_w_hh, L3_gnn_b_ih, L3_gnn_b_hh):
    import numpy as np
    import concourse.bacc as bacc
    from concourse.bass_utils import run_bass_kernel_spmd

    N, E = x.shape[0], src.shape[0]
    NB_EDGES[0] = E
    NB = -(-E // SLOT_EDGES)
    NB += -NB % 3
    PAD = NB * SLOT_EDGES

    def flat(a, fill, ahead=0):
        a = np.asarray(a)
        f = np.full((PAD + 2,) + a.shape[1:], fill, a.dtype)
        f[1:E + 1] = a
        f[0] = -1 if a.dtype.kind == "i" else 0
        return f[1 + ahead:1 + ahead + PAD]

    def slots(a, fill, first):
        f = flat(a, fill) if not isinstance(a, tuple) else a[0]
        f = f.reshape((NB, SLOT_EDGES) + f.shape[1:])
        row0 = np.broadcast_to(first, (NB, 1) + f.shape[2:]).astype(f.dtype)
        return np.ascontiguousarray(np.moveaxis(np.concatenate([row0, f], axis=1), 0, 1))

    cur = flat(dst, N).reshape(NB, SLOT_EDGES)
    before = flat(dst, N, -1).reshape(NB, SLOT_EDGES)
    after = flat(dst, N, 1)
    prev_last = before[:, :1]
    pack = lambda w: np.ascontiguousarray(np.asarray(w).T)
    att = np.zeros((D, 2 * HEADS), np.float32)
    for j, a in enumerate((L1_gnn_att_src0, L1_gnn_att_dst0)):
        for h in range(HEADS):
            att[h * HID:(h + 1) * HID, j * HEADS + h] = np.asarray(a)[0, h]
    ins = {
        "x": np.asarray(x),
        "src": slots(src, 0, prev_last),
        "dst": slots(dst, N, prev_last),
        "dst_next": slots((after,), N, prev_last),
        "dst_cols": np.ascontiguousarray(np.concatenate([cur[:, -1:], cur], axis=1)),
        "dst_prev": np.ascontiguousarray(np.concatenate([cur[:, -1:], before], axis=1)),
        "attr": slots(edge_attr_64, 0, 0),
        "etype": slots(edge_type_16, 0, 0),
        "ew": slots(edge_weight, 0, 0),
        "node_lock": np.asarray(L0_gnn_node_lock).reshape(1, -1),
        "W0e_T": pack(L0_gnn_W), "b0e": np.asarray(L0_gnn_b).reshape(1, -1),
        "W1_T": pack(L1_gnn_W0), "W1n": np.asarray(L1_gnn_W0), "att1": att, "b1": np.asarray(L1_gnn_b0).reshape(1, -1),
        "W2_T": pack(L2_gnn_W), "W2n": np.asarray(L2_gnn_W), "A2": np.asarray(L2_gnn_A),
        "a2_T": np.ascontiguousarray(np.asarray(L2_gnn_A)[0, :2 * D].reshape(2, D).T),
        "rel_T": pack(L3_gnn_relvectors), "wih_T": pack(L3_gnn_w_ih), "whh_T": pack(L3_gnn_w_hh),
        "b_ih": np.asarray(L3_gnn_b_ih).reshape(1, -1), "b_hh": np.asarray(L3_gnn_b_hh).reshape(1, -1),
    }
    nc = bacc.Bacc("TRN2", target_bir_lowering=False, num_devices=1)
    args = [nc.dram_tensor(f"in_{n}", a.shape, mybir.dt.from_np(a.dtype), kind="ExternalInput").ap()
            for n, a in ins.items()]
    args.append(nc.dram_tensor("out", (N, D), F32, kind="ExternalOutput").ap())
    for n in ("X1", "X2", "X3"):
        args.append(nc.dram_tensor(n, (N, D), F32, kind="Internal").ap())
    args.append(nc.dram_tensor("MSG", (NB * P, D), F32, kind="Internal").ap())
    gnn(nc, *args)
    r = run_bass_kernel_spmd(nc, [{f"in_{n}": a for n, a in ins.items()}], core_ids=[0])
    return r.results[0]["out"]
```

```python
from contextlib import ExitStack

import concourse.bass as bass
from concourse import mybir
from concourse.alu_op_type import AluOpType as ALU

ACT = mybir.ActivationFunctionType
AX = mybir.AxisListType
F32 = mybir.dt.float32
BF16 = mybir.dt.bfloat16
I32 = mybir.dt.int32

P = 128
D = 256
KC = D // P
HEADS = 8
HID = D // HEADS
RELS = 16
EDIM = 64
SLOT_EDGES = P - 1
EPS = 1e-5
THR_A = 0.1
THR_W = 0.1
SLOPE = 0.2
FAR = 1 << 20
NONE = -1e30


class Item:

    def __init__(self, ring, count, round_, slot):
        self.ring, self.count, self.round, self.slot = ring, count, round_ + slot // ring, slot % ring
        self.number = self.round * ring + self.slot
        self.fixed = isinstance(self.round, int)

    def back(self, d):
        other = Item(self.ring, self.count, self.round, self.slot - d)
        return None if other.fixed and not 0 <= other.number < self.count else other

    def dma(self):
        return self.round * 16 + 16


class Turns:

    def __init__(self, ring, count, longest, even=None):
        self.ring, self.count, self.longest = ring, count, longest
        self.first = -(-(longest + ring) // ring)
        self.last = (even or count) // ring

    def run(self, eng, body):
        item = lambda r, s: Item(self.ring, self.count, r, s)
        for t in range(self.first * self.ring):
            body(item(0, t))
        with eng.Fori(self.first, self.last) as r:
            for s in range(self.ring):
                body(item(r, s))
        for t in range(self.last * self.ring, self.count + self.longest):
            body(item(0, t))


class Steps:

    def __init__(self, sem, plan):
        self.sem = sem
        steps = [x.split(":") for x in plan.split()]
        self.order = {n: i for i, (n, _) in enumerate(steps)}
        self.delay = {n: int(d) for n, d in steps}
        self.n, self.skipped = len(steps), sum(self.delay.values())

    def at(self, item, name):
        turn, pos = item.number + self.delay[name], self.order[name]
        if not item.fixed:
            return self.sem, item.round * (item.ring * self.n) + \
                ((item.slot + self.delay[name]) * self.n - self.skipped + pos + 1)
        return self.sem, sum(min(max(turn + (self.order[m] <= pos) - d, 0), item.count) for m, d in self.delay.items())


def bcast_rows(ap, rows, cols):
    return bass.AP(ap.tensor, ap.offset, [[0, rows], [1, cols]])


def gnn(nc, x, src, dst, dst_next, dst_cols, dst_prev, attr, etype, ew, node_lock, W0e_T, b0e, W1_T, W1n, att1, b1,
        W2_T, W2n, A2, a2_T, rel_T, wih_T, whh_T, b_ih, b_hh, out, X1, X2, X3, MSG):
    N = x.shape[0]
    NB = src.shape[1]
    NEDGE = NB_EDGES[0]
    L = node_lock.shape[1]
    PAIR = 2 * P
    PAIRS = N // PAIR
    REST = N - PAIRS * PAIR
    assert 0 < REST <= P
    es = ExitStack()
    with es:
        def sb(name, shape, dt=F32, ctx=es):
            return ctx.enter_context(nc.sbuf_tensor(name, shape, dt))

        def ps(name, shape, ctx, dt=F32):
            return ctx.enter_context(nc.psum_tensor(name, shape, dt))

        used = []

        def sm(name, ctx=es):
            used.append(ctx.enter_context(nc.semaphore(name)))
            return used[-1]

        ident = sb("ident", [P, P])
        ones_b = sb("ones_b", [P, P], BF16)
        eps_c = sb("eps_c", [P, 2])
        mhalf = sb("mhalf", [P, 2])
        src_f = sb("src_f", [P, NB])
        dst_f = sb("dst_f", [P, NB])
        type_f = sb("type_f", [P, NB])
        w_e = sb("w_e", [P, NB])
        src_i = sb("src_i", [P, NB], I32)
        dst_i = sb("dst_i", [P, NB], I32)
        put_i = sb("put_i", [P, NB], I32)
        efeat = sb("efeat", [P, NB])
        keep = sb("keep", [P, NB])
        Weff_T = sb("Weff_T", [P, KC, D])
        b0e_r = sb("b0e_r", [P, D])
        W1x = sb("W1x", [P, KC, D + 2 * HEADS])
        b1m1_r = sb("b1m1_r", [P, D])
        ones_next = sb("ones_next", [P, P], BF16)
        bias0 = sb("bias0", [P, D], BF16)
        bias1 = sb("bias1", [P, D], BF16)
        bias_in = sb("bias_in", [P, D], BF16)
        W2T = sb("W2T", [P, KC, D])
        us_r = sb("us_r", [P, D])
        ud_r = sb("ud_r", [P, D])
        whhT = sb("whhT", [P, KC, 3 * D])
        wihT = sb("wihT", [P, KC, 3 * D])
        relw = sb("relw", [RELS, 3 * D])
        bias3 = sb("bias3", [P, 3 * D], BF16)
        bin_r = sb("bin_r", [P, D])

        state = locals()
        for phase in (prepare, dense, edge_norms, edge_sum, edge_heads, edge_attention, edge_gru):
            phase(nc, state)
            with nc.Block() as block:
                @block.gpsimd
                def _(pool):
                    for s in used:
                        pool.sem_clear(s)
            used.clear()


def prepare(nc, g):
    (N, NB, L, sb, ps, sm) = (g[n] for n in ("N", "NB", "L", "sb", "ps", "sm"))
    x = g["x"]
    with ExitStack() as c:
        loaded = sm("loaded", c)
        dve_done = sm("dve_done", c)
        pe_done = sm("pe_done", c)
        act_done = sm("act_done", c)
        pool_done = sm("pool_done", c)
        attr_loaded = [sm(f"attr_loaded{s}", c) for s in range(2)]
        attr_used = sm("attr_used", c)
        x_loaded = [sm(f"x_loaded{s}", c) for s in range(2)]
        x_squared = sm("x_squared", c)
        sq_added = sm("sq_added", c)
        lead_done = sm("lead_done", c)
        W0r = sb("W0r", [P, KC, D], F32, c)
        W1n = sb("W1n", [P, KC, D], F32, c)
        W2n = sb("W2n", [P, KC, D], F32, c)
        att = sb("att", [P, KC, 2 * HEADS], F32, c)
        a2 = sb("a2", [P, KC, 2], F32, c)
        a2b = sb("a2b", [P, KC, 2, P], F32, c)
        ae_r = sb("ae_r", [P, EDIM], F32, c)
        relT = sb("relT", [P, KC, RELS], F32, c)
        nxt_f = sb("nxt_f", [P, NB], I32, c)
        type_i = sb("type_i", [P, NB], I32, c)
        bi_r = sb("bi_r", [P, 3 * D], F32, c)
        bh_r = sb("bh_r", [P, 3 * D], F32, c)
        bsum = sb("bsum", [P, 3 * D], F32, c)
        bsum2 = sb("bsum2", [P, 3 * D], F32, c)
        bh = sb("bh", [P, 3 * D], BF16, c)
        b0c, b1c, bic = (sb(n, [P, D], F32, c) for n in ("b0c", "b1c", "bic"))
        tmp = sb("tmp", [P, NB], F32, c)
        tmp2 = sb("tmp2", [P, NB], F32, c)
        src0 = sb("src0", [P, NB], I32, c)
        dst0 = sb("dst0", [P, NB], I32, c)
        AB = NB // 6 if NB % 6 == 0 else NB
        at_sb = [sb(f"at_sb{s}", [P, AB, EDIM], F32, c) for s in range(2)]
        NROW = N // P
        NG = next(n for n in (13, 11, 6, 5) if NROW % (2 * n) == 0)
        xg = [sb(f"xg{s}", [P, NG, D], F32, c) for s in range(2)]
        sq = [sb(f"sq{s}", [P, NG, D], F32, c) for s in range(2)]
        acc = sb("acc", [P, NG, D], F32, c)
        xtail = sb("xtail", [P, D], F32, c)
        onesf = sb("onesf", [P, P], F32, c)
        accr = sb("accr", [P, D], F32, c)
        nk = sb("nk", [P, KC], F32, c)
        nk2 = sb("nk2", [P, KC], F32, c)
        na = sb("na", [P, 1], F32, c)
        thr = sb("thr", [P, KC], F32, c)
        flag = sb("flag", [P, 1], F32, c)
        absw = sb("absw", [P, KC, D], F32, c)
        pv = ps("pv", [P, KC, 2 * HEADS], c)
        pu = ps("pu", [P, 2, D], c)
        pr = ps("pr", [RELS, 512], c)
        pr2 = ps("pr2", [RELS, D], c)
        pn = ps("pn", [P, KC + 1], c)
        TAIL = N - NROW * P
        STEPS = NROW // NG
        assert STEPS * NG == NROW and STEPS % 2 == 0
        block = c.enter_context(nc.Block())

        @block.sync
        def _(sp):
            kview = lambda a: a.rearrange("(c p) n -> p c n", p=P)
            loads = [
                (W0r[:, :, :], kview(g["W0e_T"])), (g["W1x"][:, :, 0:D], kview(g["W1_T"])),
                (W1n[:, :, :], kview(g["W1n"])), (W2n[:, :, :], kview(g["W2n"])),
                (g["W2T"][:, :, :], kview(g["W2_T"])), (att[:, :, :], kview(g["att1"])),
                (a2[:, :, :], kview(g["a2_T"])),
                (ae_r[:, :], bcast_rows(g["A2"][0:1, 2 * D:], P, EDIM)),
                (relT[:, :, :], kview(g["rel_T"])), (g["wihT"][:, :, :], kview(g["wih_T"])),
                (g["whhT"][:, :, :], kview(g["whh_T"])),
                (g["b0e_r"][:, :], bcast_rows(g["b0e"], P, D)), (g["b1m1_r"][:, :], bcast_rows(g["b1"], P, D)),
                (bi_r[:, :], bcast_rows(g["b_ih"], P, 3 * D)), (bh_r[:, :], bcast_rows(g["b_hh"], P, 3 * D)),
                (src0[:, :], g["src"]), (dst0[:, :], g["dst"]), (nxt_f[:, :], g["dst_next"]),
                (type_i[:, :], g["etype"]), (g["w_e"][:, :], g["ew"]),
                (xtail[0:TAIL, :], x[NROW * P:N, :]),
            ]
            for dst_ap, src_ap in loads:
                sp.dma_start(dst_ap, src_ap).then_inc(loaded, 16)
            g["N_LOADS"] = len(loads)
            for a in range(NB // AB):
                if a >= 2:
                    sp.wait_ge(attr_used, a - 1)
                sp.dma_start(at_sb[a % 2][:, :, :], g["attr"][:, a * AB:(a + 1) * AB, :]).then_inc(attr_loaded[a % 2], 16)

        NLOAD = 21

        @block.scalar
        def _(act):
            xv = x[0:NROW * P, :].rearrange("(i p g) d -> i p g d", p=P, g=NG)
            for s in range(2):
                act.dma_start(xg[s][:, :, :], xv[s]).then_inc(x_loaded[s], 16)
            for i in range(STEPS):
                s = i % 2
                act.wait_ge(x_loaded[s], 16 * (i // 2 + 1))
                if i >= 2:
                    act.wait_ge(sq_added, i - 1)
                nc.scalar.activation(sq[s][:, :, :], xg[s][:, :, :], ACT.Square).then_inc(x_squared, 1)
                if i + 2 < STEPS:
                    act.wait_ge(x_squared, i + 1)
                    act.dma_start(xg[s][:, :, :], xv[i + 2]).then_inc(x_loaded[s], 16)
            act.wait_ge(loaded, 16 * NLOAD)
            nc.scalar.activation(xtail[0:TAIL, :], xtail[0:TAIL, :], ACT.Square).then_inc(x_squared, 1)
            act.wait_ge(pe_done, 2)
            nc.scalar.activation(nk[:, :], pn[:, 0:KC], ACT.Sqrt).then_inc(act_done, 1)
            act.wait_ge(pe_done, 3)
            nc.scalar.activation(na[:, :], pn[:, KC:KC + 1], ACT.Sqrt).then_inc(act_done, 1)

        @block.gpsimd
        def _(pool):
            nc.gpsimd.memset(g["ident"][:, :], 0.0).then_inc(pool_done, 1)
            pool.wait_ge(pool_done, 1)
            nc.gpsimd.affine_select(out=g["ident"][:, :], in_=g["ident"][:, :], compare_op=ALU.not_equal, fill=1.0,
                                    base=0, pattern=[[-1, P]], channel_multiplier=1).then_inc(pool_done, 1)
            nc.gpsimd.memset(g["ones_b"][:, :], 1.0)
            nc.gpsimd.memset(onesf[:, :], 1.0)
            nc.gpsimd.memset(g["eps_c"][:, :], EPS)
            nc.gpsimd.memset(g["mhalf"][:, :], -0.5)
            nc.gpsimd.memset(g["ones_next"][:, 0:1], 0.0)
            nc.gpsimd.memset(g["ones_next"][:, 1:P], 1.0)
            for b in ("bias0", "bias1", "bias_in"):
                nc.gpsimd.memset(g[b][:, :], 0.0)
            nc.gpsimd.memset(g["bias3"][:, :], 0.0).then_inc(pool_done, 1)

        @block.vector
        def _(dve):
            count = [0]

            def done(ins):
                count[0] += 1
                ins.then_inc(dve_done, 1)
                dve.wait_ge(dve_done, count[0])

            done(nc.vector.memset(acc[:, :, :], 0.0))
            for i in range(STEPS):
                dve.wait_ge(x_squared, i + 1)
                nc.vector.tensor_tensor(acc[:, :, :], acc[:, :, :], sq[i % 2][:, :, :], ALU.add).then_inc(sq_added, 1)
                dve.wait_ge(sq_added, i + 1)
            dve.wait_ge(loaded, 16 * NLOAD)
            done(nc.vector.tensor_reduce(accr[:, :], acc[:, :, :].rearrange("p g d -> p d g"), AX.X, ALU.add))
            dve.wait_ge(x_squared, STEPS + 1)
            done(nc.vector.tensor_tensor(accr[0:TAIL, :], accr[0:TAIL, :], xtail[0:TAIL, :], ALU.add))
            count_sq = count[0]
            g["count_sq"] = count_sq
            done(nc.vector.tensor_copy(g["src_f"][:, :], src0[:, :]))
            done(nc.vector.tensor_copy(g["dst_f"][:, :], dst0[:, :]))
            nc.vector.tensor_scalar(g["src_i"][:, :], g["src_f"][:, :], 0.0, float(N - 1), ALU.max, ALU.min)
            nc.vector.tensor_scalar(g["dst_i"][:, :], g["dst_f"][:, :], 0.0, float(N - 1), ALU.max, ALU.min)
            nc.vector.tensor_copy(g["type_f"][:, :], type_i[:, :])
            done(nc.vector.tensor_tensor(tmp[:, :], g["dst_f"][:, :], nxt_f[:, :], ALU.is_equal))
            done(nc.vector.scalar_tensor_tensor(tmp2[:, :], tmp[:, :], float(FAR), g["dst_f"][:, :], ALU.mult, ALU.add))
            done(nc.vector.tensor_copy(g["put_i"][:, :], tmp2[:, :]))
            for a in range(NB // AB):
                t = at_sb[a % 2]
                dve.wait_ge(attr_loaded[a % 2], 16 * (a // 2 + 1))
                done(nc.vector.tensor_tensor(t[:, :, :], t[:, :, :],
                                             ae_r[:, :].unsqueeze(1).to_broadcast([P, AB, EDIM]), ALU.mult))
                nc.vector.tensor_reduce(g["efeat"][:, a * AB:(a + 1) * AB], t[:, :, :], AX.X, ALU.add)\
                    .then_inc(attr_used, 1)
            done(nc.vector.tensor_scalar(g["b1m1_r"][:, :], g["b1m1_r"][:, :], -1.0, None, ALU.add))
            nc.vector.tensor_copy(g["bin_r"][:, :], bi_r[:, 2 * D:3 * D])
            nc.vector.tensor_copy(bic[:, :], bi_r[:, 2 * D:3 * D])
            nc.vector.tensor_copy(b0c[:, :], g["b0e_r"][:, :])
            nc.vector.tensor_copy(b1c[:, :], g["b1m1_r"][:, :])
            nc.vector.tensor_scalar(bsum[:, 2 * D:3 * D], bh_r[:, 2 * D:3 * D], 0.5, None, ALU.mult)
            nc.vector.tensor_scalar(g["whhT"][:, :, 2 * D:3 * D], g["whhT"][:, :, 2 * D:3 * D], 0.5, None, ALU.mult)
            done(nc.vector.tensor_tensor(bsum[:, 0:2 * D], bi_r[:, 0:2 * D], bh_r[:, 0:2 * D], ALU.add))
            dve.wait_ge(pool_done, 3)
            for row, into, n in ((bsum, "bias3", 3 * D), (b0c, "bias0", D), (b1c, "bias1", D), (bic, "bias_in", D)):
                a, b = row, bsum2
                for part in range(3):
                    done(nc.vector.tensor_copy(bh[:, 0:n], a[:, 0:n]))
                    nc.vector.tensor_copy(g[into][32 * part:32 * part + 1, :], bh[32 * part:32 * part + 1, 0:n])
                    done(nc.vector.tensor_tensor(b[:, 0:n], a[:, 0:n], bh[:, 0:n], ALU.subtract))
                    a, b = b, a
            for j in range(2):
                done(nc.vector.tensor_copy(a2b[:, :, j, :], a2[:, :, j:j + 1].to_broadcast([P, KC, P])))
            g["count_a2b"] = count[0]
            dve.wait_ge(pe_done, 1)
            nc.vector.tensor_copy(g["W1x"][:, :, D:D + 2 * HEADS], pv[:, :, :])
            nc.vector.tensor_copy(g["us_r"][:, :], pu[:, 0, :])
            nc.vector.tensor_copy(g["ud_r"][:, :], pu[:, 1, :])
            nc.vector.tensor_copy(g["relw"][:, 0:512], pr[:, :])
            done(nc.vector.tensor_copy(g["relw"][:, 512:3 * D], pr2[:, :]))
            dve.wait_ge(act_done, 1)
            done(nc.vector.tensor_copy(nk2[:, :], pn[:, 0:KC]))
            done(nc.vector.tensor_tensor(nk2[:, 0:1], nk2[:, 0:1], nk2[:, 1:2], ALU.add))
            g["count_nk"] = count[0]
            dve.wait_ge(act_done, 2)
            done(nc.vector.reciprocal(thr[:, :], nk[:, :]))
            done(nc.vector.tensor_scalar(na[:, :], na[:, :], 1.0 / D, None, ALU.mult))
            done(nc.vector.tensor_scalar(flag[:, :], na[:, :], 1e-8, None, ALU.is_gt))
            done(nc.vector.tensor_scalar(na[:, :], na[:, :], THR_W, None, ALU.mult))
            done(nc.vector.tensor_scalar(thr[:, :], thr[:, :], na[:, :], None, ALU.mult))
            done(nc.vector.scalar_tensor_tensor(absw[:, :, :], W0r[:, :, :], -1.0, W0r[:, :, :], ALU.mult, ALU.max))
            for k in range(KC):
                done(nc.vector.tensor_scalar(absw[:, k, :], absw[:, k, :], thr[:, k:k + 1], flag[:, :],
                                             ALU.is_lt, ALU.mult))
            done(nc.vector.tensor_tensor(absw[:, :, :], absw[:, :, :], W0r[:, :, :], ALU.mult))
            done(nc.vector.tensor_tensor(g["Weff_T"][:, :, :], W0r[:, :, :], absw[:, :, :], ALU.subtract))

        @block.tensor
        def _(pe):
            pe.wait_ge(loaded, 16 * NLOAD)
            for k in range(KC):
                for o in range(KC):
                    nc.tensor.matmul(pv[:, k, :], W1n[:, o, k * P:(k + 1) * P], att[:, o, :],
                                     start=(o == 0), stop=(o == KC - 1))
            pe.wait_ge(dve_done, g["count_a2b"])
            for j in range(2):
                for o in range(KC):
                    nc.tensor.matmul(pu[:, j, :], a2b[:, o, j, :], W2n[:, o, :], start=(o == 0), stop=(o == KC - 1))
            for o in range(KC):
                nc.tensor.matmul(pr[:, :], relT[:, o, :], g["wihT"][:, o, 0:512], start=(o == 0), stop=(o == KC - 1))
            for o in range(KC):
                last = nc.tensor.matmul(pr2[:, :], relT[:, o, :], g["wihT"][:, o, 512:3 * D],
                                        start=(o == 0), stop=(o == KC - 1))
            last.then_inc(pe_done, 1)
            pe.wait_ge(pool_done, 3)
            pe.wait_ge(dve_done, g["count_sq"])
            for k in range(KC):
                last = nc.tensor.matmul(pn[:, k:k + 1], accr[:, k * P:(k + 1) * P], onesf[:, 0:1], start=True, stop=True)
            last.then_inc(pe_done, 1)
            pe.wait_ge(dve_done, g["count_nk"])
            nc.tensor.matmul(pn[:, KC:KC + 1], onesf[:, :], nk2[:, 0:1], start=True, stop=True).then_inc(pe_done, 1)


def dense(nc, g):
    sb, ps, sm, N, PAIRS, REST, x = (g[n] for n in ("sb", "ps", "sm", "N", "PAIRS", "REST", "x"))
    PAIR = 2 * P
    RING = 4
    with ExitStack() as c:
        turns = Turns(RING, PAIRS + 1, 6, even=PAIRS)
        slots = range(RING)
        load_sem = [sm(f"nodes_loaded{s}", c) for s in slots]
        stored = {n: [sm(f"{n}_stored{s}", c) for s in slots] for n in ("x1", "x2", "x3", "x4")}
        V = Steps(sm("dense_vec", c), "x3:4 q:5 st0:2 ag0:2 u:3 v1:3 st1:3 ag1:3 x1:2 w:5 v3:5 st3:5 ag3:5 "
                                      "x2:3 st2:3 ag2:3 x4:5")
        O = Steps(sm("dense_pool", c), "v0:2 q2:5 e0:2 r0:2 d:5 s:5 e1:3 r1:3 e3:5 r3:5 e2:3 r2:3")
        A = Steps(sm("dense_act", c), "ex:3 x3T:4 n:5 rz0:4 rz1:4 x1T:2")
        M = Steps(sm("dense_mat", c), "t3:4 gru0:4 gru1:4 t1:2 h:2")
        t = {n: [sb(f"d_{n}{s}", [P, 2, D], F32, c) for s in slots]
             for n in ("x", "v", "x1", "x1T", "ex", "u", "x2", "x3", "x3T", "q", "q2", "n", "d", "s", "w", "x4")}
        rz = [sb(f"d_rz{s}", [P, 2, 2 * D], F32, c) for s in range(2)]
        st = [sb(f"d_st{s}", [P, 4, 2, 6], F32, c) for s in slots]
        mv = [sb(f"d_mv{s}", [P, 4, 2, 2], F32, c) for s in slots]
        ve = [sb(f"d_ve{s}", [P, 4, 2], F32, c) for s in slots]
        rs = [sb(f"d_rs{s}", [P, 4, 2], F32, c) for s in slots]
        pT1 = ps("d_pT1", [P, 2 * D], c)
        pT3 = ps("d_pT3", [P, 2 * D], c)
        pH = [ps(f"d_pH{i}", [P, 2, D], c) for i in range(2)]
        pRZ = [ps(f"d_pRZ{i}", [P, 2 * D], c) for i in range(2)]
        pN = [ps(f"d_pN{i}", [P, 2, D], c) for i in range(2)]

        def size(i):
            return (REST, 1) if i.fixed and i.number == PAIRS else (P, 2)

        def part(name, i):
            R, G = size(i)
            return t[name][i.slot][0:R, 0:G, :]

        def rows_of(a, i):
            if size(i)[1] == 1:
                return a[PAIRS * PAIR:N, :].rearrange("(p g) d -> p g d", g=1)
            return a[bass.ds(i.number * PAIR, PAIR), :].rearrange("(p g) d -> p g d", g=2)

        block = c.enter_context(nc.Block())

        @block.sync
        def _(sp):
            def turn(now):
                if i := now.back(0):
                    if old := i.back(RING):
                        sp.wait_ge(*O.at(old, "v0"))
                    sp.dma_start(part("x", i), rows_of(x, i)).then_inc(load_sem[i.slot], 16)
                for n, d, a in (("x3", 4, g["X3"]), ("x1", 2, g["X1"]), ("x2", 3, g["X2"]), ("x4", 5, g["out"])):
                    if i := now.back(d):
                        sp.wait_ge(*V.at(i, n))
                        sp.dma_start(rows_of(a, i), part(n, i)).then_inc(stored[n][i.slot], 16)
            turns.run(sp, turn)
            for n in stored:
                for s in slots:
                    sp.wait_ge(stored[n][s], 16 * len(range(s, PAIRS + 1, RING)))

        @block.vector
        def _(dve):
            def stats(i, l, frm):
                R, G = size(i)
                for j in range(G):
                    last = nc.vector.bn_stats(st[i.slot][0:R, l, j, :], t[frm][i.slot][0:R, j, :])
                last.then_inc(V.sem, 1)
                dve.wait_ge(*V.at(i, f"st{l}"))
                nc.vector.nop(nofuse=True)
                for j in range(G):
                    last = nc.vector.bn_aggr(mv[i.slot][0:R, l, j, :], st[i.slot][0:R, l, j, :])
                last.then_inc(V.sem, 1)

            def norm(i, l, into, frm):
                R, G = size(i)
                if old := i.back(RING):
                    dve.wait_ge(stored[into][i.slot], old.dma())
                dve.wait_ge(*O.at(i, f"r{l}"))
                for j in range(G):
                    last = nc.vector.tensor_scalar(t[into][i.slot][0:R, j, :], t[frm][i.slot][0:R, j, :],
                                                   mv[i.slot][0:R, l, j, 0:1], rs[i.slot][0:R, l, j:j + 1],
                                                   ALU.subtract, ALU.mult)
                last.then_inc(V.sem, 1)

            def turn(now):
                if i := now.back(4):
                    norm(i, 2, "x3", "x2")
                if i := now.back(5):
                    R, G = size(i)
                    dve.wait_ge(*A.at(i, "rz1"))
                    nc.vector.scalar_tensor_tensor(part("q", i), rz[i.slot % 2][0:R, 0:G, 0:D], 1.0,
                                                   pN[i.slot % 2][0:R, 0:G, :], ALU.add, ALU.mult).then_inc(V.sem, 1)
                if i := now.back(2):
                    dve.wait_ge(*O.at(i, "v0"))
                    stats(i, 0, "v")
                if i := now.back(3):
                    R, G = size(i)
                    dve.wait_ge(*A.at(i, "ex"))
                    nc.vector.scalar_tensor_tensor(part("u", i), pH[i.slot % 2][0:R, 0:G, :], -1.0, part("x1", i),
                                                   ALU.max, ALU.add).then_inc(V.sem, 1)
                    dve.wait_ge(*V.at(i, "u"))
                    nc.vector.scalar_tensor_tensor(part("v", i), part("ex", i), 1.0, part("u", i),
                                                   ALU.min, ALU.add).then_inc(V.sem, 1)
                    dve.wait_ge(*V.at(i, "v1"))
                    stats(i, 1, "v")
                if i := now.back(2):
                    norm(i, 0, "x1", "v")
                if i := now.back(5):
                    R, G = size(i)
                    dve.wait_ge(*O.at(i, "s"))
                    nc.vector.scalar_tensor_tensor(part("w", i), rz[i.slot % 2][0:R, 0:G, D:2 * D], 1.0, part("d", i),
                                                   ALU.add, ALU.mult).then_inc(V.sem, 1)
                    dve.wait_ge(*V.at(i, "w"))
                    nc.vector.scalar_tensor_tensor(part("v", i), part("w", i), 0.5, part("s", i),
                                                   ALU.mult, ALU.add).then_inc(V.sem, 1)
                    dve.wait_ge(*V.at(i, "v3"))
                    stats(i, 3, "v")
                if i := now.back(3):
                    norm(i, 1, "x2", "v")
                    dve.wait_ge(*V.at(i, "x2"))
                    stats(i, 2, "x2")
                if i := now.back(5):
                    norm(i, 3, "x4", "v")
            turns.run(dve, turn)

        @block.gpsimd
        def _(pool):
            def rstd(i, l):
                R, G = size(i)
                pool.wait_ge(*V.at(i, f"ag{l}"))
                nc.gpsimd.tensor_tensor(ve[i.slot][0:R, l, 0:G], mv[i.slot][0:R, l, 0:G, 1], g["eps_c"][0:R, 0:G],
                                        ALU.add).then_inc(O.sem, 1)
                pool.wait_ge(*O.at(i, f"e{l}"))
                nc.gpsimd.tensor_tensor(rs[i.slot][0:R, l, 0:G], ve[i.slot][0:R, l, 0:G], g["mhalf"][0:R, 0:G],
                                        ALU.pow).then_inc(O.sem, 1)

            def row(name, i):
                R, G = size(i)
                return g[name][0:R, :].unsqueeze(1).to_broadcast([R, G, D])

            def turn(now):
                if i := now.back(2):
                    pool.wait_ge(load_sem[i.slot], i.dma())
                    if old := i.back(RING):
                        pool.wait_ge(*V.at(old, "x4"))
                    nc.gpsimd.tensor_tensor(part("v", i), part("x", i), row("b0e_r", i), ALU.add).then_inc(O.sem, 1)
                if i := now.back(5):
                    pool.wait_ge(*V.at(i, "q"))
                    nc.gpsimd.tensor_tensor(part("q2", i), part("q", i), row("bin_r", i), ALU.add).then_inc(O.sem, 1)
                if i := now.back(2):
                    rstd(i, 0)
                if i := now.back(5):
                    pool.wait_ge(*A.at(i, "n"))
                    nc.gpsimd.tensor_tensor(part("d", i), part("x3", i), part("n", i), ALU.subtract).then_inc(O.sem, 1)
                    nc.gpsimd.tensor_tensor(part("s", i), part("x3", i), part("n", i), ALU.add).then_inc(O.sem, 1)
                if i := now.back(3):
                    rstd(i, 1)
                if i := now.back(5):
                    rstd(i, 3)
                if i := now.back(3):
                    rstd(i, 2)
            turns.run(pool, turn)

        @block.scalar
        def _(act):
            def copy_T(i, into, bank, step):
                R, G = size(i)
                W = G * KC * R
                act.wait_ge(*M.at(i, step))
                nc.scalar.activation(t[into][i.slot][:, :, :].rearrange("p a b -> p (a b)")[:, 0:W], bank[:, 0:W],
                                     ACT.Copy).then_inc(A.sem, 1)

            def turn(now):
                if i := now.back(3):
                    R, G = size(i)
                    act.wait_ge(*M.at(i, "h"))
                    nc.scalar.activation(part("ex", i), pH[i.slot % 2][0:R, 0:G, :], ACT.Exp, bias=1.0)\
                        .then_inc(A.sem, 1)
                if i := now.back(4):
                    copy_T(i, "x3T", pT3, "t3")
                if i := now.back(5):
                    act.wait_ge(*O.at(i, "q2"))
                    nc.scalar.activation(part("n", i), part("q2", i), ACT.Tanh).then_inc(A.sem, 1)
                if i := now.back(4):
                    R, G = size(i)
                    if old := i.back(2):
                        act.wait_ge(*V.at(old, "w"))
                    for j in range(2):
                        act.wait_ge(*M.at(i, f"gru{j}"))
                        o = rz[i.slot % 2][0:R, j, :] if j < G else rz[i.slot % 2][0:R, j, 0:1]
                        nc.scalar.activation(o, pRZ[min(j, G - 1)][0:R, 0:o.shape[-1]], ACT.Tanh, scale=0.5)\
                            .then_inc(A.sem, 1)
                if i := now.back(2):
                    copy_T(i, "x1T", pT1, "t1")
            turns.run(act, turn)

        @block.tensor
        def _(pe):
            def flip(i, frm, bank):
                R, G = size(i)
                for j in range(G):
                    for k in range(KC):
                        o = (j * KC + k) * R
                        last = nc.tensor.transpose(bank[:, o:o + R], t[frm][i.slot][0:R, j, k * P:(k + 1) * P],
                                                   g["ident"][0:R, 0:R])
                last.then_inc(M.sem, 1)

            def lhs(name, i, j, k):
                R, G = size(i)
                o = (j * KC + k) * R
                return t[name][i.slot][:, :, :].rearrange("p a b -> p (a b)")[:, o:o + R]

            def turn(now):
                if i := now.back(4):
                    pe.wait_ge(*V.at(i, "x3"))
                    if old := i.back(1):
                        pe.wait_ge(*A.at(old, "x3T"))
                    flip(i, "x3", pT3)
                    R, G = size(i)
                    pe.wait_ge(*A.at(i, "x3T"))
                    if old := i.back(2):
                        pe.wait_ge(*V.at(old, "q"))
                    for j in range(2):
                        if j < G:
                            if old := i.back(1):
                                pe.wait_ge(*A.at(old, f"rz{j}"))
                            terms = [(g["ones_b"][:, 0:R], g["bias3"][:, :])]
                            terms += [(lhs("x3T", i, j, k), g["whhT"][:, k, :]) for k in range(KC)]
                            for o, lo, hi in ((pRZ[j][0:R, :], 0, 2 * D), (pN[i.slot % 2][0:R, j, :], 2 * D, 3 * D)):
                                for n, (l, r) in enumerate(terms):
                                    last = nc.tensor.matmul(o, l, r[:, lo:hi], start=(n == 0), stop=(n == KC))
                        else:
                            last = nc.tensor.matmul(pN[i.slot % 2][0:R, j, 0:1], g["ones_b"][:, 0:R],
                                                    g["bias3"][:, 0:1], start=True, stop=True)
                        last.then_inc(M.sem, 1)
                if i := now.back(2):
                    pe.wait_ge(*V.at(i, "x1"))
                    if old := i.back(1):
                        pe.wait_ge(*A.at(old, "x1T"))
                    flip(i, "x1", pT1)
                    R, G = size(i)
                    pe.wait_ge(*A.at(i, "x1T"))
                    if old := i.back(2):
                        pe.wait_ge(*V.at(old, "u"))
                    for j in range(G):
                        nc.tensor.matmul(pH[i.slot % 2][0:R, j, :], g["ones_b"][:, 0:R], g["bias1"][:, :],
                                         start=True, stop=False)
                        for k in range(KC):
                            last = nc.tensor.matmul(pH[i.slot % 2][0:R, j, :], lhs("x1T", i, j, k),
                                                    g["W1x"][:, k, 0:D], start=False, stop=(k == KC - 1))
                    last.then_inc(M.sem, 1)
            turns.run(pe, turn)


def edge_norms(nc, g):
    sb, ps, sm, NB, L, x = (g[n] for n in ("sb", "ps", "sm", "NB", "L", "x"))
    RING = 8
    with ExitStack() as c:
        slots = range(RING)
        turns = Turns(RING, NB, 6)
        O = Steps(sm("norms_pool", c), "ix:0")
        M = Steps(sm("norms_mat", c), "h:4 t:3")
        A = Steps(sm("norms_act", c), "msg:5 T:3 sq:5")
        V = Steps(sm("norms_vec", c), "lk:0")
        gathered = [sm(f"n_gathered{s}", c) for s in slots]
        stored = [sm(f"n_stored{s}", c) for s in slots]
        lock_loaded = sm("lock_loaded", c)
        ready = sm("n_ready", c)
        lock_i = sb("lock_i", [P, L], I32, c)
        lock_f = sb("lock_f", [P, L], F32, c)
        hit = [sb(f"hit{s}", [P, L], F32, c) for s in range(2)]
        lockc = sb("lockc", [P, NB], F32, c)
        n2 = sb("n2", [P, NB], F32, c)
        tiles = lambda n, shape, dt=F32: [sb(f"n_{n}{s}", shape, dt, c) for s in slots]
        ix, Xs, XT, msg, msq = tiles("ix", [P, 1], I32), tiles("Xs", [P, D]), tiles("XT", [P, KC, P]), \
            tiles("msg", [P, D]), tiles("msq", [P, D])
        pT = [ps(f"n_pT{i}", [P, KC, P], c) for i in range(2)]
        pH = [ps(f"n_pH{i}", [P, D], c) for i in range(2)]
        with nc.Block() as block:
            @block.gpsimd
            def _(pool):
                def turn(now):
                    if i := now.back(0):
                        if old := i.back(RING):
                            pool.wait_ge(*M.at(old, "t"))
                        nc.gpsimd.tensor_copy(ix[i.slot][:, :], g["src_i"][:, bass.ds(i.number, 1)]).then_inc(O.sem, 1)
                        pool.wait_ge(*O.at(i, "ix"))
                        nc.gpsimd.nop(nofuse=True)
                        nc.gpsimd.indirect_dma_start(
                            out=Xs[i.slot][:, :], out_offset=None, in_=x[:, :],
                            in_offset=bass.IndirectOffsetOnAxis(ap=ix[i.slot][:, 0:1], axis=0))\
                            .then_inc(gathered[i.slot], 16)
                turns.run(pool, turn)

            @block.tensor
            def _(pe):
                def turn(now):
                    if i := now.back(4):
                        pe.wait_ge(*A.at(i, "T"))
                        if old := i.back(2):
                            pe.wait_ge(*A.at(old, "msg"))
                        for j in range(KC):
                            last = nc.tensor.matmul(pH[i.slot % 2][:, :], XT[i.slot][:, j, :], g["Weff_T"][:, j, :],
                                                    start=(j == 0), stop=(j == KC - 1))
                        last.then_inc(M.sem, 1)
                    if i := now.back(3):
                        pe.wait_ge(gathered[i.slot], i.dma())
                        if old := i.back(2):
                            pe.wait_ge(*A.at(old, "T"))
                        for j in range(KC):
                            last = nc.tensor.transpose(pT[i.slot % 2][:, j, :], Xs[i.slot][:, j * P:(j + 1) * P],
                                                       g["ident"][:, :])
                        last.then_inc(M.sem, 1)
                turns.run(pe, turn)

            @block.scalar
            def _(act):
                def turn(now):
                    if i := now.back(5):
                        act.wait_ge(*M.at(i, "h"))
                        if old := i.back(RING):
                            act.wait_ge(stored[i.slot], old.dma())
                        nc.scalar.activation(msg[i.slot][:, :], pH[i.slot % 2][:, :], ACT.Copy,
                                             scale=g["w_e"][:, bass.ds(i.number, 1)]).then_inc(A.sem, 1)
                    if i := now.back(3):
                        act.wait_ge(*M.at(i, "t"))
                        nc.scalar.activation(XT[i.slot][:, :, :], pT[i.slot % 2][:, :, :], ACT.Copy).then_inc(A.sem, 1)
                    if i := now.back(5):
                        act.wait_ge(*A.at(i, "msg"))
                        nc.scalar.activation(msq[i.slot][:, :], msg[i.slot][:, :], ACT.Square,
                                             accum_out=n2[:, bass.ds(i.number, 1)]).then_inc(A.sem, 1)
                turns.run(act, turn)

            @block.sync
            def _(sp):
                sp.dma_start(lock_i[:, :], bcast_rows(g["node_lock"], P, L)).then_inc(lock_loaded, 16)

                def turn(now):
                    if i := now.back(5):
                        sp.wait_ge(*A.at(i, "msg"))
                        sp.dma_start(g["MSG"][bass.ds(i.number * P, P), :], msg[i.slot][:, :])\
                            .then_inc(stored[i.slot], 16)
                turns.run(sp, turn)
                for s in slots:
                    sp.wait_ge(stored[s], 16 * len(range(s, NB, RING)))

            @block.vector
            def _(dve):
                dve.wait_ge(lock_loaded, 16)
                nc.vector.tensor_copy(lock_f[:, :], lock_i[:, :]).then_inc(ready, 1)
                dve.wait_ge(ready, 1)

                def turn(now):
                    if i := now.back(0):
                        if old := i.back(2):
                            dve.wait_ge(*V.at(old, "lk"))
                        nc.vector.tensor_scalar(hit[i.slot % 2][:, :], lock_f[:, :], g["dst_f"][:, bass.ds(i.number, 1)],
                                                0.0, ALU.is_equal, ALU.add, accum_out=lockc[:, bass.ds(i.number, 1)])\
                            .then_inc(V.sem, 1)
                turns.run(dve, turn)

        tot = sb("n_tot", [P, 1], F32, c)
        thr = sb("n_thr", [P, 1], F32, c)
        norm = sb("n_norm", [P, NB], F32, c)
        m0 = sb("n_m0", [P, NB], F32, c)
        m1 = sb("n_m1", [P, NB], F32, c)
        lk = sb("n_lk", [P, NB], F32, c)
        eq = sb("n_eq", [P, NB], F32, c)
        onesf = sb("n_ones", [P, P], F32, c)
        pX = ps("n_pX", [P, 1], c)
        sqrt_done, dve_done, total_done = sm("sqrt_done", c), sm("keep_dve", c), sm("total_done", c)
        with nc.Block() as block:
            @block.scalar
            def _(act):
                nc.scalar.activation(norm[:, :], n2[:, :], ACT.Sqrt).then_inc(sqrt_done, 1)

            @block.tensor
            def _(pe):
                pe.wait_ge(dve_done, 2)
                nc.tensor.matmul(pX[:, :], onesf[:, :], tot[:, :], start=True, stop=True).then_inc(total_done, 1)

            @block.vector
            def _(dve):
                count = [0]

                def done(ins):
                    count[0] += 1
                    ins.then_inc(dve_done, 1)
                    dve.wait_ge(dve_done, count[0])

                done(nc.vector.memset(onesf[:, :], 1.0))
                dve.wait_ge(sqrt_done, 1)
                done(nc.vector.tensor_reduce(tot[:, :], norm[:, :], AX.X, ALU.add))
                dve.wait_ge(total_done, 1)
                done(nc.vector.tensor_scalar(thr[:, :], pX[:, :], 1.0 / g["NEDGE"], THR_A, ALU.mult, ALU.mult))
                nc.vector.tensor_tensor(eq[:, :], g["src_f"][:, :], g["dst_f"][:, :], ALU.is_equal)
                nc.vector.tensor_scalar(lk[:, :], lockc[:, :], 0.5, None, ALU.is_gt)
                done(nc.vector.tensor_scalar(m0[:, :], norm[:, :], thr[:, :], None, ALU.is_lt))
                done(nc.vector.tensor_scalar(m1[:, :], m0[:, :], -1.0, 1.0, ALU.mult, ALU.add))
                done(nc.vector.tensor_tensor(lk[:, :], lk[:, :], eq[:, :], ALU.max))
                done(nc.vector.tensor_tensor(g["keep"][:, :], m1[:, :], lk[:, :], ALU.max))


class EdgePass:

    RING = 6

    def __init__(self, nc, g, c, name, longest, vec, pool, mat, act, table, into):
        self.nc, self.g, self.c, self.name, self.table, self.into = nc, g, c, name, table, into
        self.NB, self.N = g["NB"], g["N"]
        self.turns = Turns(self.RING, self.NB, longest)
        self.slots = range(self.RING)
        self.V, self.O, self.M, self.A = (Steps(g["sm"](f"{name}_{e}", c), plan)
                                          for e, plan in (("vec", vec), ("pool", pool), ("mat", mat), ("act", act)))
        self.Xd = self.tiles("Xd", [P, D])
        self.v = self.tiles("v", [P, D])
        self.xn = self.tiles("xn", [P, D])
        self.st = self.tiles("st", [P, 6])
        self.mv = self.tiles("mv", [P, 2])
        self.ve = self.tiles("ve", [P, 1])
        self.rs = self.tiles("rs", [P, 1])
        self.dc = self.tiles("dc", [P, P], I32)
        self.eq = self.tiles("eq", [P, P])
        self.ixs = self.tiles("ixs", [P, 1], I32)
        self.ixd = self.tiles("ixd", [P, 1], I32)
        self.ixp = self.tiles("ixp", [P, 1], I32)
        self.src_in, self.dst_in, self.cols_in, self.put_out = (
            [g["sm"](f"{name}_{n}{s}", c) for s in self.slots] for n in ("src_in", "dst_in", "cols_in", "put_out"))

    def tiles(self, n, shape, dt=F32, count=None):
        return [self.g["sb"](f"{self.name}_{n}{s}", shape, dt, self.c) for s in range(count or self.RING)]

    def banks(self, n, shape, count):
        return [self.g["ps"](f"{self.name}_{n}{i}", shape, self.c) for i in range(count)]

    def gather(self, pool, i, ix, index, into, sem):
        nc, O = self.nc, self.O
        nc.gpsimd.tensor_copy(ix[i.slot][:, :], self.g[index][:, bass.ds(i.number, 1)]).then_inc(O.sem, 1)
        pool.wait_ge(*O.at(i, index))
        nc.gpsimd.nop(nofuse=True)
        nc.gpsimd.indirect_dma_start(out=into, out_offset=None, in_=self.table[:, :],
                                     in_offset=bass.IndirectOffsetOnAxis(ap=ix[i.slot][:, 0:1], axis=0))\
            .then_inc(sem[i.slot], 16)

    def gather_dst(self, pool, i):
        if old := i.back(self.RING):
            pool.wait_ge(*self.V.at(old, "v"))
        self.gather(pool, i, self.ixd, "dst_i", self.Xd[i.slot][:, :], self.dst_in)

    def scatter(self, pool, i):
        nc, O = self.nc, self.O
        if old := i.back(self.RING):
            pool.wait_ge(self.put_out[i.slot], old.dma())
        nc.gpsimd.tensor_copy(self.ixp[i.slot][:, :], self.g["put_i"][:, bass.ds(i.number, 1)]).then_inc(O.sem, 1)
        pool.wait_ge(*O.at(i, "put"))
        pool.wait_ge(*self.V.at(i, "xn"))
        nc.gpsimd.nop(nofuse=True)
        nc.gpsimd.indirect_dma_start(out=self.into[:, :],
                                     out_offset=bass.IndirectOffsetOnAxis(ap=self.ixp[i.slot][:, 0:1], axis=0),
                                     in_=self.xn[i.slot][:, :], in_offset=None, bounds_check=self.N - 1,
                                     oob_is_err=False).then_inc(self.put_out[i.slot], 16)

    def rstd(self, pool, i):
        nc, O, s = self.nc, self.O, i.slot
        pool.wait_ge(*self.V.at(i, "ag"))
        nc.gpsimd.tensor_tensor(self.ve[s][:, :], self.mv[s][:, 1:2], self.g["eps_c"][:, 0:1], ALU.add)\
            .then_inc(O.sem, 1)
        pool.wait_ge(*O.at(i, "e"))
        nc.gpsimd.tensor_tensor(self.rs[s][:, :], self.ve[s][:, :], self.g["mhalf"][:, 0:1], ALU.pow)\
            .then_inc(O.sem, 1)

    def stats(self, dve, i):
        nc, V, s = self.nc, self.V, i.slot
        dve.wait_ge(*V.at(i, "v"))
        nc.vector.bn_stats(self.st[s][:, :], self.v[s][:, :]).then_inc(V.sem, 1)
        dve.wait_ge(*V.at(i, "st"))
        nc.vector.nop(nofuse=True)
        nc.vector.bn_aggr(self.mv[s][:, :], self.st[s][:, :]).then_inc(V.sem, 1)

    def normalise(self, dve, i):
        s = i.slot
        dve.wait_ge(*self.O.at(i, "r"))
        if old := i.back(self.RING):
            dve.wait_ge(self.put_out[s], old.dma())
        self.nc.vector.tensor_scalar(self.xn[s][:, :], self.v[s][:, :], self.mv[s][:, 0:1], self.rs[s][:, :],
                                     ALU.subtract, ALU.mult).then_inc(self.V.sem, 1)

    def same_target(self, dve, i, scale=None):
        dve.wait_ge(self.cols_in[i.slot], i.dma())
        self.nc.vector.tensor_scalar(self.eq[i.slot][:, :], self.dc[i.slot][:, :],
                                     self.g["dst_f"][:, bass.ds(i.number, 1)], scale, ALU.is_equal,
                                     *([ALU.mult] if scale is not None else [])).then_inc(self.V.sem, 1)

    def load_cols(self, sp, i):
        a = self.g["dst_cols"][bass.ds(i.number, 1), :]
        sp.dma_start(self.dc[i.slot][:, :], a.to_broadcast([P, P])).then_inc(self.cols_in[i.slot], 16)

    def wait_out(self, sp):
        for s in self.slots:
            sp.wait_ge(self.put_out[s], 16 * len(range(s, self.NB, self.RING)))


def edge_sum(nc, g):
    with ExitStack() as c:
        E = EdgePass(nc, g, c, "sum", 6, "eq:1 cy:2 v:3 st:3 ag:3 xn:4", "dst_i:1 e:3 r:3 put:5", "ag:2", "no:0",
                     g["x"], g["X1"])
        V, O, M, RING = E.V, E.O, E.M, E.RING
        m = E.tiles("m", [P, D])
        m_in = [g["sm"](f"sum_m_in{s}", c) for s in E.slots]
        pA = E.banks("pA", [P, D], 2)
        with nc.Block() as block:
            @block.sync
            def _(sp):
                def turn(now):
                    if i := now.back(0):
                        if old := i.back(RING):
                            sp.wait_ge(*M.at(old, "ag"))
                        sp.dma_start(m[i.slot][:, :], g["MSG"][bass.ds(i.number * P, P), :]).then_inc(m_in[i.slot], 16)
                        E.load_cols(sp, i)
                E.turns.run(sp, turn)
                E.wait_out(sp)

            @block.gpsimd
            def _(pool):
                def turn(now):
                    if i := now.back(1):
                        E.gather_dst(pool, i)
                    if i := now.back(3):
                        E.rstd(pool, i)
                    if i := now.back(5):
                        E.scatter(pool, i)
                E.turns.run(pool, turn)

            @block.tensor
            def _(pe):
                def turn(now):
                    if i := now.back(2):
                        pe.wait_ge(*V.at(i, "cy"))
                        if old := i.back(2):
                            pe.wait_ge(*V.at(old, "v"))
                        nc.tensor.matmul(pA[i.slot % 2][:, :], g["ones_next"][:, :], g["bias0"][:, :],
                                         start=True, stop=False)
                        nc.tensor.matmul(pA[i.slot % 2][:, :], E.eq[i.slot][:, :], m[i.slot][:, :],
                                         start=False, stop=True).then_inc(M.sem, 1)
                E.turns.run(pe, turn)

            @block.vector
            def _(dve):
                def turn(now):
                    if i := now.back(1):
                        E.same_target(dve, i, g["keep"][:, bass.ds(i.number, 1)])
                    if i := now.back(2):
                        dve.wait_ge(m_in[i.slot], i.dma())
                        if prev := i.back(1):
                            dve.wait_ge(*M.at(prev, "ag"))
                            nc.vector.tensor_copy(m[i.slot][0:1, :], pA[prev.slot % 2][0:1, :]).then_inc(V.sem, 1)
                        else:
                            nc.vector.memset(m[i.slot][0:1, :], 0.0).then_inc(V.sem, 1)
                    if i := now.back(3):
                        dve.wait_ge(*M.at(i, "ag"))
                        dve.wait_ge(E.dst_in[i.slot], i.dma())
                        nc.vector.tensor_tensor(E.v[i.slot][:, :], pA[i.slot % 2][:, :], E.Xd[i.slot][:, :], ALU.add)\
                            .then_inc(V.sem, 1)
                        E.stats(dve, i)
                    if i := now.back(4):
                        E.normalise(dve, i)
                E.turns.run(dve, turn)


class SegmentMax:

    def __init__(self, E, H, own):
        self.E, self.H, self.own = E, H, own
        self.dv = E.tiles("dv", [H, P], I32)
        self.prev_in = [E.g["sm"](f"{E.name}_prev_in{s}", E.c) for s in E.slots]
        self.ne = E.tiles("ne", [H, P], count=2)
        self.kl = E.tiles("kl", [H, P + 1])
        self.LT = E.tiles("LT", [H, 2 * P], count=2)
        self.F = E.tiles("F", [H, P], count=2)
        self.B = E.tiles("B", [H, P], count=2)
        self.m = E.tiles("m", [H, P], count=2) if own else self.B
        self.dl = E.tiles("dl", [H, 2 * P], count=3)
        self.ET = E.tiles("ET", [H, 2 * P], count=3)

    def load(self, sp, i):
        a = self.E.g["dst_prev"][bass.ds(i.number, 1), :]
        sp.dma_start(self.dv[i.slot][:, :], a.to_broadcast([self.H, P])).then_inc(self.prev_in[i.slot], 16)

    def start(self, nc, done):
        for a in self.kl:
            done(nc.vector.memset(a[:, P:P + 1], NONE))
        for a in self.dl:
            done(nc.vector.memset(a[:, :], 0.0))
        done(nc.vector.memset(self.m[1][:, :], NONE))

    def breaks(self, dve, i):
        nc, V, H, s = self.E.nc, self.E.V, self.H, i.slot
        dve.wait_ge(self.prev_in[s], i.dma())
        dve.wait_ge(self.E.cols_in[s], i.dma())
        nc.vector.tensor_tensor(self.ne[s % 2][:, :], self.dv[s][:, :], self.E.dc[s][0:H, :], ALU.not_equal)\
            .then_inc(V.sem, 1)
        dve.wait_ge(*V.at(i, "ne"))
        nc.vector.tensor_scalar(self.kl[s][:, 0:P], self.ne[s % 2][:, :], NONE, None, ALU.mult).then_inc(V.sem, 1)

    def maxima(self, dve, i):
        nc, V, s = self.E.nc, self.E.V, i.slot
        kl, F, B, m, LT, dl = self.kl[s], self.F[s % 2], self.B[s % 2], self.m[s % 2], self.LT[s % 2], self.dl[s % 3]
        before = self.m[(s - 1) % 2][:, P - 1:P]
        dve.wait_ge(*V.at(i, "LT"))
        nc.vector.tensor_tensor_scan(F[:, 1:P], kl[:, 1:P], LT[:, 1:P], before, ALU.add, ALU.max).then_inc(V.sem, 1)
        dve.wait_ge(*V.at(i, "fw"))
        nc.vector.tensor_tensor_scan(B[:, P - 1:0:-1], kl[:, P:1:-1], F[:, P - 1:0:-1], NONE, ALU.add, ALU.max)\
            .then_inc(V.sem, 1)
        dve.wait_ge(*V.at(i, "bw"))
        if self.own:
            nc.vector.tensor_tensor(m[:, 1:P], B[:, 1:P], LT[:, P + 1:2 * P], ALU.max).then_inc(V.sem, 1)
            dve.wait_ge(*V.at(i, "mx"))
            nc.vector.tensor_tensor(dl[:, P + 1:2 * P], LT[:, P + 1:2 * P], m[:, 1:P], ALU.subtract)
        nc.vector.tensor_tensor(dl[:, 1:P], LT[:, 1:P], m[:, 1:P], ALU.subtract)
        nc.vector.tensor_scalar(dl[:, 0:1], before, m[:, 1:2], 0.0, ALU.subtract, ALU.min).then_inc(V.sem, 1)


def edge_heads(nc, g):
    with ExitStack() as c:
        E = EdgePass(nc, g, c, "heads", 6,
                     "lg:2 lr:2 x:3 hw:3 cy:3 u:4 v:4 st:4 ag:4 LT:2 fw:2 bw:2 mx:2 dl:2 t2:3 de:3 rd:3 t3:3 xn:4 "
                     "eq:1 ne:1 kl:1",
                     "t4:4 dst_i:0 t1:3 src_i:0 e:4 r:4 put:5",
                     "xr:3 lt:2 ag:3 t:1 hs:1 hd:1",
                     "ex:4 T:1 ET:2 hx:1 hd:1", g["X1"], g["X2"])
        V, O, M, A, RING = E.V, E.O, E.M, E.A, E.RING
        W = HID + 1
        SM = SegmentMax(E, HEADS, True)
        Xs = E.tiles("Xs", [P, D], count=3)
        XT = E.tiles("XT", [P, 2 * KC, P], count=2)
        Hx = E.tiles("Hx", [P, HEADS, W], count=3)
        Hw = E.tiles("Hw", [P, HEADS, W], count=2)
        Hd = E.tiles("Hd", [P, D + 2 * HEADS], count=3)
        as_ = E.tiles("as", [P, HEADS])
        lg = E.tiles("lg", [P, 2, HEADS])
        lr = E.tiles("lr", [P, 2, HEADS])
        xw = E.tiles("xw", [P, 2, HEADS])
        t1, t2, t3, t4, ex, u = (E.tiles(n, [P, D], count=2) for n in ("t1", "t2", "t3", "t4", "ex", "u"))
        de = E.tiles("de", [P, HEADS])
        rd = E.tiles("rd", [P, HEADS])
        started = g["sm"]("heads_started", c)
        pT = E.banks("pT", [P, 2 * KC, P], 1)[0]
        pHs = E.banks("pHs", [P, D + HEADS], 1)[0]
        pHd = E.banks("pHd", [P, D + 2 * HEADS], 1)[0]
        pA = E.banks("pA", [P, HEADS, W], 2)
        pS = E.banks("pS", [HEADS, 2 * P], 1)[0]
        pX = E.banks("pX", [P, 2 * HEADS], 1)[0]
        head = lambda a: a.rearrange("p (h c) -> p h c", h=HEADS)
        per_head = lambda a, n: a.unsqueeze(2).to_broadcast([a.shape[0], HEADS, n])
        start_count = []

        with nc.Block() as block:
            @block.sync
            def _(sp):
                def turn(now):
                    if i := now.back(0):
                        if old := i.back(RING):
                            sp.wait_ge(*V.at(old, "kl"))
                        E.load_cols(sp, i)
                        SM.load(sp, i)
                E.turns.run(sp, turn)
                E.wait_out(sp)

            @block.gpsimd
            def _(pool):
                def turn(now):
                    if i := now.back(4):
                        pool.wait_ge(*V.at(i, "t3"))
                        nc.gpsimd.tensor_tensor(t4[i.slot % 2][:, :], t3[i.slot % 2][:, :], g["b1m1_r"][:, :], ALU.add)\
                            .then_inc(O.sem, 1)
                    if i := now.back(0):
                        E.gather_dst(pool, i)
                    if i := now.back(3):
                        pool.wait_ge(*V.at(i, "x"))
                        nc.gpsimd.tensor_tensor(head(t1[i.slot % 2][:, :]), head(Hd[i.slot % 3][:, 0:D]),
                                                per_head(xw[i.slot][:, 1, :], HID), ALU.mult).then_inc(O.sem, 1)
                    if i := now.back(0):
                        if old := i.back(3):
                            pool.wait_ge(*M.at(old, "t"))
                        E.gather(pool, i, E.ixs, "src_i", Xs[i.slot % 3][:, :], E.src_in)
                    if i := now.back(4):
                        E.rstd(pool, i)
                    if i := now.back(5):
                        E.scatter(pool, i)
                E.turns.run(pool, turn)

            @block.vector
            def _(dve):
                count = [0]

                def done(ins):
                    count[0] += 1
                    ins.then_inc(started, 1)
                    dve.wait_ge(started, count[0])

                SM.start(nc, done)
                for a in Hx:
                    done(nc.vector.memset(a[:, :, :], 1.0))
                start_count.append(count[0])

                def turn(now):
                    if i := now.back(2):
                        s, h = i.slot, Hd[i.slot % 3]
                        dve.wait_ge(*A.at(i, "hd"))
                        nc.vector.tensor_tensor(lg[s][:, 0, :], as_[s][:, :], h[:, D + HEADS:D + 2 * HEADS], ALU.add)
                        nc.vector.tensor_tensor(lg[s][:, 1, :], h[:, D:D + HEADS], h[:, D + HEADS:D + 2 * HEADS],
                                                ALU.add).then_inc(V.sem, 1)
                        dve.wait_ge(*V.at(i, "lg"))
                        nc.vector.scalar_tensor_tensor(lr[s][:, :, :], lg[s][:, :, :], SLOPE, lg[s][:, :, :],
                                                       ALU.mult, ALU.max).then_inc(V.sem, 1)
                    if i := now.back(3):
                        s = i.slot
                        dve.wait_ge(*M.at(i, "xr"))
                        nc.vector.tensor_copy(xw[s][:, :, :].rearrange("p a h -> p (a h)"), pX[:, :]).then_inc(V.sem, 1)
                        dve.wait_ge(*V.at(i, "x"))
                        nc.vector.tensor_tensor(Hw[s % 2][:, :, :], Hx[s % 3][:, :, :], per_head(xw[s][:, 0, :], W),
                                                ALU.mult).then_inc(V.sem, 1)
                        if prev := i.back(1):
                            dve.wait_ge(*V.at(i, "hw"))
                            dve.wait_ge(*M.at(prev, "ag"))
                            nc.vector.tensor_tensor(Hw[s % 2][0:1, :, :], pA[prev.slot % 2][0:1, :, :],
                                                    per_head(xw[s][0:1, 0, :], W), ALU.mult).then_inc(V.sem, 1)
                        else:
                            dve.wait_ge(*V.at(i, "hw"))
                            nc.vector.memset(Hw[s % 2][0:1, :, :], 0.0).then_inc(V.sem, 1)
                    if i := now.back(4):
                        s = i.slot
                        dve.wait_ge(*O.at(i, "t4"))
                        nc.vector.scalar_tensor_tensor(u[s % 2][:, :], t4[s % 2][:, :], -1.0, E.Xd[s][:, :],
                                                       ALU.max, ALU.add).then_inc(V.sem, 1)
                        dve.wait_ge(*A.at(i, "ex"))
                        dve.wait_ge(*V.at(i, "u"))
                        nc.vector.scalar_tensor_tensor(E.v[s][:, :], ex[s % 2][:, :], 1.0, u[s % 2][:, :],
                                                       ALU.min, ALU.add).then_inc(V.sem, 1)
                        E.stats(dve, i)
                    if i := now.back(2):
                        dve.wait_ge(*M.at(i, "lt"))
                        nc.vector.tensor_copy(SM.LT[i.slot % 2][:, :], pS[:, :]).then_inc(V.sem, 1)
                        SM.maxima(dve, i)
                    if i := now.back(3):
                        s = i.slot
                        dve.wait_ge(*M.at(i, "ag"))
                        dve.wait_ge(*O.at(i, "t1"))
                        nc.vector.tensor_tensor(head(t2[s % 2][:, :]), pA[s % 2][:, :, 0:HID], head(t1[s % 2][:, :]),
                                                ALU.add).then_inc(V.sem, 1)
                        nc.vector.scalar_tensor_tensor(de[s][:, :], pA[s % 2][:, :, HID], 1e-16, xw[s][:, 1, :],
                                                       ALU.add, ALU.add).then_inc(V.sem, 1)
                        dve.wait_ge(*V.at(i, "de"))
                        nc.vector.reciprocal(rd[s][:, :], de[s][:, :]).then_inc(V.sem, 1)
                        dve.wait_ge(*V.at(i, "rd"))
                        nc.vector.tensor_tensor(head(t3[s % 2][:, :]), head(t2[s % 2][:, :]), per_head(rd[s][:, :], HID),
                                                ALU.mult).then_inc(V.sem, 1)
                    if i := now.back(4):
                        E.normalise(dve, i)
                    if i := now.back(1):
                        E.same_target(dve, i)
                        SM.breaks(dve, i)
                E.turns.run(dve, turn)

            @block.tensor
            def _(pe):
                pe.wait_ge(started, start_count[0])

                def turn(now):
                    if i := now.back(3):
                        pe.wait_ge(*A.at(i, "ET"))
                        if old := i.back(1):
                            pe.wait_ge(*V.at(old, "x"))
                        for a in range(2):
                            last = nc.tensor.matmul(pX[:, a * HEADS:(a + 1) * HEADS],
                                                    SM.ET[i.slot % 3][:, a * P:(a + 1) * P],
                                                    g["ident"][0:HEADS, 0:HEADS], start=True, stop=True)
                        last.then_inc(M.sem, 1)
                    if i := now.back(2):
                        pe.wait_ge(*V.at(i, "lr"))
                        if old := i.back(1):
                            pe.wait_ge(*V.at(old, "LT"))
                        for a in range(2):
                            last = nc.tensor.transpose(pS[:, a * P:(a + 1) * P], lr[i.slot][:, a, :], g["ident"][:, :])
                        last.then_inc(M.sem, 1)
                    if i := now.back(3):
                        s = i.slot
                        pe.wait_ge(*V.at(i, "cy"))
                        if old := i.back(2):
                            pe.wait_ge(*V.at(old, "de"))
                        nc.tensor.matmul(pA[s % 2][:, :, :].rearrange("p h c -> p (h c)"), E.eq[s][:, :],
                                         Hw[s % 2][:, :, :].rearrange("p h c -> p (h c)"), start=True, stop=True)\
                            .then_inc(M.sem, 1)
                    if i := now.back(1):
                        s = i.slot
                        pe.wait_ge(E.src_in[s], i.dma())
                        pe.wait_ge(E.dst_in[s], i.dma())
                        if old := i.back(1):
                            pe.wait_ge(*A.at(old, "T"))
                        for a, rows in enumerate((Xs[s % 3], E.Xd[s])):
                            for j in range(KC):
                                last = nc.tensor.transpose(pT[:, a * KC + j, :], rows[:, j * P:(j + 1) * P],
                                                           g["ident"][:, :])
                        last.then_inc(M.sem, 1)
                        pe.wait_ge(*A.at(i, "T"))
                        if old := i.back(1):
                            pe.wait_ge(*A.at(old, "hd"))
                        for j in range(KC):
                            last = nc.tensor.matmul(pHs[:, :], XT[s % 2][:, j, :], g["W1x"][:, j, 0:D + HEADS],
                                                    start=(j == 0), stop=(j == KC - 1))
                        last.then_inc(M.sem, 1)
                        for j in range(KC):
                            last = nc.tensor.matmul(pHd[:, :], XT[s % 2][:, KC + j, :], g["W1x"][:, j, :],
                                                    start=(j == 0), stop=(j == KC - 1))
                        last.then_inc(M.sem, 1)
                E.turns.run(pe, turn)

            @block.scalar
            def _(act):
                act.wait_ge(started, start_count[0])

                def turn(now):
                    if i := now.back(4):
                        act.wait_ge(*O.at(i, "t4"))
                        nc.scalar.activation(ex[i.slot % 2][:, :], t4[i.slot % 2][:, :], ACT.Exp, bias=1.0)\
                            .then_inc(A.sem, 1)
                    if i := now.back(1):
                        act.wait_ge(*M.at(i, "t"))
                        nc.scalar.activation(XT[i.slot % 2][:, :, :], pT[:, :, :], ACT.Copy).then_inc(A.sem, 1)
                    if i := now.back(2):
                        act.wait_ge(*V.at(i, "dl"))
                        nc.scalar.activation(SM.ET[i.slot % 3][:, :], SM.dl[i.slot % 3][:, :], ACT.Exp)\
                            .then_inc(A.sem, 1)
                    if i := now.back(1):
                        s = i.slot
                        act.wait_ge(*M.at(i, "hs"))
                        if old := i.back(3):
                            act.wait_ge(*O.at(old, "t1"))
                            act.wait_ge(*V.at(old, "hw"))
                        nc.scalar.activation(Hx[s % 3][:, :, 0:HID], head(pHs[:, 0:D]), ACT.Copy)
                        nc.scalar.activation(as_[s][:, :], pHs[:, D:D + HEADS], ACT.Copy).then_inc(A.sem, 1)
                        act.wait_ge(*M.at(i, "hd"))
                        nc.scalar.activation(Hd[s % 3][:, :], pHd[:, :], ACT.Copy).then_inc(A.sem, 1)
                E.turns.run(act, turn)


def edge_attention(nc, g):
    with ExitStack() as c:
        E = EdgePass(nc, g, c, "att", 7,
                     "s1:2 s2:2 lg:2 lr:2 x:3 eq:3 cy:3 rd:4 v:5 st:5 ag:5 LT:2 fw:2 bw:2 dl:2 xn:5 ne:1 kl:1",
                     "src_i:0 dst_i:0 e:5 r:5 put:6",
                     "xr:3 lt:2 ag:3 t:4 h:4",
                     "T:4 ET:2 A:3", g["X2"], g["X3"])
        V, O, M, A, RING = E.V, E.O, E.M, E.A, E.RING
        W = D + 1
        SM = SegmentMax(E, 1, False)
        Xs = E.tiles("Xs", [P, W])
        junk = E.tiles("junk", [P, D], count=2)
        junk2 = E.tiles("junk2", [P, D], count=2)
        sc = E.tiles("sc", [P, 2])
        lg = E.tiles("lg", [P, 1])
        lr = E.tiles("lr", [P, 1])
        xw = E.tiles("xw", [P, 1])
        As = E.tiles("As", [P, W])
        AT = E.tiles("AT", [P, KC, P], count=2)
        rd = E.tiles("rd", [P, 1])
        started = g["sm"]("att_started", c)
        pT = E.banks("pT", [P, KC, P], 1)[0]
        pH = E.banks("pH", [P, D], 2)
        pA = E.banks("pA", [P, W], 2)
        pS = E.banks("pS", [1, P], 1)[0]
        pX = E.banks("pX", [P, 1], 1)[0]
        start_count = []

        with nc.Block() as block:
            @block.sync
            def _(sp):
                def turn(now):
                    if i := now.back(0):
                        if old := i.back(RING):
                            sp.wait_ge(*V.at(old, "eq"))
                        E.load_cols(sp, i)
                        SM.load(sp, i)
                E.turns.run(sp, turn)
                E.wait_out(sp)

            @block.vector
            def _(dve):
                count = [0]

                def done(ins):
                    count[0] += 1
                    ins.then_inc(started, 1)
                    dve.wait_ge(started, count[0])

                SM.start(nc, done)
                for a in Xs:
                    done(nc.vector.memset(a[:, :], 1.0))
                start_count.append(count[0])

                def turn(now):
                    if i := now.back(2):
                        s = i.slot
                        dve.wait_ge(E.src_in[s], i.dma())
                        nc.vector.tensor_tensor_reduce(out=junk[s % 2][:, :], in0=Xs[s][:, 0:D], in1=g["us_r"][:, :],
                                                       scale=1.0, scalar=0.0, op0=ALU.mult, op1=ALU.add,
                                                       accum_out=sc[s][:, 0:1]).then_inc(V.sem, 1)
                        dve.wait_ge(E.dst_in[s], i.dma())
                        nc.vector.tensor_tensor_reduce(out=junk2[s % 2][:, :], in0=E.Xd[s][:, :], in1=g["ud_r"][:, :],
                                                       scale=1.0, scalar=0.0, op0=ALU.mult, op1=ALU.add,
                                                       accum_out=sc[s][:, 1:2]).then_inc(V.sem, 1)
                        dve.wait_ge(*V.at(i, "s2"))
                        nc.vector.scalar_tensor_tensor(lg[s][:, :], sc[s][:, 0:1], sc[s][:, 1:2],
                                                       g["efeat"][:, bass.ds(i.number, 1)], ALU.add, ALU.add)\
                            .then_inc(V.sem, 1)
                        dve.wait_ge(*V.at(i, "lg"))
                        nc.vector.scalar_tensor_tensor(lr[s][:, :], lg[s][:, :], SLOPE, lg[s][:, :],
                                                       ALU.mult, ALU.max).then_inc(V.sem, 1)
                    if i := now.back(3):
                        s = i.slot
                        dve.wait_ge(*M.at(i, "xr"))
                        nc.vector.tensor_copy(xw[s][:, :], pX[:, :]).then_inc(V.sem, 1)
                        dve.wait_ge(*V.at(i, "x"))
                        E.same_target(dve, i, xw[s][:, :])
                        if prev := i.back(1):
                            dve.wait_ge(*A.at(prev, "A"))
                            nc.vector.tensor_copy(Xs[s][0:1, :], pA[prev.slot % 2][0:1, :]).then_inc(V.sem, 1)
                        else:
                            nc.vector.memset(Xs[s][0:1, :], 0.0).then_inc(V.sem, 1)
                    if i := now.back(4):
                        dve.wait_ge(*A.at(i, "A"))
                        nc.vector.reciprocal(rd[i.slot][:, :], As[i.slot][:, D:W]).then_inc(V.sem, 1)
                    if i := now.back(5):
                        s = i.slot
                        dve.wait_ge(*M.at(i, "h"))
                        dve.wait_ge(*V.at(i, "rd"))
                        nc.vector.scalar_tensor_tensor(E.v[s][:, :], pH[s % 2][:, :], rd[s][:, :], E.Xd[s][:, :],
                                                       ALU.mult, ALU.add).then_inc(V.sem, 1)
                        E.stats(dve, i)
                    if i := now.back(2):
                        dve.wait_ge(*M.at(i, "lt"))
                        nc.vector.tensor_copy(SM.LT[i.slot % 2][:, 0:P], pS[:, :]).then_inc(V.sem, 1)
                        SM.maxima(dve, i)
                    if i := now.back(5):
                        E.normalise(dve, i)
                    if i := now.back(1):
                        SM.breaks(dve, i)
                E.turns.run(dve, turn)

            @block.gpsimd
            def _(pool):
                pool.wait_ge(started, start_count[0])

                def turn(now):
                    if i := now.back(0):
                        if old := i.back(RING):
                            pool.wait_ge(*M.at(old, "ag"))
                        E.gather(pool, i, E.ixs, "src_i", Xs[i.slot][:, 0:D], E.src_in)
                        E.gather_dst(pool, i)
                    if i := now.back(5):
                        E.rstd(pool, i)
                    if i := now.back(6):
                        E.scatter(pool, i)
                E.turns.run(pool, turn)

            @block.tensor
            def _(pe):
                pe.wait_ge(started, start_count[0])

                def turn(now):
                    if i := now.back(3):
                        pe.wait_ge(*A.at(i, "ET"))
                        if old := i.back(1):
                            pe.wait_ge(*V.at(old, "x"))
                        nc.tensor.matmul(pX[:, :], SM.ET[i.slot % 3][:, 0:P], g["ident"][0:1, 0:1],
                                         start=True, stop=True).then_inc(M.sem, 1)
                    if i := now.back(2):
                        pe.wait_ge(*V.at(i, "lr"))
                        if old := i.back(1):
                            pe.wait_ge(*V.at(old, "LT"))
                        nc.tensor.transpose(pS[:, :], lr[i.slot][:, :], g["ident"][:, :]).then_inc(M.sem, 1)
                    if i := now.back(3):
                        s = i.slot
                        pe.wait_ge(*V.at(i, "cy"))
                        if old := i.back(2):
                            pe.wait_ge(*A.at(old, "A"))
                        nc.tensor.matmul(pA[s % 2][:, :], E.eq[s][:, :], Xs[s][:, :], start=True, stop=True)\
                            .then_inc(M.sem, 1)
                    if i := now.back(4):
                        s = i.slot
                        pe.wait_ge(*A.at(i, "A"))
                        if old := i.back(1):
                            pe.wait_ge(*A.at(old, "T"))
                        for j in range(KC):
                            last = nc.tensor.transpose(pT[:, j, :], As[s][:, j * P:(j + 1) * P], g["ident"][:, :])
                        last.then_inc(M.sem, 1)
                        pe.wait_ge(*A.at(i, "T"))
                        if old := i.back(2):
                            pe.wait_ge(*V.at(old, "v"))
                        for j in range(KC):
                            last = nc.tensor.matmul(pH[s % 2][:, :], AT[s % 2][:, j, :], g["W2T"][:, j, :],
                                                    start=(j == 0), stop=(j == KC - 1))
                        last.then_inc(M.sem, 1)
                E.turns.run(pe, turn)

            @block.scalar
            def _(act):
                def turn(now):
                    if i := now.back(4):
                        act.wait_ge(*M.at(i, "t"))
                        nc.scalar.activation(AT[i.slot % 2][:, :, :], pT[:, :, :], ACT.Copy).then_inc(A.sem, 1)
                    if i := now.back(2):
                        act.wait_ge(*V.at(i, "dl"))
                        nc.scalar.activation(SM.ET[i.slot % 3][:, 0:P], SM.dl[i.slot % 3][:, 0:P], ACT.Exp)\
                            .then_inc(A.sem, 1)
                    if i := now.back(3):
                        act.wait_ge(*M.at(i, "ag"))
                        nc.scalar.activation(As[i.slot][:, :], pA[i.slot % 2][:, :], ACT.Copy).then_inc(A.sem, 1)
                E.turns.run(act, turn)


def edge_gru(nc, g):
    with ExitStack() as c:
        E = EdgePass(nc, g, c, "gru", 7,
                     "cy:2 q:5 q1:5 oh:1 eq:1 w:5 v:5 st:5 ag:5 xn:5",
                     "src_i:0 dst_i:1 d:5 s:5 e:5 r:5 put:6",
                     "ag:2 gru:4 ct:3 t:3",
                     "A:2 rz:4 cT:3 aT:3 n:5", g["X3"], g["out"])
        V, O, M, A, RING = E.V, E.O, E.M, E.A, E.RING
        W = D + RELS
        Xs = E.tiles("Xs", [P, W])
        As = E.tiles("As", [P, W], count=3)
        aT = E.tiles("aT", [P, 2 * KC, P], count=2)
        cT = E.tiles("cT", [RELS, P], count=2)
        rz = E.tiles("rz", [P, 2 * D], count=2)
        q, q1, n, d, sm_, w = (E.tiles(m, [P, D], count=2) for m in ("q", "q1", "n", "d", "sm", "w"))
        rel_i = g["sb"]("rel_i", [P, RELS], I32, c)
        rel_f = g["sb"]("rel_f", [P, RELS], F32, c)
        started = g["sm"]("gru_started", c)
        pA = E.banks("pA", [P, W], 2)
        pC = E.banks("pC", [RELS, P], 1)[0]
        pT = E.banks("pT", [P, 2 * KC, P], 1)[0]
        pRZ = E.banks("pRZ", [P, 2 * D], 2)
        pN = E.banks("pN", [P, 2, D], 2)

        with nc.Block() as block:
            @block.sync
            def _(sp):
                def turn(now):
                    if i := now.back(0):
                        if old := i.back(RING):
                            sp.wait_ge(*V.at(old, "eq"))
                        E.load_cols(sp, i)
                E.turns.run(sp, turn)
                E.wait_out(sp)

            @block.gpsimd
            def _(pool):
                nc.gpsimd.iota(rel_i[:, :], pattern=[[1, RELS]], base=0, channel_multiplier=0).then_inc(started, 1)

                def turn(now):
                    if i := now.back(0):
                        if old := i.back(RING):
                            pool.wait_ge(*M.at(old, "ag"))
                        E.gather(pool, i, E.ixs, "src_i", Xs[i.slot][:, 0:D], E.src_in)
                    if i := now.back(1):
                        E.gather_dst(pool, i)
                    if i := now.back(5):
                        s = i.slot
                        pool.wait_ge(*A.at(i, "n"))
                        nc.gpsimd.tensor_tensor(d[s % 2][:, :], E.Xd[s][:, :], n[s % 2][:, :], ALU.subtract)\
                            .then_inc(O.sem, 1)
                        nc.gpsimd.tensor_tensor(sm_[s % 2][:, :], E.Xd[s][:, :], n[s % 2][:, :], ALU.add)\
                            .then_inc(O.sem, 1)
                        E.rstd(pool, i)
                    if i := now.back(6):
                        E.scatter(pool, i)
                E.turns.run(pool, turn)

            @block.vector
            def _(dve):
                dve.wait_ge(started, 1)
                nc.vector.tensor_copy(rel_f[:, :], rel_i[:, :]).then_inc(started, 1)
                dve.wait_ge(started, 2)

                def turn(now):
                    if i := now.back(2):
                        s = i.slot
                        dve.wait_ge(E.src_in[s], i.dma())
                        dve.wait_ge(*V.at(i, "oh"))
                        if prev := i.back(1):
                            dve.wait_ge(*A.at(prev, "A"))
                            nc.vector.tensor_copy(Xs[s][0:1, :], pA[prev.slot % 2][0:1, :]).then_inc(V.sem, 1)
                        else:
                            nc.vector.memset(Xs[s][0:1, :], 0.0).then_inc(V.sem, 1)
                    if i := now.back(5):
                        s = i.slot
                        dve.wait_ge(*A.at(i, "rz"))
                        nc.vector.scalar_tensor_tensor(q[s % 2][:, :], rz[s % 2][:, 0:D], 1.0, pN[s % 2][:, 1, :],
                                                       ALU.add, ALU.mult).then_inc(V.sem, 1)
                        dve.wait_ge(*V.at(i, "q"))
                        nc.vector.tensor_tensor(q1[s % 2][:, :], q[s % 2][:, :], pN[s % 2][:, 0, :], ALU.add)\
                            .then_inc(V.sem, 1)
                    if i := now.back(1):
                        s = i.slot
                        if old := i.back(RING):
                            dve.wait_ge(*M.at(old, "ag"))
                        nc.vector.tensor_scalar(Xs[s][:, D:W], rel_f[:, :], g["type_f"][:, bass.ds(i.number, 1)], None,
                                                ALU.is_equal).then_inc(V.sem, 1)
                        E.same_target(dve, i)
                    if i := now.back(5):
                        s = i.slot
                        dve.wait_ge(*O.at(i, "s"))
                        nc.vector.scalar_tensor_tensor(w[s % 2][:, :], rz[s % 2][:, D:2 * D], 1.0, d[s % 2][:, :],
                                                       ALU.add, ALU.mult).then_inc(V.sem, 1)
                        dve.wait_ge(*V.at(i, "w"))
                        nc.vector.scalar_tensor_tensor(E.v[s][:, :], w[s % 2][:, :], 0.5, sm_[s % 2][:, :],
                                                       ALU.mult, ALU.add).then_inc(V.sem, 1)
                        E.stats(dve, i)
                        E.normalise(dve, i)
                E.turns.run(dve, turn)

            @block.tensor
            def _(pe):
                def turn(now):
                    if i := now.back(2):
                        s = i.slot
                        pe.wait_ge(*V.at(i, "cy"))
                        if old := i.back(2):
                            pe.wait_ge(*A.at(old, "A"))
                        nc.tensor.matmul(pA[s % 2][:, :], E.eq[s][:, :], Xs[s][:, :], start=True, stop=True)\
                            .then_inc(M.sem, 1)
                    if i := now.back(4):
                        s = i.slot
                        pe.wait_ge(*A.at(i, "aT"))
                        if old := i.back(2):
                            pe.wait_ge(*V.at(old, "q1"))
                        for o, lo, hi, bias, ins in ((pRZ[s % 2][:, :], 0, 2 * D, g["bias3"][:, 0:2 * D], (0, 1)),
                                                     (pN[s % 2][:, 0, :], 2 * D, 3 * D, g["bias_in"][:, :], (0,)),
                                                     (pN[s % 2][:, 1, :], 2 * D, 3 * D, g["bias3"][:, 2 * D:3 * D], (1,))):
                            terms = [(g["ones_b"][:, :], bias)]
                            if 0 in ins:
                                terms.append((cT[s % 2][:, :], g["relw"][:, lo:hi]))
                            for a in ins:
                                wT = g["whhT"] if a else g["wihT"]
                                terms += [(aT[s % 2][:, a * KC + j, :], wT[:, j, lo:hi]) for j in range(KC)]
                            for x_, (l, r) in enumerate(terms):
                                last = nc.tensor.matmul(o, l, r, start=(x_ == 0), stop=(x_ == len(terms) - 1))
                        last.then_inc(M.sem, 1)
                    if i := now.back(3):
                        s = i.slot
                        pe.wait_ge(*A.at(i, "A"))
                        if old := i.back(1):
                            pe.wait_ge(*A.at(old, "aT"))
                        nc.tensor.transpose(pC[:, :], As[s % 3][:, D:W], g["ident"][:, :]).then_inc(M.sem, 1)
                        pe.wait_ge(E.dst_in[s], i.dma())
                        for a, rows in enumerate((As[s % 3], E.Xd[s])):
                            for j in range(KC):
                                last = nc.tensor.transpose(pT[:, a * KC + j, :], rows[:, j * P:(j + 1) * P],
                                                           g["ident"][:, :])
                        last.then_inc(M.sem, 1)
                E.turns.run(pe, turn)

            @block.scalar
            def _(act):
                def turn(now):
                    if i := now.back(2):
                        act.wait_ge(*M.at(i, "ag"))
                        nc.scalar.activation(As[i.slot % 3][:, :], pA[i.slot % 2][:, :], ACT.Copy).then_inc(A.sem, 1)
                    if i := now.back(4):
                        act.wait_ge(*M.at(i, "gru"))
                        if old := i.back(2):
                            act.wait_ge(*V.at(old, "w"))
                        nc.scalar.activation(rz[i.slot % 2][:, :], pRZ[i.slot % 2][:, :], ACT.Tanh, scale=0.5)\
                            .then_inc(A.sem, 1)
                    if i := now.back(3):
                        act.wait_ge(*M.at(i, "ct"))
                        nc.scalar.activation(cT[i.slot % 2][:, :], pC[:, :], ACT.Copy).then_inc(A.sem, 1)
                        act.wait_ge(*M.at(i, "t"))
                        nc.scalar.activation(aT[i.slot % 2][:, :, :], pT[:, :, :], ACT.Copy).then_inc(A.sem, 1)
                    if i := now.back(5):
                        act.wait_ge(*V.at(i, "q1"))
                        nc.scalar.activation(n[i.slot % 2][:, :], q1[i.slot % 2][:, :], ACT.Tanh).then_inc(A.sem, 1)
                E.turns.run(act, turn)


NB_EDGES = [0]


def kernel(x, src, dst, edge_attr_64, edge_type_16, edge_weight, L0_gnn_node_lock, L0_gnn_W, L0_gnn_b, L1_gnn_W0,
           L1_gnn_att_src0, L1_gnn_att_dst0, L1_gnn_b0, L1_gnn_W1, L1_gnn_att_src1, L1_gnn_att_dst1, L1_gnn_b1,
           L2_gnn_W, L2_gnn_A, L3_gnn_relvectors, L3_gnn_w_ih, L3_gnn_w_hh, L3_gnn_b_ih, L3_gnn_b_hh):
    import numpy as np
    import concourse.bacc as bacc
    from concourse.bass_utils import run_bass_kernel_spmd

    N, E = x.shape[0], src.shape[0]
    NB_EDGES[0] = E
    NB = -(-E // SLOT_EDGES)
    NB += -NB % 6
    PAD = NB * SLOT_EDGES

    def flat(a, fill, ahead=0):
        a = np.asarray(a)
        f = np.full((PAD + 2,) + a.shape[1:], fill, a.dtype)
        f[1:E + 1] = a
        f[0] = -1 if a.dtype.kind == "i" else 0
        return f[1 + ahead:1 + ahead + PAD]

    def slots(a, fill, first):
        f = flat(a, fill) if not isinstance(a, tuple) else a[0]
        f = f.reshape((NB, SLOT_EDGES) + f.shape[1:])
        row0 = np.broadcast_to(first, (NB, 1) + f.shape[2:]).astype(f.dtype)
        return np.ascontiguousarray(np.moveaxis(np.concatenate([row0, f], axis=1), 0, 1))

    cur = flat(dst, N).reshape(NB, SLOT_EDGES)
    before = flat(dst, N, -1).reshape(NB, SLOT_EDGES)
    after = flat(dst, N, 1)
    prev_last = before[:, :1]
    pack = lambda w: np.ascontiguousarray(np.asarray(w).T)
    att = np.zeros((D, 2 * HEADS), np.float32)
    for j, a in enumerate((L1_gnn_att_src0, L1_gnn_att_dst0)):
        for h in range(HEADS):
            att[h * HID:(h + 1) * HID, j * HEADS + h] = np.asarray(a)[0, h]
    ins = {
        "x": np.asarray(x),
        "src": slots(src, 0, prev_last),
        "dst": slots(dst, N, prev_last),
        "dst_next": slots((after,), N, prev_last),
        "dst_cols": np.ascontiguousarray(np.concatenate([cur[:, -1:], cur], axis=1)),
        "dst_prev": np.ascontiguousarray(np.concatenate([cur[:, -1:], before], axis=1)),
        "attr": slots(edge_attr_64, 0, 0),
        "etype": slots(edge_type_16, 0, 0),
        "ew": slots(edge_weight, 0, 0),
        "node_lock": np.asarray(L0_gnn_node_lock).reshape(1, -1),
        "W0e_T": pack(L0_gnn_W), "b0e": np.asarray(L0_gnn_b).reshape(1, -1),
        "W1_T": pack(L1_gnn_W0), "W1n": np.asarray(L1_gnn_W0), "att1": att, "b1": np.asarray(L1_gnn_b0).reshape(1, -1),
        "W2_T": pack(L2_gnn_W), "W2n": np.asarray(L2_gnn_W), "A2": np.asarray(L2_gnn_A),
        "a2_T": np.ascontiguousarray(np.asarray(L2_gnn_A)[0, :2 * D].reshape(2, D).T),
        "rel_T": pack(L3_gnn_relvectors), "wih_T": pack(L3_gnn_w_ih), "whh_T": pack(L3_gnn_w_hh),
        "b_ih": np.asarray(L3_gnn_b_ih).reshape(1, -1), "b_hh": np.asarray(L3_gnn_b_hh).reshape(1, -1),
    }
    nc = bacc.Bacc("TRN2", target_bir_lowering=False, num_devices=1)
    args = [nc.dram_tensor(f"in_{n}", a.shape, mybir.dt.from_np(a.dtype), kind="ExternalInput").ap()
            for n, a in ins.items()]
    args.append(nc.dram_tensor("out", (N, D), F32, kind="ExternalOutput").ap())
    for n in ("X1", "X2", "X3"):
        args.append(nc.dram_tensor(n, (N, D), F32, kind="Internal").ap())
    args.append(nc.dram_tensor("MSG", (NB * P, D), F32, kind="Internal").ap())
    gnn(nc, *args)
    r = run_bass_kernel_spmd(nc, [{f"in_{n}": a for n, a in ins.items()}], core_ids=[0])
    return r.results[0]["out"]
```

```python
from contextlib import ExitStack

import concourse.bass as bass
from concourse import mybir
from concourse.alu_op_type import AluOpType as ALU

ACT = mybir.ActivationFunctionType
AX = mybir.AxisListType
F32 = mybir.dt.float32
BF16 = mybir.dt.bfloat16
I32 = mybir.dt.int32

P = 128
D = 256
KC = D // P
HEADS = 8
HID = D // HEADS
RELS = 16
EDIM = 64
SLOT_EDGES = P - 1
EPS = 1e-5
THR_A = 0.1
THR_W = 0.1
SLOPE = 0.2
FAR = 1 << 20
NONE = -1e30


class Item:

    def __init__(self, ring, count, round_, slot):
        self.ring, self.count, self.round, self.slot = ring, count, round_ + slot // ring, slot % ring
        self.number = self.round * ring + self.slot
        self.fixed = isinstance(self.round, int)

    def back(self, d):
        other = Item(self.ring, self.count, self.round, self.slot - d)
        return None if other.fixed and not 0 <= other.number < self.count else other

    def dma(self):
        return self.round * 16 + 16


class Turns:

    def __init__(self, ring, count, longest, even=None):
        self.ring, self.count, self.longest = ring, count, longest
        self.first = -(-(longest + ring) // ring)
        self.last = (even or count) // ring

    def run(self, eng, body):
        item = lambda r, s: Item(self.ring, self.count, r, s)
        for t in range(self.first * self.ring):
            body(item(0, t))
        with eng.Fori(self.first, self.last) as r:
            for s in range(self.ring):
                body(item(r, s))
        for t in range(self.last * self.ring, self.count + self.longest):
            body(item(0, t))


class Steps:

    def __init__(self, sem, plan):
        self.sem = sem
        steps = [x.split(":") for x in plan.split()]
        self.order = {n: i for i, (n, _) in enumerate(steps)}
        self.delay = {n: int(d) for n, d in steps}
        self.n, self.skipped = len(steps), sum(self.delay.values())

    def at(self, item, name):
        turn, pos = item.number + self.delay[name], self.order[name]
        if not item.fixed:
            return self.sem, item.round * (item.ring * self.n) + \
                ((item.slot + self.delay[name]) * self.n - self.skipped + pos + 1)
        return self.sem, sum(min(max(turn + (self.order[m] <= pos) - d, 0), item.count) for m, d in self.delay.items())


def bcast_rows(ap, rows, cols):
    return bass.AP(ap.tensor, ap.offset, [[0, rows], [1, cols]])


def gnn(nc, x, src, dst, dst_next, dst_cols, dst_prev, attr, etype, ew, node_lock, W0e_T, b0e, W1_T, W1n, att1, b1,
        W2_T, W2n, A2, a2_T, rel, wih_T, whh_T, b_ih, b_hh, out, X1, X2, X3, MSG):
    N = x.shape[0]
    NB = src.shape[1]
    NEDGE = NB_EDGES[0]
    L = node_lock.shape[1]
    PAIR = 2 * P
    PAIRS = N // PAIR
    REST = N - PAIRS * PAIR
    assert 0 < REST <= P
    es = ExitStack()
    with es:
        def sb(name, shape, dt=F32, ctx=es):
            return ctx.enter_context(nc.sbuf_tensor(name, shape, dt))

        def ps(name, shape, ctx, dt=F32):
            return ctx.enter_context(nc.psum_tensor(name, shape, dt))

        used = []

        def sm(name, ctx=es):
            used.append(ctx.enter_context(nc.semaphore(name)))
            return used[-1]

        ident = sb("ident", [P, P])
        ones_b = sb("ones_b", [P, P], BF16)
        sumsq = sb("sumsq", [P, 2, D])
        mhalf = sb("mhalf", [P, 2])
        src_f = sb("src_f", [P, NB])
        dst_f = sb("dst_f", [P, NB])
        rel_i = sb("rel_i", [P, NB], I32)
        w_e = sb("w_e", [P, NB])
        src_i = sb("src_i", [P, NB], I32)
        dst_i = sb("dst_i", [P, NB], I32)
        put_i = sb("put_i", [P, NB], I32)
        efeat = sb("efeat", [P, NB])
        keep = sb("keep", [P, NB])
        Weff_T = sb("Weff_T", [P, KC, D])
        b0e_r = sb("b0e_r", [P, D])
        W1x = sb("W1x", [P, KC, D + 2 * HEADS])
        b1m1_r = sb("b1m1_r", [P, D])
        ones_next = sb("ones_next", [P, P], BF16)
        bias0 = sb("bias0", [P, D], BF16)
        bias1 = sb("bias1", [P, D], BF16)
        bias_in = sb("bias_in", [P, D], BF16)
        W2T = sb("W2T", [P, KC, D])
        us_r = sb("us_r", [P, D])
        ud_r = sb("ud_r", [P, D])
        whhT = sb("whhT", [P, KC, 3 * D])
        wihT = sb("wihT", [P, KC, 3 * D])
        bias3 = sb("bias3", [P, 3 * D], BF16)
        bin_r = sb("bin_r", [P, D])

        def queue_sems(name):
            return [es.enter_context(nc.semaphore(f"{name}{s}")) for s in range(EdgePass.RING)]

        state = locals()
        for phase in (prepare, dense, prune, edge_norms, edge_sum, edge_heads, edge_attention, edge_gru):
            phase(nc, state)
            with nc.Block() as block:
                @block.gpsimd
                def _(pool):
                    for s in used:
                        pool.sem_clear(s)
            used.clear()


def prepare(nc, g):
    (N, NB, L, sb, ps, sm) = (g[n] for n in ("N", "NB", "L", "sb", "ps", "sm"))
    x = g["x"]
    with ExitStack() as c:
        loaded = sm("loaded", c)
        dve_done = sm("dve_done", c)
        pe_done = sm("pe_done", c)
        pool_done = sm("pool_done", c)
        attr_loaded = [sm(f"attr_loaded{s}", c) for s in range(2)]
        attr_used = sm("attr_used", c)
        W1n = sb("W1n", [P, KC, D], F32, c)
        W2n = sb("W2n", [P, KC, D], F32, c)
        att = sb("att", [P, KC, 2 * HEADS], F32, c)
        a2 = sb("a2", [P, KC, 2], F32, c)
        a2b = sb("a2b", [P, KC, 2, P], F32, c)
        ae_r = sb("ae_r", [P, EDIM], F32, c)
        next_i = sb("next_i", [P, NB], I32, c)
        bi_r = sb("bi_r", [P, 3 * D], F32, c)
        bh_r = sb("bh_r", [P, 3 * D], F32, c)
        bsum = sb("bsum", [P, 3 * D], F32, c)
        bsum2 = sb("bsum2", [P, 3 * D], F32, c)
        bh = sb("bh", [P, 3 * D], BF16, c)
        b0c, b1c, bic = (sb(n, [P, D], F32, c) for n in ("b0c", "b1c", "bic"))
        tmp = sb("tmp", [P, NB], F32, c)
        tmp2 = sb("tmp2", [P, NB], F32, c)
        src0 = sb("src0", [P, NB], I32, c)
        dst0 = sb("dst0", [P, NB], I32, c)
        AB = NB // 6 if NB % 6 == 0 else NB
        at_sb = [sb(f"at_sb{s}", [P, AB, EDIM], F32, c) for s in range(2)]
        pv = ps("pv", [P, KC, 2 * HEADS], c)
        pu = ps("pu", [P, 2, D], c)
        block = c.enter_context(nc.Block())

        @block.sync
        def _(sp):
            kview = lambda a: a.rearrange("(c p) n -> p c n", p=P)
            loads = [
                (g["W1x"][:, :, 0:D], kview(g["W1_T"])),
                (W1n[:, :, :], kview(g["W1n"])), (W2n[:, :, :], kview(g["W2n"])),
                (g["W2T"][:, :, :], kview(g["W2_T"])), (att[:, :, :], kview(g["att1"])),
                (a2[:, :, :], kview(g["a2_T"])),
                (ae_r[:, :], bcast_rows(g["A2"][0:1, 2 * D:], P, EDIM)),
                (g["wihT"][:, :, :], kview(g["wih_T"])),
                (g["whhT"][:, :, :], kview(g["whh_T"])),
                (g["b0e_r"][:, :], bcast_rows(g["b0e"], P, D)), (g["b1m1_r"][:, :], bcast_rows(g["b1"], P, D)),
                (bi_r[:, :], bcast_rows(g["b_ih"], P, 3 * D)), (bh_r[:, :], bcast_rows(g["b_hh"], P, 3 * D)),
                (src0[:, :], g["src"]), (dst0[:, :], g["dst"]), (next_i[:, :], g["dst_next"]),
                (g["rel_i"][:, :], g["etype"]), (g["w_e"][:, :], g["ew"]),
            ]
            for dst_ap, src_ap in loads:
                sp.dma_start(dst_ap, src_ap).then_inc(loaded, 16)
            for a in range(NB // AB):
                if a >= 2:
                    sp.wait_ge(attr_used, a - 1)
                sp.dma_start(at_sb[a % 2][:, :, :], g["attr"][:, a * AB:(a + 1) * AB, :]).then_inc(attr_loaded[a % 2], 16)

        NLOAD = 18

        @block.gpsimd
        def _(pool):
            nc.gpsimd.memset(g["ident"][:, :], 0.0).then_inc(pool_done, 1)
            pool.wait_ge(pool_done, 1)
            nc.gpsimd.affine_select(out=g["ident"][:, :], in_=g["ident"][:, :], compare_op=ALU.not_equal, fill=1.0,
                                    base=0, pattern=[[-1, P]], channel_multiplier=1).then_inc(pool_done, 1)
            nc.gpsimd.memset(g["ones_b"][:, :], 1.0)
            nc.gpsimd.memset(g["sumsq"][:, :, :], 0.0)
            nc.gpsimd.memset(g["mhalf"][:, :], -0.5)
            nc.gpsimd.memset(g["ones_next"][:, 0:1], 0.0)
            nc.gpsimd.memset(g["ones_next"][:, 1:P], 1.0)
            for b in ("bias0", "bias1", "bias_in"):
                nc.gpsimd.memset(g[b][:, :], 0.0)
            nc.gpsimd.memset(g["bias3"][:, :], 0.0).then_inc(pool_done, 1)

        @block.vector
        def _(dve):
            count = [0]

            def done(ins):
                count[0] += 1
                ins.then_inc(dve_done, 1)
                dve.wait_ge(dve_done, count[0])

            dve.wait_ge(loaded, 16 * NLOAD)
            done(nc.vector.tensor_copy(g["src_f"][:, :], src0[:, :]))
            done(nc.vector.tensor_copy(g["dst_f"][:, :], dst0[:, :]))
            nc.vector.tensor_scalar(g["src_i"][:, :], g["src_f"][:, :], 0.0, float(N - 1), ALU.max, ALU.min)
            nc.vector.tensor_scalar(g["dst_i"][:, :], g["dst_f"][:, :], 0.0, float(N - 1), ALU.max, ALU.min)
            done(nc.vector.tensor_tensor(tmp[:, :], g["dst_f"][:, :], next_i[:, :], ALU.is_equal))
            done(nc.vector.scalar_tensor_tensor(tmp2[:, :], tmp[:, :], float(FAR), g["dst_f"][:, :], ALU.mult, ALU.add))
            done(nc.vector.tensor_copy(g["put_i"][:, :], tmp2[:, :]))
            for a in range(NB // AB):
                t = at_sb[a % 2]
                dve.wait_ge(attr_loaded[a % 2], 16 * (a // 2 + 1))
                done(nc.vector.tensor_tensor(t[:, :, :], t[:, :, :],
                                             ae_r[:, :].unsqueeze(1).to_broadcast([P, AB, EDIM]), ALU.mult))
                nc.vector.tensor_reduce(g["efeat"][:, a * AB:(a + 1) * AB], t[:, :, :], AX.X, ALU.add)\
                    .then_inc(attr_used, 1)
            done(nc.vector.tensor_scalar(g["b1m1_r"][:, :], g["b1m1_r"][:, :], -1.0, None, ALU.add))
            nc.vector.tensor_copy(g["bin_r"][:, :], bi_r[:, 2 * D:3 * D])
            nc.vector.tensor_copy(bic[:, :], bi_r[:, 2 * D:3 * D])
            nc.vector.tensor_copy(b0c[:, :], g["b0e_r"][:, :])
            nc.vector.tensor_copy(b1c[:, :], g["b1m1_r"][:, :])
            nc.vector.tensor_scalar(bsum[:, 2 * D:3 * D], bh_r[:, 2 * D:3 * D], 0.5, None, ALU.mult)
            nc.vector.tensor_scalar(g["whhT"][:, :, 2 * D:3 * D], g["whhT"][:, :, 2 * D:3 * D], 0.5, None, ALU.mult)
            done(nc.vector.tensor_tensor(bsum[:, 0:2 * D], bi_r[:, 0:2 * D], bh_r[:, 0:2 * D], ALU.add))
            dve.wait_ge(pool_done, 3)
            for row, into, n in ((bsum, "bias3", 3 * D), (b0c, "bias0", D), (b1c, "bias1", D), (bic, "bias_in", D)):
                a, b = row, bsum2
                for part in range(3):
                    done(nc.vector.tensor_copy(bh[:, 0:n], a[:, 0:n]))
                    nc.vector.tensor_copy(g[into][32 * part:32 * part + 1, :], bh[32 * part:32 * part + 1, 0:n])
                    done(nc.vector.tensor_tensor(b[:, 0:n], a[:, 0:n], bh[:, 0:n], ALU.subtract))
                    a, b = b, a
            for j in range(2):
                done(nc.vector.tensor_copy(a2b[:, :, j, :], a2[:, :, j:j + 1].to_broadcast([P, KC, P])))
            g["count_a2b"] = count[0]
            dve.wait_ge(pe_done, 1)
            nc.vector.tensor_copy(g["W1x"][:, :, D:D + 2 * HEADS], pv[:, :, :])
            nc.vector.tensor_copy(g["us_r"][:, :], pu[:, 0, :])
            done(nc.vector.tensor_copy(g["ud_r"][:, :], pu[:, 1, :]))

        @block.tensor
        def _(pe):
            pe.wait_ge(loaded, 16 * NLOAD)
            for k in range(KC):
                for o in range(KC):
                    nc.tensor.matmul(pv[:, k, :], W1n[:, o, k * P:(k + 1) * P], att[:, o, :],
                                     start=(o == 0), stop=(o == KC - 1))
            pe.wait_ge(dve_done, g["count_a2b"])
            for j in range(2):
                for o in range(KC):
                    last = nc.tensor.matmul(pu[:, j, :], a2b[:, o, j, :], W2n[:, o, :],
                                            start=(o == 0), stop=(o == KC - 1))
            last.then_inc(pe_done, 1)


def prune(nc, g):
    sb, ps, sm = g["sb"], g["ps"], g["sm"]
    with ExitStack() as c:
        w0_loaded, dve_done, pe_done, act_done = (sm(n, c) for n in ("w0_loaded", "prune_dve", "prune_pe", "prune_act"))
        W0r = sb("W0r", [P, KC, D], F32, c)
        onesf = sb("onesf", [P, P], F32, c)
        accr = sb("accr", [P, D], F32, c)
        nk = sb("nk", [P, KC], F32, c)
        nk2 = sb("nk2", [P, KC], F32, c)
        na = sb("na", [P, 1], F32, c)
        thr = sb("thr", [P, KC], F32, c)
        flag = sb("flag", [P, 1], F32, c)
        absw = sb("absw", [P, KC, D], F32, c)
        pn = ps("pn", [P, KC + 1], c)
        at = {}
        block = c.enter_context(nc.Block())

        @block.sync
        def _(sp):
            sp.dma_start(W0r[:, :, :], g["W0e_T"].rearrange("(c p) n -> p c n", p=P)).then_inc(w0_loaded, 16)

        @block.vector
        def _(dve):
            count = [0]

            def done(ins):
                count[0] += 1
                ins.then_inc(dve_done, 1)
                dve.wait_ge(dve_done, count[0])

            nc.vector.memset(onesf[:, :], 1.0)
            done(nc.vector.tensor_tensor(accr[:, :], g["sumsq"][:, 0, :], g["sumsq"][:, 1, :], ALU.add))
            at["sums"] = count[0]
            dve.wait_ge(w0_loaded, 16)
            dve.wait_ge(act_done, 1)
            done(nc.vector.tensor_copy(nk2[:, :], pn[:, 0:KC]))
            done(nc.vector.tensor_tensor(nk2[:, 0:1], nk2[:, 0:1], nk2[:, 1:2], ALU.add))
            at["norms"] = count[0]
            dve.wait_ge(act_done, 2)
            done(nc.vector.reciprocal(thr[:, :], nk[:, :]))
            done(nc.vector.tensor_scalar(na[:, :], na[:, :], 1.0 / D, None, ALU.mult))
            done(nc.vector.tensor_scalar(flag[:, :], na[:, :], 1e-8, None, ALU.is_gt))
            done(nc.vector.tensor_scalar(na[:, :], na[:, :], THR_W, None, ALU.mult))
            done(nc.vector.tensor_scalar(thr[:, :], thr[:, :], na[:, :], None, ALU.mult))
            done(nc.vector.scalar_tensor_tensor(absw[:, :, :], W0r[:, :, :], -1.0, W0r[:, :, :], ALU.mult, ALU.max))
            for k in range(KC):
                done(nc.vector.tensor_scalar(absw[:, k, :], absw[:, k, :], thr[:, k:k + 1], flag[:, :],
                                             ALU.is_lt, ALU.mult))
            done(nc.vector.tensor_tensor(absw[:, :, :], absw[:, :, :], W0r[:, :, :], ALU.mult))
            done(nc.vector.tensor_tensor(g["Weff_T"][:, :, :], W0r[:, :, :], absw[:, :, :], ALU.subtract))

        @block.tensor
        def _(pe):
            pe.wait_ge(dve_done, at["sums"])
            for k in range(KC):
                last = nc.tensor.matmul(pn[:, k:k + 1], accr[:, k * P:(k + 1) * P], onesf[:, 0:1], start=True, stop=True)
            last.then_inc(pe_done, 1)
            pe.wait_ge(dve_done, at["norms"])
            nc.tensor.matmul(pn[:, KC:KC + 1], onesf[:, :], nk2[:, 0:1], start=True, stop=True).then_inc(pe_done, 1)

        @block.scalar
        def _(act):
            act.wait_ge(pe_done, 1)
            nc.scalar.activation(nk[:, :], pn[:, 0:KC], ACT.Sqrt).then_inc(act_done, 1)
            act.wait_ge(pe_done, 2)
            nc.scalar.activation(na[:, :], pn[:, KC:KC + 1], ACT.Sqrt).then_inc(act_done, 1)


def dense(nc, g):
    sb, ps, sm, N, PAIRS, REST, x = (g[n] for n in ("sb", "ps", "sm", "N", "PAIRS", "REST", "x"))
    PAIR = 2 * P
    RING = 4
    with ExitStack() as c:
        turns = Turns(RING, PAIRS + 1, 13, even=PAIRS)
        slots = range(RING)
        load_sem = [sm(f"nodes_loaded{s}", c) for s in slots]
        stored = {n: [sm(f"{n}_stored{s}", c) for s in slots] for n in ("x1", "x2", "x3", "x4")}
        V = Steps(sm("dense_vec", c), "q:10 u:5 nb:11 v1:5 v3:11 st0:2 st1:5 st3:11 ag0:2 ag1:5 ag3:11 x1:3 m2:6 x2:6 "
                                      "y2:6 x4:12")
        O = Steps(sm("dense_pool", c), "r0:3 r1:6 r2:7 r3:12 q2:10 v0:1 xa:10 sa:2")
        A = Steps(sm("dense_act", c), "e0:3 e1:6 e2:7 e3:12 ex:5 za:10 zb:10 x1T:4 n:10 sq:1 x3:7 x3T:8 rz0:9 rz1:9")
        M = Steps(sm("dense_mat", c), "t1:4 t3:8 gru0:9 h:4 gru1:9")
        t = {n: [sb(f"d_{n}{s}", [P, 2, D], F32, c) for s in range(places)]
             for places, names in ((RING, ("x", "v0", "x1", "x2", "x3", "x4")),
                                   (2, ("sq", "v1", "v3", "x1T", "ex", "u", "x3T", "q", "q2", "n", "za", "zb", "xa", "nb")))
             for n in names}
        rz = [sb(f"d_rz{s}", [P, 2, 2 * D], F32, c) for s in range(2)]
        st = [sb(f"d_st{s}", [P, 4, 2, 6], F32, c) for s in slots]
        mv = [sb(f"d_mv{s}", [P, 4, 2, 2], F32, c) for s in slots]
        ve = [sb(f"d_ve{s}", [P, 4, 2], F32, c) for s in slots]
        m2 = [sb(f"d_m2{s}", [P, 2, 2], F32, c) for s in slots]
        rs = [sb(f"d_rs{s}", [P, 4, 2], F32, c) for s in slots]
        pT1 = ps("d_pT1", [P, 2 * D], c)
        pT3 = ps("d_pT3", [P, 2 * D], c)
        pH = [ps(f"d_pH{i}", [P, 2, D], c) for i in range(2)]
        pRZ = [ps(f"d_pRZ{i}", [P, 2 * D], c) for i in range(2)]
        pN = [ps(f"d_pN{i}", [P, 2, D], c) for i in range(2)]

        def size(i):
            return (REST, 1) if i.fixed and i.number == PAIRS else (P, 2)

        def place(name, i):
            return t[name][i.slot % len(t[name])]

        def part(name, i):
            R, G = size(i)
            return place(name, i)[0:R, 0:G, :]

        def rows_of(a, i):
            if size(i)[1] == 1:
                return a[PAIRS * PAIR:N, :].rearrange("(p g) d -> p g d", g=1)
            return a[bass.ds(i.number * PAIR, PAIR), :].rearrange("(p g) d -> p g d", g=2)

        block = c.enter_context(nc.Block())

        @block.sync
        def _(sp):
            def turn(now):
                if i := now.back(0):
                    if old := i.back(RING):
                        sp.wait_ge(*O.at(old, "sa"))
                    sp.dma_start(part("x", i), rows_of(x, i)).then_inc(load_sem[i.slot], 16)
                for n, d, a in (("x1", 4, g["X1"]), ("x2", 7, g["X2"]), ("x3", 8, g["X3"]), ("x4", 13, g["out"])):
                    if i := now.back(d):
                        sp.wait_ge(*(A if n == "x3" else V).at(i, n))
                        sp.dma_start(rows_of(a, i), part(n, i)).then_inc(stored[n][i.slot], 16)
            turns.run(sp, turn)
            for n in stored:
                for s in slots:
                    sp.wait_ge(stored[n][s], 16 * len(range(s, PAIRS + 1, RING)))

        @block.vector
        def _(dve):
            def stats(i, l, frm):
                R, G = size(i)
                for j in range(G):
                    last = nc.vector.bn_stats(st[i.slot][0:R, l, j, :], place(frm, i)[0:R, j, :])
                last.then_inc(V.sem, 1)

            def moments(i, l):
                R, G = size(i)
                dve.wait_ge(*V.at(i, f"st{l}"))
                nc.vector.nop(nofuse=True)
                for j in range(G):
                    last = nc.vector.bn_aggr(mv[i.slot][0:R, l, j, :], st[i.slot][0:R, l, j, :])
                last.then_inc(V.sem, 1)

            def norm(i, l, into, frm):
                R, G = size(i)
                if old := i.back(RING):
                    dve.wait_ge(stored[into][i.slot], old.dma())
                dve.wait_ge(*O.at(i, f"r{l}"))
                for j in range(G):
                    last = nc.vector.tensor_scalar(place(into, i)[0:R, j, :], place(frm, i)[0:R, j, :],
                                                   mv[i.slot][0:R, l, j, 0:1], rs[i.slot][0:R, l, j:j + 1],
                                                   ALU.subtract, ALU.mult)
                last.then_inc(V.sem, 1)

            def turn(now):
                if i := now.back(10):
                    R, G = size(i)
                    dve.wait_ge(*A.at(i, "rz1"))
                    nc.vector.scalar_tensor_tensor(part("q", i), rz[i.slot % 2][0:R, 0:G, 0:D], 1.0,
                                                   pN[i.slot % 2][0:R, 0:G, :], ALU.add, ALU.mult).then_inc(V.sem, 1)
                if i := now.back(5):
                    R, G = size(i)
                    dve.wait_ge(*A.at(i, "ex"))
                    nc.vector.scalar_tensor_tensor(part("u", i), pH[i.slot % 2][0:R, 0:G, :], -1.0, part("x1", i),
                                                   ALU.max, ALU.add).then_inc(V.sem, 1)
                if i := now.back(11):
                    dve.wait_ge(*A.at(i, "n"))
                    nc.vector.tensor_tensor(part("nb", i), part("n", i), part("zb", i), ALU.mult).then_inc(V.sem, 1)
                if i := now.back(5):
                    dve.wait_ge(*V.at(i, "u"))
                    nc.vector.scalar_tensor_tensor(part("v1", i), part("ex", i), 1.0, part("u", i),
                                                   ALU.min, ALU.add).then_inc(V.sem, 1)
                if i := now.back(11):
                    dve.wait_ge(*V.at(i, "nb"))
                    dve.wait_ge(*O.at(i, "xa"))
                    nc.vector.tensor_tensor(part("v3", i), part("nb", i), part("xa", i), ALU.add).then_inc(V.sem, 1)
                if i := now.back(2):
                    dve.wait_ge(*O.at(i, "v0"))
                    stats(i, 0, "v0")
                if i := now.back(5):
                    dve.wait_ge(*V.at(i, "v1"))
                    stats(i, 1, "v1")
                if i := now.back(11):
                    dve.wait_ge(*V.at(i, "v3"))
                    stats(i, 3, "v3")
                if i := now.back(2):
                    moments(i, 0)
                if i := now.back(5):
                    moments(i, 1)
                if i := now.back(11):
                    moments(i, 3)
                if i := now.back(3):
                    norm(i, 0, "x1", "v0")
                if i := now.back(6):
                    R, G = size(i)
                    dve.wait_ge(*O.at(i, "r1"))
                    nc.vector.tensor_tensor(m2[i.slot][0:R, 0, 0:G], mv[i.slot][0:R, 1, 0:G, 1], rs[i.slot][0:R, 1, 0:G],
                                            ALU.mult).then_inc(V.sem, 1)
                    if old := i.back(RING):
                        dve.wait_ge(*A.at(old, "x3"))
                    norm(i, 1, "x2", "v1")
                    dve.wait_ge(*V.at(i, "m2"))
                    nc.vector.tensor_tensor(m2[i.slot][0:R, 1, 0:G], m2[i.slot][0:R, 0, 0:G], rs[i.slot][0:R, 1, 0:G],
                                            ALU.mult).then_inc(V.sem, 1)
                if i := now.back(12):
                    norm(i, 3, "x4", "v3")
            turns.run(dve, turn)

        @block.gpsimd
        def _(pool):
            def rstd(i, l):
                R, G = size(i)
                pool.wait_ge(*A.at(i, f"e{l}"))
                nc.gpsimd.tensor_tensor(rs[i.slot][0:R, l, 0:G], ve[i.slot][0:R, l, 0:G], g["mhalf"][0:R, 0:G],
                                        ALU.pow).then_inc(O.sem, 1)

            def row(name, i):
                R, G = size(i)
                return g[name][0:R, :].unsqueeze(1).to_broadcast([R, G, D])

            def turn(now):
                if i := now.back(3):
                    rstd(i, 0)
                if i := now.back(6):
                    rstd(i, 1)
                if i := now.back(7):
                    rstd(i, 2)
                if i := now.back(12):
                    rstd(i, 3)
                if i := now.back(10):
                    pool.wait_ge(*V.at(i, "q"))
                    nc.gpsimd.tensor_tensor(part("q2", i), part("q", i), row("bin_r", i), ALU.add).then_inc(O.sem, 1)
                if i := now.back(1):
                    pool.wait_ge(load_sem[i.slot], i.dma())
                    if old := i.back(RING):
                        pool.wait_ge(*V.at(old, "x1"))
                    nc.gpsimd.tensor_tensor(part("v0", i), part("x", i), row("b0e_r", i), ALU.add).then_inc(O.sem, 1)
                if i := now.back(10):
                    pool.wait_ge(*A.at(i, "za"))
                    nc.gpsimd.tensor_tensor(part("xa", i), part("x3", i), part("za", i), ALU.mult).then_inc(O.sem, 1)
                if i := now.back(2):
                    R, G = size(i)
                    pool.wait_ge(*A.at(i, "sq"))
                    if old := i.back(1):
                        pool.wait_ge(*O.at(old, "sa"))
                    total = g["sumsq"][0:R, 0:G, :]
                    nc.gpsimd.tensor_tensor(total, total, part("sq", i), ALU.add).then_inc(O.sem, 1)
            turns.run(pool, turn)

        @block.scalar
        def _(act):
            def copy_T(i, into, bank, step):
                R, G = size(i)
                W = G * KC * R
                act.wait_ge(*M.at(i, step))
                nc.scalar.activation(place(into, i)[:, :, :].rearrange("p a b -> p (a b)")[:, 0:W], bank[:, 0:W],
                                     ACT.Copy).then_inc(A.sem, 1)

            def eps(i, l):
                R, G = size(i)
                act.wait_ge(*V.at(i, f"ag{l}" if l != 2 else "y2"))
                variance = mv[i.slot][0:R, l, 0:G, 1] if l != 2 else m2[i.slot][0:R, 1, 0:G]
                nc.scalar.activation(ve[i.slot][0:R, l, 0:G], variance, ACT.Copy, bias=EPS).then_inc(A.sem, 1)

            def gates(i, j):
                R, G = size(i)
                if old := i.back(2):
                    act.wait_ge(*V.at(old, "q"))
                act.wait_ge(*M.at(i, f"gru{j}"))
                o = rz[i.slot % 2][0:R, j, :] if j < G else rz[i.slot % 2][0:R, j, 0:1]
                nc.scalar.activation(o, pRZ[min(j, G - 1)][0:R, 0:o.shape[-1]], ACT.Tanh, scale=0.5)\
                    .then_inc(A.sem, 1)

            def turn(now):
                if i := now.back(3):
                    eps(i, 0)
                if i := now.back(6):
                    eps(i, 1)
                if i := now.back(7):
                    eps(i, 2)
                if i := now.back(12):
                    eps(i, 3)
                if i := now.back(5):
                    R, G = size(i)
                    act.wait_ge(*M.at(i, "h"))
                    nc.scalar.activation(part("ex", i), pH[i.slot % 2][0:R, 0:G, :], ACT.Exp, bias=1.0)\
                        .then_inc(A.sem, 1)
                if i := now.back(10):
                    R, G = size(i)
                    gate = rz[i.slot % 2][0:R, 0:G, D:2 * D]
                    act.wait_ge(*A.at(i, "rz1"))
                    nc.scalar.activation(part("za", i), gate, ACT.Copy, scale=0.5, bias=1.5).then_inc(A.sem, 1)
                    nc.scalar.activation(part("zb", i), gate, ACT.Copy, scale=-0.5, bias=0.5).then_inc(A.sem, 1)
                if i := now.back(4):
                    copy_T(i, "x1T", pT1, "t1")
                if i := now.back(10):
                    act.wait_ge(*O.at(i, "q2"))
                    nc.scalar.activation(part("n", i), part("q2", i), ACT.Tanh).then_inc(A.sem, 1)
                if i := now.back(1):
                    act.wait_ge(load_sem[i.slot], i.dma())
                    if old := i.back(2):
                        act.wait_ge(*O.at(old, "sa"))
                    nc.scalar.activation(part("sq", i), part("x", i), ACT.Square).then_inc(A.sem, 1)
                if i := now.back(7):
                    R, G = size(i)
                    act.wait_ge(*V.at(i, "x2"))
                    act.wait_ge(*O.at(i, "r2"))
                    if old := i.back(RING):
                        act.wait_ge(stored["x3"][i.slot], old.dma())
                        act.wait_ge(*O.at(old, "xa"))
                    for j in range(G):
                        last = nc.scalar.activation(place("x3", i)[0:R, j, :], place("x2", i)[0:R, j, :], ACT.Copy,
                                                    scale=rs[i.slot][0:R, 2, j:j + 1])
                    last.then_inc(A.sem, 1)
                if i := now.back(8):
                    copy_T(i, "x3T", pT3, "t3")
                if i := now.back(9):
                    gates(i, 0)
                    gates(i, 1)
            turns.run(act, turn)

        @block.tensor
        def _(pe):
            def flip(i, frm, bank):
                R, G = size(i)
                for j in range(G):
                    for k in range(KC):
                        o = (j * KC + k) * R
                        last = nc.tensor.transpose(bank[:, o:o + R], place(frm, i)[0:R, j, k * P:(k + 1) * P],
                                                   g["ident"][0:R, 0:R])
                last.then_inc(M.sem, 1)

            def lhs(name, i, j, k):
                R, G = size(i)
                o = (j * KC + k) * R
                return place(name, i)[:, :, :].rearrange("p a b -> p (a b)")[:, o:o + R]

            def gru(i, j):
                R, G = size(i)
                pe.wait_ge(*A.at(i, "x3T"))
                if old := i.back(2):
                    pe.wait_ge(*V.at(old, "q"))
                if j < G:
                    if old := i.back(1):
                        pe.wait_ge(*A.at(old, f"rz{j}"))
                    terms = [(g["ones_b"][:, 0:R], g["bias3"][:, :])]
                    terms += [(lhs("x3T", i, j, k), g["whhT"][:, k, :]) for k in range(KC)]
                    for o, lo, hi in ((pRZ[j][0:R, :], 0, 2 * D), (pN[i.slot % 2][0:R, j, :], 2 * D, 3 * D)):
                        for n, (l, r) in enumerate(terms):
                            last = nc.tensor.matmul(o, l, r[:, lo:hi], start=(n == 0), stop=(n == KC))
                else:
                    last = nc.tensor.matmul(pN[i.slot % 2][0:R, j, 0:1], g["ones_b"][:, 0:R],
                                            g["bias3"][:, 0:1], start=True, stop=True)
                last.then_inc(M.sem, 1)

            def turn(now):
                if i := now.back(4):
                    pe.wait_ge(*V.at(i, "x1"))
                    if old := i.back(1):
                        pe.wait_ge(*A.at(old, "x1T"))
                    flip(i, "x1", pT1)
                if i := now.back(8):
                    pe.wait_ge(*A.at(i, "x3"))
                    if old := i.back(1):
                        pe.wait_ge(*A.at(old, "x3T"))
                    flip(i, "x3", pT3)
                if i := now.back(9):
                    gru(i, 0)
                if i := now.back(4):
                    R, G = size(i)
                    pe.wait_ge(*A.at(i, "x1T"))
                    if old := i.back(2):
                        pe.wait_ge(*V.at(old, "u"))
                    for j in range(G):
                        nc.tensor.matmul(pH[i.slot % 2][0:R, j, :], g["ones_b"][:, 0:R], g["bias1"][:, :],
                                         start=True, stop=False)
                        for k in range(KC):
                            last = nc.tensor.matmul(pH[i.slot % 2][0:R, j, :], lhs("x1T", i, j, k),
                                                    g["W1x"][:, k, 0:D], start=False, stop=(k == KC - 1))
                    last.then_inc(M.sem, 1)
                if i := now.back(9):
                    gru(i, 1)
            turns.run(pe, turn)


def edge_norms(nc, g):
    sb, ps, sm, NB, L, x = (g[n] for n in ("sb", "ps", "sm", "NB", "L", "x"))
    RING = 8
    with ExitStack() as c:
        slots = range(RING)
        turns = Turns(RING, NB, 6)
        M = Steps(sm("norms_mat", c), "t:4 h:5")
        A = Steps(sm("norms_act", c), "T:4 msg:6 sq:6 ix:0")
        V = Steps(sm("norms_vec", c), "lk:0")
        gathered = g["queue_sems"]("norms_src_in")
        stored = [sm(f"n_stored{s}", c) for s in slots]
        lock_loaded = sm("lock_loaded", c)
        ready = sm("n_ready", c)
        lock_i = sb("lock_i", [P, L], I32, c)
        lock_f = sb("lock_f", [P, L], F32, c)
        hit = [sb(f"hit{s}", [P, L], F32, c) for s in range(2)]
        lockc = sb("lockc", [P, NB], F32, c)
        n2 = sb("n2", [P, NB], F32, c)
        tiles = lambda n, shape, dt=F32: [sb(f"n_{n}{s}", shape, dt, c) for s in slots]
        ix, Xs, XT, msg, msq = tiles("ix", [P, 1], I32), tiles("Xs", [P, D]), tiles("XT", [P, KC, P]), \
            tiles("msg", [P, D]), tiles("msq", [P, D])
        pT = [ps(f"n_pT{i}", [P, KC, P], c) for i in range(2)]
        pH = [ps(f"n_pH{i}", [P, D], c) for i in range(2)]
        with nc.Block() as block:
            @block.gpsimd
            def _(pool):
                def turn(now):
                    if i := now.back(1):
                        if old := i.back(RING):
                            pool.wait_ge(*M.at(old, "t"))
                        pool.wait_ge(*A.at(i, "ix"))
                        nc.gpsimd.nop(nofuse=True)
                        nc.gpsimd.indirect_dma_start(
                            out=Xs[i.slot][:, :], out_offset=None, in_=x[:, :],
                            in_offset=bass.IndirectOffsetOnAxis(ap=ix[i.slot][:, 0:1], axis=0))\
                            .then_inc(gathered[i.slot], 16)
                turns.run(pool, turn)

            @block.tensor
            def _(pe):
                def turn(now):
                    if i := now.back(4):
                        pe.wait_ge(gathered[i.slot], i.dma())
                        if old := i.back(2):
                            pe.wait_ge(*A.at(old, "T"))
                        for j in range(KC):
                            last = nc.tensor.transpose(pT[i.slot % 2][:, j, :], Xs[i.slot][:, j * P:(j + 1) * P],
                                                       g["ident"][:, :])
                        last.then_inc(M.sem, 1)
                    if i := now.back(5):
                        pe.wait_ge(*A.at(i, "T"))
                        if old := i.back(2):
                            pe.wait_ge(*A.at(old, "msg"))
                        for j in range(KC):
                            last = nc.tensor.matmul(pH[i.slot % 2][:, :], XT[i.slot][:, j, :], g["Weff_T"][:, j, :],
                                                    start=(j == 0), stop=(j == KC - 1))
                        last.then_inc(M.sem, 1)
                turns.run(pe, turn)

            @block.scalar
            def _(act):
                def turn(now):
                    if i := now.back(4):
                        act.wait_ge(*M.at(i, "t"))
                        nc.scalar.activation(XT[i.slot][:, :, :], pT[i.slot % 2][:, :, :], ACT.Copy).then_inc(A.sem, 1)
                    if i := now.back(6):
                        act.wait_ge(*M.at(i, "h"))
                        if old := i.back(RING):
                            act.wait_ge(stored[i.slot], old.dma())
                        nc.scalar.activation(msg[i.slot][:, :], pH[i.slot % 2][:, :], ACT.Copy,
                                             scale=g["w_e"][:, bass.ds(i.number, 1)]).then_inc(A.sem, 1)
                        act.wait_ge(*A.at(i, "msg"))
                        nc.scalar.activation(msq[i.slot][:, :], msg[i.slot][:, :], ACT.Square,
                                             accum_out=n2[:, bass.ds(i.number, 1)]).then_inc(A.sem, 1)
                    if i := now.back(0):
                        if old := i.back(RING):
                            act.wait_ge(gathered[i.slot], old.dma())
                        nc.scalar.activation(ix[i.slot][:, :], g["src_i"][:, bass.ds(i.number, 1)], ACT.Copy)\
                            .then_inc(A.sem, 1)
                turns.run(act, turn)

            @block.sync
            def _(sp):
                sp.dma_start(lock_i[:, :], bcast_rows(g["node_lock"], P, L)).then_inc(lock_loaded, 16)

                def turn(now):
                    if i := now.back(6):
                        sp.wait_ge(*A.at(i, "msg"))
                        sp.dma_start(g["MSG"][bass.ds(i.number * P, P), :], msg[i.slot][:, :])\
                            .then_inc(stored[i.slot], 16)
                turns.run(sp, turn)
                for s in slots:
                    sp.wait_ge(stored[s], 16 * len(range(s, NB, RING)))

            @block.vector
            def _(dve):
                dve.wait_ge(lock_loaded, 16)
                nc.vector.tensor_copy(lock_f[:, :], lock_i[:, :]).then_inc(ready, 1)
                dve.wait_ge(ready, 1)

                def turn(now):
                    if i := now.back(0):
                        if old := i.back(2):
                            dve.wait_ge(*V.at(old, "lk"))
                        nc.vector.tensor_scalar(hit[i.slot % 2][:, :], lock_f[:, :], g["dst_f"][:, bass.ds(i.number, 1)],
                                                0.0, ALU.is_equal, ALU.add, accum_out=lockc[:, bass.ds(i.number, 1)])\
                            .then_inc(V.sem, 1)
                turns.run(dve, turn)

        tot = sb("n_tot", [P, 1], F32, c)
        thr = sb("n_thr", [P, 1], F32, c)
        norm = sb("n_norm", [P, NB], F32, c)
        m0 = sb("n_m0", [P, NB], F32, c)
        m1 = sb("n_m1", [P, NB], F32, c)
        lk = sb("n_lk", [P, NB], F32, c)
        eq = sb("n_eq", [P, NB], F32, c)
        onesf = sb("n_ones", [P, P], F32, c)
        pX = ps("n_pX", [P, 1], c)
        sqrt_done, dve_done, total_done = sm("sqrt_done", c), sm("keep_dve", c), sm("total_done", c)
        with nc.Block() as block:
            @block.scalar
            def _(act):
                nc.scalar.activation(norm[:, :], n2[:, :], ACT.Sqrt).then_inc(sqrt_done, 1)

            @block.tensor
            def _(pe):
                pe.wait_ge(dve_done, 2)
                nc.tensor.matmul(pX[:, :], onesf[:, :], tot[:, :], start=True, stop=True).then_inc(total_done, 1)

            @block.vector
            def _(dve):
                count = [0]

                def done(ins):
                    count[0] += 1
                    ins.then_inc(dve_done, 1)
                    dve.wait_ge(dve_done, count[0])

                done(nc.vector.memset(onesf[:, :], 1.0))
                dve.wait_ge(sqrt_done, 1)
                done(nc.vector.tensor_reduce(tot[:, :], norm[:, :], AX.X, ALU.add))
                dve.wait_ge(total_done, 1)
                done(nc.vector.tensor_scalar(thr[:, :], pX[:, :], 1.0 / g["NEDGE"], THR_A, ALU.mult, ALU.mult))
                nc.vector.tensor_tensor(eq[:, :], g["src_f"][:, :], g["dst_f"][:, :], ALU.is_equal)
                nc.vector.tensor_scalar(lk[:, :], lockc[:, :], 0.5, None, ALU.is_gt)
                done(nc.vector.tensor_scalar(m0[:, :], norm[:, :], thr[:, :], None, ALU.is_lt))
                done(nc.vector.tensor_scalar(m1[:, :], m0[:, :], -1.0, 1.0, ALU.mult, ALU.add))
                done(nc.vector.tensor_tensor(lk[:, :], lk[:, :], eq[:, :], ALU.max))
                done(nc.vector.tensor_tensor(g["keep"][:, :], m1[:, :], lk[:, :], ALU.max))


class EdgePass:

    RING = 8

    def __init__(self, nc, g, c, name, longest, vec, pool, mat, act, table, into):
        self.nc, self.g, self.c, self.name, self.table, self.into = nc, g, c, name, table, into
        self.NB, self.N = g["NB"], g["N"]
        self.turns = Turns(self.RING, self.NB, longest)
        self.slots = range(self.RING)
        self.V, self.O, self.M, self.A = (Steps(g["sm"](f"{name}_{e}", c), plan)
                                          for e, plan in (("vec", vec), ("pool", pool), ("mat", mat), ("act", act)))
        self.Xd = self.tiles("Xd", [P, D])
        self.v = self.tiles("v", [P, D])
        self.xn = self.tiles("xn", [P, D])
        self.st = self.tiles("st", [P, 6])
        self.mv = self.tiles("mv", [P, 2])
        self.ve = self.tiles("ve", [P, 1])
        self.rs = self.tiles("rs", [P, 1])
        self.dc = self.tiles("dc", [P, P], I32)
        self.eq = self.tiles("eq", [P, P])
        self.ixs = self.tiles("ixs", [P, 1], I32)
        self.ixd = self.tiles("ixd", [P, 1], I32)
        self.ixp = self.tiles("ixp", [P, 1], I32)
        self.src_in, self.dst_in, self.put_out = (g["queue_sems"](f"{name}_{n}") for n in ("src_in", "dst_in", "put_out"))
        self.cols_in = [g["sm"](f"{name}_cols_in{s}", c) for s in self.slots]

    def tiles(self, n, shape, dt=F32, count=None):
        return [self.g["sb"](f"{self.name}_{n}{s}", shape, dt, self.c) for s in range(count or self.RING)]

    def banks(self, n, shape, count):
        return [self.g["ps"](f"{self.name}_{n}{i}", shape, self.c) for i in range(count)]

    def gather(self, pool, i, ix, index, into, sem, table=None):
        nc = self.nc
        pool.wait_ge(*self.A.at(i, index))
        nc.gpsimd.nop(nofuse=True)
        nc.gpsimd.indirect_dma_start(out=into, out_offset=None, in_=(self.table if table is None else table)[:, :],
                                     in_offset=bass.IndirectOffsetOnAxis(ap=ix[i.slot][:, 0:1], axis=0))\
            .then_inc(sem[i.slot], 16)

    def indices(self, act, i, ix, index, sem):
        if old := i.back(self.RING):
            act.wait_ge(sem[i.slot], old.dma())
        self.nc.scalar.activation(ix[i.slot][:, :], self.g[index][:, bass.ds(i.number, 1)], ACT.Copy)\
            .then_inc(self.A.sem, 1)

    def indices_in(self, act, i):
        self.indices(act, i, self.ixs, "src_i", self.src_in)
        self.indices(act, i, self.ixd, "dst_i", self.dst_in)

    def indices_out(self, act, i):
        self.indices(act, i, self.ixp, "put_i", self.put_out)

    def gather_dst(self, pool, i):
        if old := i.back(self.RING):
            pool.wait_ge(*self.V.at(old, "v"))
        self.gather(pool, i, self.ixd, "dst_i", self.Xd[i.slot][:, :], self.dst_in)

    def scatter(self, pool, i):
        nc = self.nc
        pool.wait_ge(*self.A.at(i, "put_i"))
        pool.wait_ge(*self.V.at(i, "xn"))
        nc.gpsimd.nop(nofuse=True)
        nc.gpsimd.indirect_dma_start(out=self.into[:, :],
                                     out_offset=bass.IndirectOffsetOnAxis(ap=self.ixp[i.slot][:, 0:1], axis=0),
                                     in_=self.xn[i.slot][:, :], in_offset=None, bounds_check=self.N - 1,
                                     oob_is_err=False).then_inc(self.put_out[i.slot], 16)

    def rstd(self, pool, i):
        nc, s = self.nc, i.slot
        pool.wait_ge(*self.A.at(i, "e"))
        nc.gpsimd.tensor_tensor(self.rs[s][:, :], self.ve[s][:, :], self.g["mhalf"][:, 0:1], ALU.pow)\
            .then_inc(self.O.sem, 1)

    def eps(self, act, i):
        act.wait_ge(*self.V.at(i, "ag"))
        self.nc.scalar.activation(self.ve[i.slot][:, :], self.mv[i.slot][:, 1:2], ACT.Copy, bias=EPS)\
            .then_inc(self.A.sem, 1)

    def stats(self, dve, i):
        nc, V, s = self.nc, self.V, i.slot
        dve.wait_ge(*V.at(i, "v"))
        nc.vector.bn_stats(self.st[s][:, :], self.v[s][:, :]).then_inc(V.sem, 1)

    def moments(self, dve, i):
        nc, V, s = self.nc, self.V, i.slot
        dve.wait_ge(*V.at(i, "st"))
        nc.vector.nop(nofuse=True)
        nc.vector.bn_aggr(self.mv[s][:, :], self.st[s][:, :]).then_inc(V.sem, 1)

    def normalise(self, dve, i, scaler=None):
        s = i.slot
        dve.wait_ge(*(scaler or self.O).at(i, "r"))
        if old := i.back(self.RING):
            dve.wait_ge(self.put_out[s], old.dma())
        self.nc.vector.tensor_scalar(self.xn[s][:, :], self.v[s][:, :], self.mv[s][:, 0:1], self.rs[s][:, :],
                                     ALU.subtract, ALU.mult).then_inc(self.V.sem, 1)

    def same_target(self, dve, i, scale=None):
        dve.wait_ge(self.cols_in[i.slot], i.dma())
        self.nc.vector.tensor_scalar(self.eq[i.slot][:, :], self.dc[i.slot][:, :],
                                     self.g["dst_f"][:, bass.ds(i.number, 1)], scale, ALU.is_equal,
                                     *([ALU.mult] if scale is not None else [])).then_inc(self.V.sem, 1)

    def load_cols(self, sp, i):
        a = self.g["dst_cols"][bass.ds(i.number, 1), :]
        sp.dma_start(self.dc[i.slot][:, :], a.to_broadcast([P, P])).then_inc(self.cols_in[i.slot], 16)

    def wait_out(self, sp):
        for s in self.slots:
            sp.wait_ge(self.put_out[s], 16 * len(range(s, self.NB, self.RING)))


def edge_sum(nc, g):
    with ExitStack() as c:
        E = EdgePass(nc, g, c, "sum", 6, "eq:1 cy:2 v:3 r:4 st:3 xn:4 ag:3", "", "ag:2",
                     "dst_i:0 put_i:4 e:3 sd:3",
                     g["x"], g["X1"])
        V, O, M, RING = E.V, E.O, E.M, E.RING
        m = E.tiles("m", [P, D])
        sd = E.tiles("sd", [P, 1])
        m_in = [g["sm"](f"sum_m_in{s}", c) for s in E.slots]
        pA = E.banks("pA", [P, D], 2)
        with nc.Block() as block:
            @block.sync
            def _(sp):
                def turn(now):
                    if i := now.back(0):
                        if old := i.back(RING):
                            sp.wait_ge(*M.at(old, "ag"))
                        sp.dma_start(m[i.slot][:, :], g["MSG"][bass.ds(i.number * P, P), :]).then_inc(m_in[i.slot], 16)
                        E.load_cols(sp, i)
                E.turns.run(sp, turn)
                E.wait_out(sp)

            @block.gpsimd
            def _(pool):
                def turn(now):
                    if i := now.back(1):
                        E.gather_dst(pool, i)
                    if i := now.back(5):
                        E.scatter(pool, i)
                E.turns.run(pool, turn)

            @block.scalar
            def _(act):
                def turn(now):
                    if i := now.back(0):
                        E.indices(act, i, E.ixd, "dst_i", E.dst_in)
                    if i := now.back(4):
                        E.indices_out(act, i)
                    if i := now.back(3):
                        E.eps(act, i)
                        act.wait_ge(*E.A.at(i, "e"))
                        nc.scalar.activation(sd[i.slot][:, :], E.ve[i.slot][:, :], ACT.Sqrt).then_inc(E.A.sem, 1)
                E.turns.run(act, turn)

            @block.tensor
            def _(pe):
                def turn(now):
                    if i := now.back(2):
                        pe.wait_ge(*V.at(i, "cy"))
                        if old := i.back(2):
                            pe.wait_ge(*V.at(old, "v"))
                        nc.tensor.matmul(pA[i.slot % 2][:, :], g["ones_next"][:, :], g["bias0"][:, :],
                                         start=True, stop=False)
                        nc.tensor.matmul(pA[i.slot % 2][:, :], E.eq[i.slot][:, :], m[i.slot][:, :],
                                         start=False, stop=True).then_inc(M.sem, 1)
                E.turns.run(pe, turn)

            @block.vector
            def _(dve):
                def turn(now):
                    if i := now.back(1):
                        E.same_target(dve, i, g["keep"][:, bass.ds(i.number, 1)])
                    if i := now.back(2):
                        dve.wait_ge(m_in[i.slot], i.dma())
                        if prev := i.back(1):
                            dve.wait_ge(*M.at(prev, "ag"))
                            nc.vector.tensor_copy(m[i.slot][0:1, :], pA[prev.slot % 2][0:1, :]).then_inc(V.sem, 1)
                        else:
                            nc.vector.memset(m[i.slot][0:1, :], 0.0).then_inc(V.sem, 1)
                    if i := now.back(3):
                        dve.wait_ge(*M.at(i, "ag"))
                        dve.wait_ge(E.dst_in[i.slot], i.dma())
                        nc.vector.tensor_tensor(E.v[i.slot][:, :], pA[i.slot % 2][:, :], E.Xd[i.slot][:, :], ALU.add)\
                            .then_inc(V.sem, 1)
                    if i := now.back(4):
                        dve.wait_ge(*E.A.at(i, "sd"))
                        nc.vector.reciprocal(E.rs[i.slot][:, :], sd[i.slot][:, :]).then_inc(V.sem, 1)
                    if i := now.back(3):
                        E.stats(dve, i)
                    if i := now.back(4):
                        E.normalise(dve, i, V)
                    if i := now.back(3):
                        E.moments(dve, i)
                E.turns.run(dve, turn)


class SegmentMax:

    def __init__(self, E, H, own):
        self.E, self.H, self.own = E, H, own
        self.dv = E.tiles("dv", [H, P], I32)
        self.prev_in = [E.g["sm"](f"{E.name}_prev_in{s}", E.c) for s in E.slots]
        self.ne = E.tiles("ne", [H, P], count=2)
        self.kl = E.tiles("kl", [H, P + 1])
        self.LT = E.tiles("LT", [H, 2 * P], count=2)
        self.F = E.tiles("F", [H, P], count=2)
        self.B = E.tiles("B", [H, P], count=2)
        self.m = E.tiles("m", [H, P], count=2) if own else self.B
        self.dl = E.tiles("dl", [H, 2 * P], count=4)
        self.ET = E.tiles("ET", [H, 2 * P], count=4)

    def load(self, sp, i):
        a = self.E.g["dst_prev"][bass.ds(i.number, 1), :]
        sp.dma_start(self.dv[i.slot][:, :], a.to_broadcast([self.H, P])).then_inc(self.prev_in[i.slot], 16)

    def start(self, nc, done):
        for a in self.kl:
            done(nc.vector.memset(a[:, P:P + 1], NONE))
        for a in self.dl:
            done(nc.vector.memset(a[:, :], 0.0))
        done(nc.vector.memset(self.m[1][:, :], NONE))

    def breaks(self, dve, i):
        nc, V, H, s = self.E.nc, self.E.V, self.H, i.slot
        dve.wait_ge(self.prev_in[s], i.dma())
        dve.wait_ge(self.E.cols_in[s], i.dma())
        if old := i.back(2):
            dve.wait_ge(*self.E.A.at(old, "kl"))
        nc.vector.tensor_tensor(self.ne[s % 2][:, :], self.dv[s][:, :], self.E.dc[s][0:H, :], ALU.not_equal)\
            .then_inc(V.sem, 1)

    def scores(self, act, i, bank):
        act.wait_ge(*self.E.M.at(i, "lt"))
        if old := i.back(2):
            act.wait_ge(*self.E.V.at(old, "dl"))
        self.E.nc.scalar.activation(self.LT[i.slot % 2][:, 0:bank.shape[-1]], bank[:, :], ACT.Copy)\
            .then_inc(self.E.A.sem, 1)

    def kills(self, act, i):
        act.wait_ge(*self.E.V.at(i, "ne"))
        if old := i.back(self.E.RING):
            act.wait_ge(*self.E.V.at(old, "bw"))
        self.E.nc.scalar.activation(self.kl[i.slot][:, 0:P], self.ne[i.slot % 2][:, :], ACT.Copy, scale=NONE)\
            .then_inc(self.E.A.sem, 1)

    def before(self, i):
        return self.m[(i.slot - 1) % 2][:, P - 1:P]

    def forwards(self, dve, i):
        s = i.slot
        kl, F, LT = self.kl[s], self.F[s % 2], self.LT[s % 2]
        dve.wait_ge(*self.E.A.at(i, "LT"))
        dve.wait_ge(*self.E.A.at(i, "kl"))
        self.E.nc.vector.tensor_tensor_scan(F[:, 1:P], kl[:, 1:P], LT[:, 1:P], self.before(i), ALU.add, ALU.max)\
            .then_inc(self.E.V.sem, 1)

    def backwards(self, dve, i):
        s = i.slot
        kl, F, B = self.kl[s], self.F[s % 2], self.B[s % 2]
        dve.wait_ge(*self.E.V.at(i, "fw"))
        self.E.nc.vector.tensor_tensor_scan(B[:, P - 1:0:-1], kl[:, P:1:-1], F[:, P - 1:0:-1], NONE, ALU.add, ALU.max)\
            .then_inc(self.E.V.sem, 1)

    def with_own(self, dve, i):
        s = i.slot
        dve.wait_ge(*self.E.V.at(i, "bw"))
        self.E.nc.vector.tensor_tensor(self.m[s % 2][:, 1:P], self.B[s % 2][:, 1:P], self.LT[s % 2][:, P + 1:2 * P],
                                       ALU.max).then_inc(self.E.V.sem, 1)

    def shift(self, dve, i):
        nc, s = self.E.nc, i.slot
        m, LT, dl = self.m[s % 2], self.LT[s % 2], self.dl[s % 4]
        dve.wait_ge(*self.E.V.at(i, "mx" if self.own else "bw"))
        if self.own:
            nc.vector.tensor_tensor(dl[:, P + 1:2 * P], LT[:, P + 1:2 * P], m[:, 1:P], ALU.subtract)
        nc.vector.tensor_tensor(dl[:, 1:P], LT[:, 1:P], m[:, 1:P], ALU.subtract)
        nc.vector.tensor_scalar(dl[:, 0:1], self.before(i), m[:, 1:2], 0.0, ALU.subtract, ALU.min)\
            .then_inc(self.E.V.sem, 1)


def edge_heads(nc, g):
    with ExitStack() as c:
        E = EdgePass(nc, g, c, "heads", 9,
                     "lg:4 t2:6 de:6 lr:4 rd:6 x:5 t3:6 hw:5 xn:8 fw:4 cy:5 u:7 bw:4 v:7 mx:4 st:7 dl:4 ag:7 "
                     "eq:3 ne:3",
                     "t4:7 t1:5 r:7",
                     "t:3 xr:5 lt:4 hs:3 hd:3 ag:5",
                     "T:3 kl:4 LT:4 src_i:0 dst_i:0 put_i:8 ex:7 hx:3 hd:3 ET:4 e:7",
                     g["X1"], g["X2"])
        V, O, M, A, RING = E.V, E.O, E.M, E.A, E.RING
        W = HID + 1
        SM = SegmentMax(E, HEADS, True)
        Xs = E.tiles("Xs", [P, D], count=4)
        XT = E.tiles("XT", [P, 2 * KC, P], count=2)
        Hx = E.tiles("Hx", [P, HEADS, W], count=4)
        Hw = E.tiles("Hw", [P, HEADS, W], count=2)
        Hd = E.tiles("Hd", [P, D + 2 * HEADS], count=4)
        as_ = E.tiles("as", [P, HEADS])
        lg = E.tiles("lg", [P, 2, HEADS])
        lr = E.tiles("lr", [P, 2, HEADS])
        xw = E.tiles("xw", [P, 2, HEADS])
        t1, t2, t3, t4, ex, u = (E.tiles(n, [P, D], count=2) for n in ("t1", "t2", "t3", "t4", "ex", "u"))
        de = E.tiles("de", [P, HEADS])
        rd = E.tiles("rd", [P, HEADS])
        started = g["sm"]("heads_started", c)
        pT = E.banks("pT", [P, 2 * KC, P], 1)[0]
        pHs = E.banks("pHs", [P, D + HEADS], 1)[0]
        pHd = E.banks("pHd", [P, D + 2 * HEADS], 1)[0]
        pA = E.banks("pA", [P, HEADS, W], 2)
        pS = E.banks("pS", [HEADS, 2 * P], 1)[0]
        pX = E.banks("pX", [P, 2 * HEADS], 1)[0]
        head = lambda a: a.rearrange("p (h c) -> p h c", h=HEADS)
        per_head = lambda a, n: a.unsqueeze(2).to_broadcast([a.shape[0], HEADS, n])
        start_count = []

        with nc.Block() as block:
            @block.sync
            def _(sp):
                def turn(now):
                    if i := now.back(0):
                        if old := i.back(RING):
                            sp.wait_ge(*V.at(old, "ne"))
                        E.load_cols(sp, i)
                        SM.load(sp, i)
                E.turns.run(sp, turn)
                E.wait_out(sp)

            @block.gpsimd
            def _(pool):
                def turn(now):
                    if i := now.back(7):
                        pool.wait_ge(*V.at(i, "t3"))
                        nc.gpsimd.tensor_tensor(t4[i.slot % 2][:, :], t3[i.slot % 2][:, :], g["b1m1_r"][:, :], ALU.add)\
                            .then_inc(O.sem, 1)
                    if i := now.back(1):
                        E.gather_dst(pool, i)
                        if old := i.back(4):
                            pool.wait_ge(*M.at(old, "t"))
                        E.gather(pool, i, E.ixs, "src_i", Xs[i.slot % 4][:, :], E.src_in)
                    if i := now.back(5):
                        pool.wait_ge(*V.at(i, "x"))
                        nc.gpsimd.tensor_tensor(head(t1[i.slot % 2][:, :]), head(Hd[i.slot % 4][:, 0:D]),
                                                per_head(xw[i.slot][:, 1, :], HID), ALU.mult).then_inc(O.sem, 1)
                    if i := now.back(9):
                        E.scatter(pool, i)
                    if i := now.back(7):
                        E.rstd(pool, i)
                E.turns.run(pool, turn)

            @block.vector
            def _(dve):
                count = [0]

                def done(ins):
                    count[0] += 1
                    ins.then_inc(started, 1)
                    dve.wait_ge(started, count[0])

                SM.start(nc, done)
                for a in Hx:
                    done(nc.vector.memset(a[:, :, :], 1.0))
                start_count.append(count[0])

                def turn(now):
                    if i := now.back(4):
                        s, h = i.slot, Hd[i.slot % 4]
                        dve.wait_ge(*A.at(i, "hd"))
                        nc.vector.tensor_tensor(lg[s][:, 0, :], as_[s][:, :], h[:, D + HEADS:D + 2 * HEADS], ALU.add)
                        nc.vector.tensor_tensor(lg[s][:, 1, :], h[:, D:D + HEADS], h[:, D + HEADS:D + 2 * HEADS],
                                                ALU.add).then_inc(V.sem, 1)
                    if i := now.back(6):
                        s = i.slot
                        dve.wait_ge(*M.at(i, "ag"))
                        dve.wait_ge(*O.at(i, "t1"))
                        nc.vector.tensor_tensor(head(t2[s % 2][:, :]), pA[s % 2][:, :, 0:HID], head(t1[s % 2][:, :]),
                                                ALU.add).then_inc(V.sem, 1)
                        nc.vector.scalar_tensor_tensor(de[s][:, :], pA[s % 2][:, :, HID], 1e-16, xw[s][:, 1, :],
                                                       ALU.add, ALU.add).then_inc(V.sem, 1)
                    if i := now.back(4):
                        s = i.slot
                        dve.wait_ge(*V.at(i, "lg"))
                        nc.vector.scalar_tensor_tensor(lr[s][:, :, :], lg[s][:, :, :], SLOPE, lg[s][:, :, :],
                                                       ALU.mult, ALU.max).then_inc(V.sem, 1)
                    if i := now.back(6):
                        s = i.slot
                        dve.wait_ge(*V.at(i, "de"))
                        nc.vector.reciprocal(rd[s][:, :], de[s][:, :]).then_inc(V.sem, 1)
                    if i := now.back(5):
                        s = i.slot
                        dve.wait_ge(*M.at(i, "xr"))
                        nc.vector.tensor_copy(xw[s][:, :, :].rearrange("p a h -> p (a h)"), pX[:, :]).then_inc(V.sem, 1)
                    if i := now.back(6):
                        s = i.slot
                        dve.wait_ge(*V.at(i, "rd"))
                        nc.vector.tensor_tensor(head(t3[s % 2][:, :]), head(t2[s % 2][:, :]), per_head(rd[s][:, :], HID),
                                                ALU.mult).then_inc(V.sem, 1)
                    if i := now.back(5):
                        s = i.slot
                        dve.wait_ge(*V.at(i, "x"))
                        nc.vector.tensor_tensor(Hw[s % 2][:, :, :], Hx[s % 4][:, :, :], per_head(xw[s][:, 0, :], W),
                                                ALU.mult).then_inc(V.sem, 1)
                    if i := now.back(4):
                        SM.forwards(dve, i)
                    if i := now.back(8):
                        E.normalise(dve, i)
                    if i := now.back(5):
                        s = i.slot
                        if prev := i.back(1):
                            dve.wait_ge(*V.at(i, "hw"))
                            dve.wait_ge(*M.at(prev, "ag"))
                            nc.vector.tensor_tensor(Hw[s % 2][0:1, :, :], pA[prev.slot % 2][0:1, :, :],
                                                    per_head(xw[s][0:1, 0, :], W), ALU.mult).then_inc(V.sem, 1)
                        else:
                            dve.wait_ge(*V.at(i, "hw"))
                            nc.vector.memset(Hw[s % 2][0:1, :, :], 0.0).then_inc(V.sem, 1)
                    if i := now.back(7):
                        s = i.slot
                        dve.wait_ge(*O.at(i, "t4"))
                        nc.vector.scalar_tensor_tensor(u[s % 2][:, :], t4[s % 2][:, :], -1.0, E.Xd[s][:, :],
                                                       ALU.max, ALU.add).then_inc(V.sem, 1)
                    if i := now.back(4):
                        SM.backwards(dve, i)
                    if i := now.back(7):
                        s = i.slot
                        dve.wait_ge(*A.at(i, "ex"))
                        dve.wait_ge(*V.at(i, "u"))
                        nc.vector.scalar_tensor_tensor(E.v[s][:, :], ex[s % 2][:, :], 1.0, u[s % 2][:, :],
                                                       ALU.min, ALU.add).then_inc(V.sem, 1)
                    if i := now.back(4):
                        SM.with_own(dve, i)
                    if i := now.back(7):
                        E.stats(dve, i)
                    if i := now.back(4):
                        SM.shift(dve, i)
                    if i := now.back(7):
                        E.moments(dve, i)
                    if i := now.back(3):
                        E.same_target(dve, i)
                        SM.breaks(dve, i)
                E.turns.run(dve, turn)

            @block.tensor
            def _(pe):
                pe.wait_ge(started, start_count[0])

                def turn(now):
                    if i := now.back(3):
                        s = i.slot
                        pe.wait_ge(E.src_in[s], i.dma())
                        pe.wait_ge(E.dst_in[s], i.dma())
                        if old := i.back(1):
                            pe.wait_ge(*A.at(old, "T"))
                        for a, rows in enumerate((Xs[s % 4], E.Xd[s])):
                            for j in range(KC):
                                last = nc.tensor.transpose(pT[:, a * KC + j, :], rows[:, j * P:(j + 1) * P],
                                                           g["ident"][:, :])
                        last.then_inc(M.sem, 1)
                    if i := now.back(5):
                        pe.wait_ge(*A.at(i, "ET"))
                        if old := i.back(1):
                            pe.wait_ge(*V.at(old, "x"))
                        for a in range(2):
                            last = nc.tensor.matmul(pX[:, a * HEADS:(a + 1) * HEADS],
                                                    SM.ET[i.slot % 4][:, a * P:(a + 1) * P],
                                                    g["ident"][0:HEADS, 0:HEADS], start=True, stop=True)
                        last.then_inc(M.sem, 1)
                    if i := now.back(4):
                        pe.wait_ge(*V.at(i, "lr"))
                        if old := i.back(1):
                            pe.wait_ge(*A.at(old, "LT"))
                        for a in range(2):
                            last = nc.tensor.transpose(pS[:, a * P:(a + 1) * P], lr[i.slot][:, a, :], g["ident"][:, :])
                        last.then_inc(M.sem, 1)
                    if i := now.back(3):
                        s = i.slot
                        pe.wait_ge(*A.at(i, "T"))
                        if old := i.back(1):
                            pe.wait_ge(*A.at(old, "hd"))
                        for j in range(KC):
                            last = nc.tensor.matmul(pHs[:, :], XT[s % 2][:, j, :], g["W1x"][:, j, 0:D + HEADS],
                                                    start=(j == 0), stop=(j == KC - 1))
                        last.then_inc(M.sem, 1)
                        for j in range(KC):
                            last = nc.tensor.matmul(pHd[:, :], XT[s % 2][:, KC + j, :], g["W1x"][:, j, :],
                                                    start=(j == 0), stop=(j == KC - 1))
                        last.then_inc(M.sem, 1)
                    if i := now.back(5):
                        s = i.slot
                        pe.wait_ge(*V.at(i, "cy"))
                        if old := i.back(2):
                            pe.wait_ge(*V.at(old, "de"))
                        nc.tensor.matmul(pA[s % 2][:, :, :].rearrange("p h c -> p (h c)"), E.eq[s][:, :],
                                         Hw[s % 2][:, :, :].rearrange("p h c -> p (h c)"), start=True, stop=True)\
                            .then_inc(M.sem, 1)
                E.turns.run(pe, turn)

            @block.scalar
            def _(act):
                act.wait_ge(started, start_count[0])

                def turn(now):
                    if i := now.back(3):
                        act.wait_ge(*M.at(i, "t"))
                        nc.scalar.activation(XT[i.slot % 2][:, :, :], pT[:, :, :], ACT.Copy).then_inc(A.sem, 1)
                    if i := now.back(4):
                        SM.kills(act, i)
                        SM.scores(act, i, pS)
                    if i := now.back(0):
                        E.indices_in(act, i)
                    if i := now.back(8):
                        E.indices_out(act, i)
                    if i := now.back(7):
                        act.wait_ge(*O.at(i, "t4"))
                        nc.scalar.activation(ex[i.slot % 2][:, :], t4[i.slot % 2][:, :], ACT.Exp, bias=1.0)\
                            .then_inc(A.sem, 1)
                    if i := now.back(3):
                        s = i.slot
                        act.wait_ge(*M.at(i, "hs"))
                        if old := i.back(4):
                            act.wait_ge(*O.at(old, "t1"))
                            act.wait_ge(*V.at(old, "hw"))
                        nc.scalar.activation(Hx[s % 4][:, :, 0:HID], head(pHs[:, 0:D]), ACT.Copy)
                        nc.scalar.activation(as_[s][:, :], pHs[:, D:D + HEADS], ACT.Copy).then_inc(A.sem, 1)
                        act.wait_ge(*M.at(i, "hd"))
                        nc.scalar.activation(Hd[s % 4][:, :], pHd[:, :], ACT.Copy).then_inc(A.sem, 1)
                    if i := now.back(4):
                        act.wait_ge(*V.at(i, "dl"))
                        nc.scalar.activation(SM.ET[i.slot % 4][:, :], SM.dl[i.slot % 4][:, :], ACT.Exp)\
                            .then_inc(A.sem, 1)
                    if i := now.back(7):
                        E.eps(act, i)
                E.turns.run(act, turn)


def edge_attention(nc, g):
    with ExitStack() as c:
        E = EdgePass(nc, g, c, "att", 8,
                     "x:4 eq:4 fw:3 v:6 bw:3 st:6 dl:3 rd:5 ag:6 s1:2 s2:2 xn:7 lg:2 ne:2 lr:2",
                     "r:6",
                     "xr:4 lt:3 t:5 ag:4 h:5",
                     "cy:4 kl:3 LT:3 T:5 A:4 e:6 ET:3 src_i:0 dst_i:0 put_i:7", g["X2"], g["X3"])
        V, O, M, A, RING = E.V, E.O, E.M, E.A, E.RING
        W = D + 1
        SM = SegmentMax(E, 1, False)
        Xs = E.tiles("Xs", [P, W])
        junk = E.tiles("junk", [P, D], count=2)
        junk2 = E.tiles("junk2", [P, D], count=2)
        sc = E.tiles("sc", [P, 2])
        lg = E.tiles("lg", [P, 1])
        lr = E.tiles("lr", [P, 1])
        xw = E.tiles("xw", [P, 1])
        As = E.tiles("As", [P, W])
        AT = E.tiles("AT", [P, KC, P], count=2)
        rd = E.tiles("rd", [P, 1])
        started = g["sm"]("att_started", c)
        pT = E.banks("pT", [P, KC, P], 1)[0]
        pH = E.banks("pH", [P, D], 2)
        pA = E.banks("pA", [P, W], 2)
        pS = E.banks("pS", [1, P], 1)[0]
        pX = E.banks("pX", [P, 1], 1)[0]
        start_count = []

        with nc.Block() as block:
            @block.sync
            def _(sp):
                def turn(now):
                    if i := now.back(0):
                        if old := i.back(RING):
                            sp.wait_ge(*V.at(old, "eq"))
                        E.load_cols(sp, i)
                        SM.load(sp, i)
                E.turns.run(sp, turn)
                E.wait_out(sp)

            @block.vector
            def _(dve):
                count = [0]

                def done(ins):
                    count[0] += 1
                    ins.then_inc(started, 1)
                    dve.wait_ge(started, count[0])

                SM.start(nc, done)
                for a in Xs:
                    done(nc.vector.memset(a[:, :], 1.0))
                start_count.append(count[0])

                def turn(now):
                    if i := now.back(4):
                        s = i.slot
                        dve.wait_ge(*M.at(i, "xr"))
                        nc.vector.tensor_copy(xw[s][:, :], pX[:, :]).then_inc(V.sem, 1)
                        dve.wait_ge(*V.at(i, "x"))
                        E.same_target(dve, i, xw[s][:, :])
                    if i := now.back(3):
                        SM.forwards(dve, i)
                    if i := now.back(6):
                        s = i.slot
                        dve.wait_ge(*M.at(i, "h"))
                        dve.wait_ge(*V.at(i, "rd"))
                        nc.vector.scalar_tensor_tensor(E.v[s][:, :], pH[s % 2][:, :], rd[s][:, :], E.Xd[s][:, :],
                                                       ALU.mult, ALU.add).then_inc(V.sem, 1)
                    if i := now.back(3):
                        SM.backwards(dve, i)
                    if i := now.back(6):
                        E.stats(dve, i)
                    if i := now.back(3):
                        SM.shift(dve, i)
                    if i := now.back(5):
                        dve.wait_ge(*A.at(i, "A"))
                        nc.vector.reciprocal(rd[i.slot][:, :], As[i.slot][:, D:W]).then_inc(V.sem, 1)
                    if i := now.back(6):
                        E.moments(dve, i)
                    if i := now.back(2):
                        s = i.slot
                        dve.wait_ge(E.src_in[s], i.dma())
                        nc.vector.tensor_tensor_reduce(out=junk[s % 2][:, :], in0=Xs[s][:, 0:D], in1=g["us_r"][:, :],
                                                       scale=1.0, scalar=0.0, op0=ALU.mult, op1=ALU.add,
                                                       accum_out=sc[s][:, 0:1]).then_inc(V.sem, 1)
                        dve.wait_ge(E.dst_in[s], i.dma())
                        nc.vector.tensor_tensor_reduce(out=junk2[s % 2][:, :], in0=E.Xd[s][:, :], in1=g["ud_r"][:, :],
                                                       scale=1.0, scalar=0.0, op0=ALU.mult, op1=ALU.add,
                                                       accum_out=sc[s][:, 1:2]).then_inc(V.sem, 1)
                    if i := now.back(7):
                        E.normalise(dve, i)
                    if i := now.back(2):
                        s = i.slot
                        dve.wait_ge(*V.at(i, "s2"))
                        nc.vector.scalar_tensor_tensor(lg[s][:, :], sc[s][:, 0:1], sc[s][:, 1:2],
                                                       g["efeat"][:, bass.ds(i.number, 1)], ALU.add, ALU.add)\
                            .then_inc(V.sem, 1)
                        SM.breaks(dve, i)
                        dve.wait_ge(*V.at(i, "lg"))
                        nc.vector.scalar_tensor_tensor(lr[s][:, :], lg[s][:, :], SLOPE, lg[s][:, :],
                                                       ALU.mult, ALU.max).then_inc(V.sem, 1)
                E.turns.run(dve, turn)

            @block.gpsimd
            def _(pool):
                pool.wait_ge(started, start_count[0])

                def turn(now):
                    if i := now.back(1):
                        if old := i.back(RING):
                            pool.wait_ge(*M.at(old, "ag"))
                        E.gather(pool, i, E.ixs, "src_i", Xs[i.slot][:, 0:D], E.src_in)
                        E.gather_dst(pool, i)
                    if i := now.back(8):
                        E.scatter(pool, i)
                    if i := now.back(6):
                        E.rstd(pool, i)
                E.turns.run(pool, turn)

            @block.tensor
            def _(pe):
                pe.wait_ge(started, start_count[0])

                def turn(now):
                    if i := now.back(4):
                        pe.wait_ge(*A.at(i, "ET"))
                        if old := i.back(1):
                            pe.wait_ge(*V.at(old, "x"))
                        nc.tensor.matmul(pX[:, :], SM.ET[i.slot % 4][:, 0:P], g["ident"][0:1, 0:1],
                                         start=True, stop=True).then_inc(M.sem, 1)
                    if i := now.back(3):
                        pe.wait_ge(*V.at(i, "lr"))
                        if old := i.back(1):
                            pe.wait_ge(*A.at(old, "LT"))
                        nc.tensor.transpose(pS[:, :], lr[i.slot][:, :], g["ident"][:, :]).then_inc(M.sem, 1)
                    if i := now.back(5):
                        s = i.slot
                        pe.wait_ge(*A.at(i, "A"))
                        if old := i.back(1):
                            pe.wait_ge(*A.at(old, "T"))
                        for j in range(KC):
                            last = nc.tensor.transpose(pT[:, j, :], As[s][:, j * P:(j + 1) * P], g["ident"][:, :])
                        last.then_inc(M.sem, 1)
                    if i := now.back(4):
                        s = i.slot
                        pe.wait_ge(*A.at(i, "cy"))
                        pe.wait_ge(*V.at(i, "eq"))
                        if old := i.back(2):
                            pe.wait_ge(*A.at(old, "A"))
                        nc.tensor.matmul(pA[s % 2][:, :], E.eq[s][:, :], Xs[s][:, :], start=True, stop=True)\
                            .then_inc(M.sem, 1)
                    if i := now.back(5):
                        s = i.slot
                        pe.wait_ge(*A.at(i, "T"))
                        if old := i.back(2):
                            pe.wait_ge(*V.at(old, "v"))
                        for j in range(KC):
                            last = nc.tensor.matmul(pH[s % 2][:, :], AT[s % 2][:, j, :], g["W2T"][:, j, :],
                                                    start=(j == 0), stop=(j == KC - 1))
                        last.then_inc(M.sem, 1)
                E.turns.run(pe, turn)

            @block.scalar
            def _(act):
                def turn(now):
                    if i := now.back(4):
                        row = Xs[i.slot][0:1, :]
                        act.wait_ge(*V.at(i, "s1"))
                        if prev := i.back(1):
                            act.wait_ge(*M.at(prev, "ag"))
                            nc.scalar.activation(row, pA[prev.slot % 2][0:1, :], ACT.Copy).then_inc(A.sem, 1)
                        else:
                            nc.scalar.activation(row, row, ACT.Copy, scale=0.0).then_inc(A.sem, 1)
                    if i := now.back(3):
                        SM.kills(act, i)
                        SM.scores(act, i, pS)
                    if i := now.back(5):
                        act.wait_ge(*M.at(i, "t"))
                        nc.scalar.activation(AT[i.slot % 2][:, :, :], pT[:, :, :], ACT.Copy).then_inc(A.sem, 1)
                    if i := now.back(4):
                        act.wait_ge(*M.at(i, "ag"))
                        nc.scalar.activation(As[i.slot][:, :], pA[i.slot % 2][:, :], ACT.Copy).then_inc(A.sem, 1)
                    if i := now.back(6):
                        E.eps(act, i)
                    if i := now.back(3):
                        act.wait_ge(*V.at(i, "dl"))
                        nc.scalar.activation(SM.ET[i.slot % 4][:, 0:P], SM.dl[i.slot % 4][:, 0:P], ACT.Exp)\
                            .then_inc(A.sem, 1)
                    if i := now.back(0):
                        E.indices_in(act, i)
                    if i := now.back(7):
                        E.indices_out(act, i)
                E.turns.run(act, turn)


def edge_gru(nc, g):
    with ExitStack() as c:
        E = EdgePass(nc, g, c, "gru", 8,
                     "q:6 q1:6 sr:2 eq:2 xn:7 nb:6 v:6 st:6 ag:6",
                     "xa:6 r:6",
                     "ag:3 t:4 gru:5",
                     "za:6 zb:6 A:3 n:6 aT:4 cy:2 src_i:0 dst_i:0 rel_i:0 put_i:7 e:6 rz:5", g["X3"], g["out"])
        V, O, M, A, RING = E.V, E.O, E.M, E.A, E.RING
        Xs = E.tiles("Xs", [P, D])
        Xr = E.tiles("Xr", [P, D])
        ixr = E.tiles("ixr", [P, 1], I32)
        rel_in = g["queue_sems"]("gru_rel_in")
        As = E.tiles("As", [P, D], count=4)
        aT = E.tiles("aT", [P, 2 * KC, P], count=2)
        rz = E.tiles("rz", [P, 2 * D], count=2)
        q, q1, n, za, zb, xa, nb = (E.tiles(m, [P, D], count=2) for m in ("q", "q1", "n", "za", "zb", "xa", "nb"))
        pA = E.banks("pA", [P, D], 2)
        pT = E.banks("pT", [P, 2 * KC, P], 1)[0]
        pRZ = E.banks("pRZ", [P, 2 * D], 2)
        pN = E.banks("pN", [P, 2, D], 2)

        with nc.Block() as block:
            @block.sync
            def _(sp):
                def turn(now):
                    if i := now.back(0):
                        if old := i.back(RING):
                            sp.wait_ge(*V.at(old, "eq"))
                        E.load_cols(sp, i)
                E.turns.run(sp, turn)
                E.wait_out(sp)

            @block.gpsimd
            def _(pool):
                def turn(now):
                    if i := now.back(2):
                        E.gather_dst(pool, i)
                    if i := now.back(6):
                        s = i.slot
                        pool.wait_ge(*A.at(i, "za"))
                        nc.gpsimd.tensor_tensor(xa[s % 2][:, :], E.Xd[s][:, :], za[s % 2][:, :], ALU.mult)\
                            .then_inc(O.sem, 1)
                    if i := now.back(1):
                        if old := i.back(RING):
                            pool.wait_ge(*M.at(old, "ag"))
                        E.gather(pool, i, E.ixs, "src_i", Xs[i.slot][:, :], E.src_in)
                        E.gather(pool, i, ixr, "rel_i", Xr[i.slot][:, :], rel_in, g["rel"])
                    if i := now.back(8):
                        E.scatter(pool, i)
                    if i := now.back(6):
                        E.rstd(pool, i)
                E.turns.run(pool, turn)

            @block.vector
            def _(dve):
                def turn(now):
                    if i := now.back(6):
                        s = i.slot
                        dve.wait_ge(*A.at(i, "rz"))
                        nc.vector.scalar_tensor_tensor(q[s % 2][:, :], rz[s % 2][:, 0:D], 1.0, pN[s % 2][:, 1, :],
                                                       ALU.add, ALU.mult).then_inc(V.sem, 1)
                        dve.wait_ge(*V.at(i, "q"))
                        nc.vector.tensor_tensor(q1[s % 2][:, :], q[s % 2][:, :], pN[s % 2][:, 0, :], ALU.add)\
                            .then_inc(V.sem, 1)
                    if i := now.back(2):
                        s = i.slot
                        dve.wait_ge(E.src_in[s], i.dma())
                        dve.wait_ge(rel_in[s], i.dma())
                        nc.vector.tensor_tensor(Xs[s][:, :], Xs[s][:, :], Xr[s][:, :], ALU.add).then_inc(V.sem, 1)
                        E.same_target(dve, i)
                    if i := now.back(7):
                        E.normalise(dve, i)
                    if i := now.back(6):
                        s = i.slot
                        dve.wait_ge(*A.at(i, "n"))
                        nc.vector.tensor_tensor(nb[s % 2][:, :], n[s % 2][:, :], zb[s % 2][:, :], ALU.mult)\
                            .then_inc(V.sem, 1)
                        dve.wait_ge(*V.at(i, "nb"))
                        dve.wait_ge(*O.at(i, "xa"))
                        nc.vector.tensor_tensor(E.v[s][:, :], nb[s % 2][:, :], xa[s % 2][:, :], ALU.add)\
                            .then_inc(V.sem, 1)
                        E.stats(dve, i)
                        E.moments(dve, i)
                E.turns.run(dve, turn)

            @block.tensor
            def _(pe):
                def turn(now):
                    if i := now.back(3):
                        s = i.slot
                        pe.wait_ge(*A.at(i, "cy"))
                        pe.wait_ge(*V.at(i, "eq"))
                        if old := i.back(2):
                            pe.wait_ge(*A.at(old, "A"))
                        nc.tensor.matmul(pA[s % 2][:, :], E.eq[s][:, :], Xs[s][:, :], start=True, stop=True)\
                            .then_inc(M.sem, 1)
                    if i := now.back(4):
                        s = i.slot
                        pe.wait_ge(*A.at(i, "A"))
                        if old := i.back(1):
                            pe.wait_ge(*A.at(old, "aT"))
                        pe.wait_ge(E.dst_in[s], i.dma())
                        for a, rows in enumerate((As[s % 4], E.Xd[s])):
                            for j in range(KC):
                                last = nc.tensor.transpose(pT[:, a * KC + j, :], rows[:, j * P:(j + 1) * P],
                                                           g["ident"][:, :])
                        last.then_inc(M.sem, 1)
                    if i := now.back(5):
                        s = i.slot
                        pe.wait_ge(*A.at(i, "aT"))
                        if old := i.back(2):
                            pe.wait_ge(*V.at(old, "q1"))
                        for o, lo, hi, bias, ins in ((pRZ[s % 2][:, :], 0, 2 * D, g["bias3"][:, 0:2 * D], (0, 1)),
                                                     (pN[s % 2][:, 0, :], 2 * D, 3 * D, g["bias_in"][:, :], (0,)),
                                                     (pN[s % 2][:, 1, :], 2 * D, 3 * D, g["bias3"][:, 2 * D:3 * D], (1,))):
                            terms = [(g["ones_b"][:, :], bias)]
                            for a in ins:
                                wT = g["whhT"] if a else g["wihT"]
                                terms += [(aT[s % 2][:, a * KC + j, :], wT[:, j, lo:hi]) for j in range(KC)]
                            for x_, (l, r) in enumerate(terms):
                                last = nc.tensor.matmul(o, l, r, start=(x_ == 0), stop=(x_ == len(terms) - 1))
                        last.then_inc(M.sem, 1)
                E.turns.run(pe, turn)

            @block.scalar
            def _(act):
                def turn(now):
                    if i := now.back(6):
                        act.wait_ge(*A.at(i, "rz"))
                        nc.scalar.activation(za[i.slot % 2][:, :], rz[i.slot % 2][:, D:2 * D], ACT.Copy, scale=0.5,
                                             bias=1.5).then_inc(A.sem, 1)
                        nc.scalar.activation(zb[i.slot % 2][:, :], rz[i.slot % 2][:, D:2 * D], ACT.Copy, scale=-0.5,
                                             bias=0.5).then_inc(A.sem, 1)
                    if i := now.back(3):
                        act.wait_ge(*M.at(i, "ag"))
                        nc.scalar.activation(As[i.slot % 4][:, :], pA[i.slot % 2][:, :], ACT.Copy).then_inc(A.sem, 1)
                    if i := now.back(6):
                        act.wait_ge(*V.at(i, "q1"))
                        nc.scalar.activation(n[i.slot % 2][:, :], q1[i.slot % 2][:, :], ACT.Tanh).then_inc(A.sem, 1)
                    if i := now.back(4):
                        act.wait_ge(*M.at(i, "t"))
                        nc.scalar.activation(aT[i.slot % 2][:, :, :], pT[:, :, :], ACT.Copy).then_inc(A.sem, 1)
                    if i := now.back(2):
                        row = Xs[i.slot][0:1, :]
                        act.wait_ge(*V.at(i, "sr"))
                        if prev := i.back(1):
                            act.wait_ge(*M.at(prev, "ag"))
                            nc.scalar.activation(row, pA[prev.slot % 2][0:1, :], ACT.Copy).then_inc(A.sem, 1)
                        else:
                            nc.scalar.activation(row, row, ACT.Copy, scale=0.0).then_inc(A.sem, 1)
                    if i := now.back(0):
                        E.indices_in(act, i)
                        E.indices(act, i, ixr, "rel_i", rel_in)
                    if i := now.back(7):
                        E.indices_out(act, i)
                    if i := now.back(6):
                        E.eps(act, i)
                    if i := now.back(5):
                        act.wait_ge(*M.at(i, "gru"))
                        if old := i.back(2):
                            act.wait_ge(*V.at(old, "q"))
                        nc.scalar.activation(rz[i.slot % 2][:, :], pRZ[i.slot % 2][:, :], ACT.Tanh, scale=0.5)\
                            .then_inc(A.sem, 1)
                E.turns.run(act, turn)


NB_EDGES = [0]


def kernel(x, src, dst, edge_attr_64, edge_type_16, edge_weight, L0_gnn_node_lock, L0_gnn_W, L0_gnn_b, L1_gnn_W0,
           L1_gnn_att_src0, L1_gnn_att_dst0, L1_gnn_b0, L1_gnn_W1, L1_gnn_att_src1, L1_gnn_att_dst1, L1_gnn_b1,
           L2_gnn_W, L2_gnn_A, L3_gnn_relvectors, L3_gnn_w_ih, L3_gnn_w_hh, L3_gnn_b_ih, L3_gnn_b_hh):
    import numpy as np
    import concourse.bacc as bacc
    from concourse.bass_utils import run_bass_kernel_spmd

    N, E = x.shape[0], src.shape[0]
    NB_EDGES[0] = E
    NB = -(-E // SLOT_EDGES)
    NB += -NB % 6
    PAD = NB * SLOT_EDGES

    def flat(a, fill, ahead=0):
        a = np.asarray(a)
        f = np.full((PAD + 2,) + a.shape[1:], fill, a.dtype)
        f[1:E + 1] = a
        f[0] = -1 if a.dtype.kind == "i" else 0
        return f[1 + ahead:1 + ahead + PAD]

    def slots(a, fill, first):
        f = flat(a, fill) if not isinstance(a, tuple) else a[0]
        f = f.reshape((NB, SLOT_EDGES) + f.shape[1:])
        row0 = np.broadcast_to(first, (NB, 1) + f.shape[2:]).astype(f.dtype)
        return np.ascontiguousarray(np.moveaxis(np.concatenate([row0, f], axis=1), 0, 1))

    cur = flat(dst, N).reshape(NB, SLOT_EDGES)
    before = flat(dst, N, -1).reshape(NB, SLOT_EDGES)
    after = flat(dst, N, 1)
    prev_last = before[:, :1]
    pack = lambda w: np.ascontiguousarray(np.asarray(w).T)
    att = np.zeros((D, 2 * HEADS), np.float32)
    for j, a in enumerate((L1_gnn_att_src0, L1_gnn_att_dst0)):
        for h in range(HEADS):
            att[h * HID:(h + 1) * HID, j * HEADS + h] = np.asarray(a)[0, h]
    ins = {
        "x": np.asarray(x),
        "src": slots(src, 0, prev_last),
        "dst": slots(dst, N, prev_last),
        "dst_next": slots((after,), N, prev_last),
        "dst_cols": np.ascontiguousarray(np.concatenate([cur[:, -1:], cur], axis=1)),
        "dst_prev": np.ascontiguousarray(np.concatenate([cur[:, -1:], before], axis=1)),
        "attr": slots(edge_attr_64, 0, 0),
        "etype": slots(edge_type_16, 0, 0),
        "ew": slots(edge_weight, 0, 0),
        "node_lock": np.asarray(L0_gnn_node_lock).reshape(1, -1),
        "W0e_T": pack(L0_gnn_W), "b0e": np.asarray(L0_gnn_b).reshape(1, -1),
        "W1_T": pack(L1_gnn_W0), "W1n": np.asarray(L1_gnn_W0), "att1": att, "b1": np.asarray(L1_gnn_b0).reshape(1, -1),
        "W2_T": pack(L2_gnn_W), "W2n": np.asarray(L2_gnn_W), "A2": np.asarray(L2_gnn_A),
        "a2_T": np.ascontiguousarray(np.asarray(L2_gnn_A)[0, :2 * D].reshape(2, D).T),
        "rel": np.asarray(L3_gnn_relvectors), "wih_T": pack(L3_gnn_w_ih), "whh_T": pack(L3_gnn_w_hh),
        "b_ih": np.asarray(L3_gnn_b_ih).reshape(1, -1), "b_hh": np.asarray(L3_gnn_b_hh).reshape(1, -1),
    }
    nc = bacc.Bacc("TRN2", target_bir_lowering=False, num_devices=1)
    args = [nc.dram_tensor(f"in_{n}", a.shape, mybir.dt.from_np(a.dtype), kind="ExternalInput").ap()
            for n, a in ins.items()]
    args.append(nc.dram_tensor("out", (N, D), F32, kind="ExternalOutput").ap())
    for n in ("X1", "X2", "X3"):
        args.append(nc.dram_tensor(n, (N, D), F32, kind="Internal").ap())
    args.append(nc.dram_tensor("MSG", (NB * P, D), F32, kind="Internal").ap())
    gnn(nc, *args)
    r = run_bass_kernel_spmd(nc, [{f"in_{n}": a for n, a in ins.items()}], core_ids=[0])
    return r.results[0]["out"]
```
